# Optimizing a Trainium2 kernel written in Bass

```python
import numpy as np
import jax
import jax.numpy as jnp

def _softmax(x, axis=-1):
    return jax.nn.softmax(x, axis=axis)

def _gelu(x):
    return jax.nn.gelu(x, approximate=True)

def _silu(x):
    return jax.nn.silu(x)

def _sigmoid(x):
    return jax.nn.sigmoid(x)

def _layernorm(x, axis=-1, eps=1e-05):
    m = jnp.mean(x, axis=axis, keepdims=True)
    v = jnp.var(x, axis=axis, keepdims=True)
    return (x - m) / jnp.sqrt(v + eps)

def _scatter_add(tgt, idx, src, axis=0):
    return tgt.at[idx].add(src)

def _segment_sum(src, seg, n):
    return jax.ops.segment_sum(src, seg, n)
kernel_name = 'mk_decoder_postln_d1_seqx_r4_547b1c'

def setup_inputs(seed: int=0):
    np.random.seed(seed)
    _w = jnp.asarray

    def _rec_inputs():
        import jax
        import jax.numpy as jnp
        _rk = jax.random.key(seed)
        x = 7.22e-05 + 1 * jax.random.normal(jax.random.fold_in(_rk, 1), (2, 1024, 256), jnp.float32)
        _lenS = 1024 - jax.random.randint(jax.random.fold_in(_rk, 7), (2,), 0, max(1, 1024 // 4) + 1, jnp.int32)
        _lenS2 = 77 - jax.random.randint(jax.random.fold_in(_rk, 8), (2,), 0, max(1, 77 // 4) + 1, jnp.int32)
        _ctx_1024P = jax.random.normal(jax.random.fold_in(_rk, 11), (2, 16, 256), jnp.float32)
        _ctx_1024c = jax.random.dirichlet(jax.random.fold_in(_rk, 511), 0.3 * jnp.ones((16,), jnp.float32), (2, 77))
        _ctx_1024t = jnp.einsum('bsk,bkd->bsd', _ctx_1024c, _ctx_1024P)
        _ctx_1024t = _ctx_1024t * jax.lax.rsqrt(jnp.mean(jnp.square(_ctx_1024t)) + 1e-12) * 0.953939
        ctx_1024 = 4.13588e-05 + 0.999923 * (_ctx_1024t + 0.3 * jax.random.normal(jax.random.fold_in(_rk, 611), (2, 77, 256), jnp.float32))
        _validS = jnp.arange(1024)[None, :] < _lenS[:, None]
        _validS2 = jnp.arange(77)[None, :] < _lenS2[:, None]
        _causal = jnp.tril(jnp.ones((1024, 1024), dtype=bool))
        mask_1x1xSxS2_ff0 = jnp.where(jnp.ones((1, 1, 1024, 77), dtype=bool), 0.0, -1000000000.0).astype(jnp.float32)
        return (x, ctx_1024, mask_1x1xSxS2_ff0)
    x, ctx_1024, mask_1x1xSxS2_ff0 = _rec_inputs()

    def _L0_attn_setup():
        import jax, jax.numpy as jnp
        import numpy as np
        D = 256
        H = 16
        KVH = 4
        HD = D // H
        LAT = 64
        WIN = 64
        B, S = (1, 512)
        BASE_G, BASE_L = (1000000.0, 10000.0)
        EPS = 1e-06

        def rmsnorm(x, w):
            return x * jax.lax.rsqrt(jnp.mean(x * x, axis=-1, keepdims=True) + EPS) * w

        def qk_norm(x):
            return x * jax.lax.rsqrt(jnp.mean(x * x, axis=-1, keepdims=True) + EPS)

        def rope(x, base):
            s, hd = (x.shape[-2], x.shape[-1])
            inv_freq = 1.0 / base ** (jnp.arange(0, hd, 2, dtype=jnp.float32) / hd)
            freqs = jnp.arange(s, dtype=jnp.float32)[:, None] * inv_freq[None, :]
            cos, sin = (jnp.cos(freqs), jnp.sin(freqs))
            xe, xo = (x[..., ::2], x[..., 1::2])
            out = jnp.stack([xe * cos - xo * sin, xe * sin + xo * cos], axis=-1)
            return out.reshape(x.shape)

        def split_heads(x, n_heads):
            b, s, _ = x.shape
            return x.reshape(b, s, n_heads, HD).transpose(0, 2, 1, 3)

        def repeat_kv(x):
            return jnp.repeat(x, H // KVH, axis=1)

        def sdpa(q, k, v, mask):
            scores = jnp.einsum('bhqd,bhkd->bhqk', q, k) / np.sqrt(HD).astype(np.float32)
            scores = jnp.where(mask, scores, jnp.float32(-1e+30))
            probs = jax.nn.softmax(scores, axis=-1)
            return jnp.einsum('bhqk,bhkd->bhqd', probs, v)

        def merge_heads(x):
            b, h, s, hd = x.shape
            return x.transpose(0, 2, 1, 3).reshape(b, s, h * hd)

        def global_latent_attn(x, wq, w_kv_down, w_k_up, w_v_up, wo):
            q = split_heads(x @ wq, H)
            latent = x @ w_kv_down
            k = split_heads(latent @ w_k_up, KVH)
            v = split_heads(latent @ w_v_up, KVH)
            q, k = (rope(q, BASE_G), rope(k, BASE_G))
            q, k = (qk_norm(q), qk_norm(k))
            k, v = (repeat_kv(k), repeat_kv(v))
            i = jnp.arange(x.shape[1])
            causal = i[:, None] >= i[None, :]
            return merge_heads(sdpa(q, k, v, causal)) @ wo

        def local_gqa_attn(x, wq, wk, wv, wo):
            q = split_heads(x @ wq, H)
            k = split_heads(x @ wk, KVH)
            v = split_heads(x @ wv, KVH)
            q, k = (rope(q, BASE_L), rope(k, BASE_L))
            q, k = (qk_norm(q), qk_norm(k))
            k, v = (repeat_kv(k), repeat_kv(v))
            i = jnp.arange(x.shape[1])
            diff = i[:, None] - i[None, :]
            mask = (diff >= 0) & (diff < WIN)
            return merge_heads(sdpa(q, k, v, mask)) @ wo
        key = jax.random.key(seed)
        ks = jax.random.split(key, 12)
        std = 0.02
        return {'hidden': jax.random.normal(ks[0], (B, S, D), dtype=jnp.float32), 'norm1_w': jnp.ones((D,), jnp.float32), 'norm2_w': jnp.ones((D,), jnp.float32), 'g_wq': jax.random.normal(ks[1], (D, H * HD), jnp.float32) * std, 'g_kv_down': jax.random.normal(ks[2], (D, LAT), jnp.float32) * std, 'g_k_up': jax.random.normal(ks[3], (LAT, KVH * HD), jnp.float32) * std, 'g_v_up': jax.random.normal(ks[4], (LAT, KVH * HD), jnp.float32) * std, 'g_wo': jax.random.normal(ks[5], (D, D), jnp.float32) * std, 'l_wq': jax.random.normal(ks[6], (D, H * HD), jnp.float32) * std, 'l_wk': jax.random.normal(ks[7], (D, KVH * HD), jnp.float32) * std, 'l_wv': jax.random.normal(ks[8], (D, KVH * HD), jnp.float32) * std, 'l_wo': jax.random.normal(ks[9], (D, D), jnp.float32) * std}
    _L0_attn_all = _L0_attn_setup()
    _L0_attn_in = {k: v for k, v in _L0_attn_all.items() if k in ('norm1_w', 'norm2_w', 'g_wq', 'g_kv_down', 'g_k_up', 'g_v_up', 'g_wo', 'l_wq', 'l_wk', 'l_wv', 'l_wo')}
    del _L0_attn_all

    def _L0_xattn_setup():
        import jax, jax.numpy as jnp
        import numpy as np
        D_MODEL = 256
        NUM_HEADS = 16
        D_QKV = D_MODEL // NUM_HEADS
        B, S = (4, 512)
        FMAX = jnp.finfo(jnp.float32).max

        def _split_heads(x):
            b, s, _ = x.shape
            return x.reshape(b, s, NUM_HEADS, D_QKV).transpose(0, 2, 1, 3)
        key = jax.random.key(seed)
        ks = jax.random.split(key, 12)
        s = 1.0 / np.sqrt(D_MODEL)
        return {'q_in': jax.random.normal(ks[0], (B, S, D_MODEL), jnp.float32), 'k_in': jax.random.normal(ks[1], (B, S, D_MODEL), jnp.float32), 'v_in': jax.random.normal(ks[2], (B, S, D_MODEL), jnp.float32), 'mask': jnp.zeros((1, 1, S, S), jnp.float32), 'Wq': jax.random.normal(ks[3], (D_MODEL, D_MODEL), jnp.float32) * s, 'bq': jnp.zeros((D_MODEL,), jnp.float32), 'Wk': jax.random.normal(ks[4], (D_MODEL, D_MODEL), jnp.float32) * s, 'bk': jnp.zeros((D_MODEL,), jnp.float32), 'Wv': jax.random.normal(ks[5], (D_MODEL, D_MODEL), jnp.float32) * s, 'bv': jnp.zeros((D_MODEL,), jnp.float32), 'Wo': jax.random.normal(ks[6], (D_MODEL, D_MODEL), jnp.float32) * s, 'bo': jnp.zeros((D_MODEL,), jnp.float32)}
    _L0_xattn_all = _L0_xattn_setup()
    _L0_xattn_in = {k: v for k, v in _L0_xattn_all.items() if k in ('Wq', 'bq', 'Wk', 'bk', 'Wv', 'bv', 'Wo', 'bo')}
    del _L0_xattn_all

    def _L0_ffn_setup():
        import jax, jax.numpy as jnp
        import numpy as np
        TOP_K = 2
        key = jax.random.key(seed)
        ks = jax.random.split(key, 5)
        B, S, H, I, E = (4, 512, 256, 1024, 8)
        scale_hi = (2.0 / (H + I)) ** 0.5
        scale_he = (2.0 / (H + E)) ** 0.5
        return {'x': jax.random.normal(ks[0], (B, S, H), dtype=jnp.float32), 'router_w': jax.random.normal(ks[1], (E, H), dtype=jnp.float32) * scale_he, 'gate_w': jax.random.normal(ks[2], (E, I, H), dtype=jnp.float32) * scale_hi, 'up_w': jax.random.normal(ks[3], (E, I, H), dtype=jnp.float32) * scale_hi, 'down_w': jax.random.normal(ks[4], (E, H, I), dtype=jnp.float32) * scale_hi}
    _L0_ffn_all = _L0_ffn_setup()
    _L0_ffn_in = {k: v for k, v in _L0_ffn_all.items() if k in ('router_w', 'gate_w', 'up_w', 'down_w')}
    del _L0_ffn_all
    return {'x': x, 'ctx_1024': ctx_1024, 'mask_1x1xSxS2_ff0': mask_1x1xSxS2_ff0, 'L0_attn_norm1_w': _L0_attn_in['norm1_w'], 'L0_attn_norm2_w': _L0_attn_in['norm2_w'], 'L0_attn_g_wq': _L0_attn_in['g_wq'], 'L0_attn_g_kv_down': _L0_attn_in['g_kv_down'], 'L0_attn_g_k_up': _L0_attn_in['g_k_up'], 'L0_attn_g_v_up': _L0_attn_in['g_v_up'], 'L0_attn_g_wo': _L0_attn_in['g_wo'], 'L0_attn_l_wq': _L0_attn_in['l_wq'], 'L0_attn_l_wk': _L0_attn_in['l_wk'], 'L0_attn_l_wv': _L0_attn_in['l_wv'], 'L0_attn_l_wo': _L0_attn_in['l_wo'], 'L0_xattn_Wq': _L0_xattn_in['Wq'], 'L0_xattn_bq': _L0_xattn_in['bq'], 'L0_xattn_Wk': _L0_xattn_in['Wk'], 'L0_xattn_bk': _L0_xattn_in['bk'], 'L0_xattn_Wv': _L0_xattn_in['Wv'], 'L0_xattn_bv': _L0_xattn_in['bv'], 'L0_xattn_Wo': _L0_xattn_in['Wo'], 'L0_xattn_bo': _L0_xattn_in['bo'], 'L0_ffn_router_w': _L0_ffn_in['router_w'], 'L0_ffn_gate_w': _L0_ffn_in['gate_w'], 'L0_ffn_up_w': _L0_ffn_in['up_w'], 'L0_ffn_down_w': _L0_ffn_in['down_w']}

def reference(x, ctx_1024, mask_1x1xSxS2_ff0, L0_attn_norm1_w, L0_attn_norm2_w, L0_attn_g_wq, L0_attn_g_kv_down, L0_attn_g_k_up, L0_attn_g_v_up, L0_attn_g_wo, L0_attn_l_wq, L0_attn_l_wk, L0_attn_l_wv, L0_attn_l_wo, L0_xattn_Wq, L0_xattn_bq, L0_xattn_Wk, L0_xattn_bk, L0_xattn_Wv, L0_xattn_bv, L0_xattn_Wo, L0_xattn_bo, L0_ffn_router_w, L0_ffn_gate_w, L0_ffn_up_w, L0_ffn_down_w):
    import jax
    import jax.numpy as jnp

    def _L0_attn_ref(hidden, norm1_w, norm2_w, g_wq, g_kv_down, g_k_up, g_v_up, g_wo, l_wq, l_wk, l_wv, l_wo):
        import jax, jax.numpy as jnp
        import numpy as np
        D = 256
        H = 16
        KVH = 4
        HD = D // H
        LAT = 64
        WIN = 64
        B, S = (1, 512)
        BASE_G, BASE_L = (1000000.0, 10000.0)
        EPS = 1e-06

        def rmsnorm(x, w):
            return x * jax.lax.rsqrt(jnp.mean(x * x, axis=-1, keepdims=True) + EPS) * w

        def qk_norm(x):
            return x * jax.lax.rsqrt(jnp.mean(x * x, axis=-1, keepdims=True) + EPS)

        def rope(x, base):
            s, hd = (x.shape[-2], x.shape[-1])
            inv_freq = 1.0 / base ** (jnp.arange(0, hd, 2, dtype=jnp.float32) / hd)
            freqs = jnp.arange(s, dtype=jnp.float32)[:, None] * inv_freq[None, :]
            cos, sin = (jnp.cos(freqs), jnp.sin(freqs))
            xe, xo = (x[..., ::2], x[..., 1::2])
            out = jnp.stack([xe * cos - xo * sin, xe * sin + xo * cos], axis=-1)
            return out.reshape(x.shape)

        def split_heads(x, n_heads):
            b, s, _ = x.shape
            return x.reshape(b, s, n_heads, HD).transpose(0, 2, 1, 3)

        def repeat_kv(x):
            return jnp.repeat(x, H // KVH, axis=1)

        def sdpa(q, k, v, mask):
            scores = jnp.einsum('bhqd,bhkd->bhqk', q, k) / np.sqrt(HD).astype(np.float32)
            scores = jnp.where(mask, scores, jnp.float32(-1e+30))
            probs = jax.nn.softmax(scores, axis=-1)
            return jnp.einsum('bhqk,bhkd->bhqd', probs, v)

        def merge_heads(x):
            b, h, s, hd = x.shape
            return x.transpose(0, 2, 1, 3).reshape(b, s, h * hd)

        def global_latent_attn(x, wq, w_kv_down, w_k_up, w_v_up, wo):
            q = split_heads(x @ wq, H)
            latent = x @ w_kv_down
            k = split_heads(latent @ w_k_up, KVH)
            v = split_heads(latent @ w_v_up, KVH)
            q, k = (rope(q, BASE_G), rope(k, BASE_G))
            q, k = (qk_norm(q), qk_norm(k))
            k, v = (repeat_kv(k), repeat_kv(v))
            i = jnp.arange(x.shape[1])
            causal = i[:, None] >= i[None, :]
            return merge_heads(sdpa(q, k, v, causal)) @ wo

        def local_gqa_attn(x, wq, wk, wv, wo):
            q = split_heads(x @ wq, H)
            k = split_heads(x @ wk, KVH)
            v = split_heads(x @ wv, KVH)
            q, k = (rope(q, BASE_L), rope(k, BASE_L))
            q, k = (qk_norm(q), qk_norm(k))
            k, v = (repeat_kv(k), repeat_kv(v))
            i = jnp.arange(x.shape[1])
            diff = i[:, None] - i[None, :]
            mask = (diff >= 0) & (diff < WIN)
            return merge_heads(sdpa(q, k, v, mask)) @ wo
        x = hidden
        x = x + global_latent_attn(rmsnorm(x, norm1_w), g_wq, g_kv_down, g_k_up, g_v_up, g_wo)
        x = x + local_gqa_attn(rmsnorm(x, norm2_w), l_wq, l_wk, l_wv, l_wo)
        return x

    def _L0_xattn_ref(q_in, k_in, v_in, mask, Wq, bq, Wk, bk, Wv, bv, Wo, bo):
        import jax, jax.numpy as jnp
        import numpy as np
        D_MODEL = 256
        NUM_HEADS = 16
        D_QKV = D_MODEL // NUM_HEADS
        B, S = (4, 512)
        FMAX = jnp.finfo(jnp.float32).max

        def _split_heads(x):
            b, s, _ = x.shape
            return x.reshape(b, s, NUM_HEADS, D_QKV).transpose(0, 2, 1, 3)
        q = _split_heads(q_in @ Wq + bq)
        k = _split_heads(k_in @ Wk + bk)
        v = _split_heads(v_in @ Wv + bv)
        logits = jnp.einsum('bhqd,bhkd->bhqk', q, k) / jnp.sqrt(jnp.asarray(D_QKV, jnp.float32))
        logits = logits - mask * FMAX
        w = jax.nn.softmax(logits, axis=-1)
        o = jnp.einsum('bhqk,bhkd->bhqd', w, v)
        o = o.transpose(0, 2, 1, 3).reshape(q_in.shape[0], q_in.shape[1], D_MODEL)
        return o @ Wo + bo

    def _L0_ffn_ref(x, router_w, gate_w, up_w, down_w):
        import jax, jax.numpy as jnp
        import numpy as np
        TOP_K = 2
        B, S, H = x.shape
        E = router_w.shape[0]
        xf = x.reshape(-1, H)
        logits = xf @ router_w.T
        probs = jax.nn.softmax(logits, axis=-1)
        topk_p, topk_i = jax.lax.top_k(probs, TOP_K)
        topk_p = topk_p / topk_p.sum(axis=-1, keepdims=True)

        def body(out, inputs):
            e, gw, uw, dw = inputs
            sel = topk_i == e
            mask = sel.any(axis=-1)
            w_tok = (topk_p * sel).sum(axis=-1)
            cnt = mask.sum().astype(xf.dtype)
            mean_w = jnp.where(cnt > 0, w_tok.sum() / jnp.maximum(cnt, 1.0), 0.0)
            h = jax.nn.silu(xf @ gw.T) * (xf @ uw.T)
            eo = h @ dw.T
            out = out + mask[:, None].astype(xf.dtype) * eo * mean_w
            return (out, None)
        out0 = jnp.zeros_like(xf)
        out, _ = jax.lax.scan(body, out0, (jnp.arange(E), gate_w, up_w, down_w))
        return out.reshape(B, S, H)
    x = _layernorm(x + _L0_attn_ref(x, L0_attn_norm1_w, L0_attn_norm2_w, L0_attn_g_wq, L0_attn_g_kv_down, L0_attn_g_k_up, L0_attn_g_v_up, L0_attn_g_wo, L0_attn_l_wq, L0_attn_l_wk, L0_attn_l_wv, L0_attn_l_wo), axis=-1)
    x = _layernorm(x + _L0_xattn_ref(x, ctx_1024, ctx_1024, mask_1x1xSxS2_ff0, L0_xattn_Wq, L0_xattn_bq, L0_xattn_Wk, L0_xattn_bk, L0_xattn_Wv, L0_xattn_bv, L0_xattn_Wo, L0_xattn_bo), axis=-1)
    x = _layernorm(x + _L0_ffn_ref(x, L0_ffn_router_w, L0_ffn_gate_w, L0_ffn_up_w, L0_ffn_down_w), axis=-1)
    return x

_drawn_inputs = setup_inputs


def setup_inputs(seed=0):
    import zlib

    import numpy as np

    out = dict(_drawn_inputs(seed))
    spreads = {'L0_attn_norm1_w': (1.0, 0.6),
     'L0_attn_norm2_w': (1.0, 0.6),
     'L0_xattn_bq': (0.0, 0.1),
     'L0_xattn_bk': (0.0, 0.8),
     'L0_xattn_bv': (0.0, 0.1),
     'L0_xattn_bo': (0.0, 0.1)}
    factors = {'L0_attn_g_wq': 8.0,
     'L0_attn_g_kv_down': 8.0,
     'L0_attn_g_k_up': 8.0,
     'L0_attn_g_v_up': 8.0,
     'L0_attn_g_wo': 8.0,
     'L0_attn_l_wq': 3.531,
     'L0_attn_l_wk': 3.341,
     'L0_attn_l_wo': 2.739}
    for name, (base, spread) in spreads.items():
        noise = np.random.default_rng([zlib.crc32(name.encode()), seed]).standard_normal(out[name].shape)
        drawn = base * np.exp(spread * noise) if base else spread * noise
        out[name] = jnp.asarray(drawn.astype(out[name].dtype))
    for name, factor in factors.items():
        out[name] = (out[name] * factor).astype(out[name].dtype)
    return out
```

```python
from contextlib import ExitStack

import numpy as np
import concourse.bass as bass
from concourse import mybir

P = 128
NB, S, D = 2, 1024, 256
T = NB * S
NT = T // P
TB = S // P
DC = D // P
H, G, HD = 16, 4, 16
HG = H // G
LAT = 64
WIN = 64
U = 4
NI = NT // U
XB = U // 2
QKV = (H + 2 * G) * HD
QKH = H + G
VW = 3 * HD + 1
BG = NB * G
EPS_RMS, EPS_LN = 1e-6, 1e-5
SCALE = float(HD) ** -0.5
HIDE = -30000.0

F32, F32R = mybir.dt.float32, mybir.dt.float32r
BF16, F16 = mybir.dt.bfloat16, mybir.dt.float16
ALU = mybir.AluOpType
ACT = mybir.ActivationFunctionType
AX = mybir.AxisListType
ds = bass.ds

GLOBAL_UNITS = [(q, k) for q in range(TB) for k in range(q + 1)]
GLOBAL_STEPS = [[(q, k, P) for q, k in GLOBAL_UNITS[n:n + 2]] for n in range(0, len(GLOBAL_UNITS), 2)]
LOCAL_STEPS = [[(q, q, P)] + [(q, q - 1, WIN)] * (q > 0) for q in range(TB)]
STEPS = [GLOBAL_STEPS, LOCAL_STEPS]
DONE = [[max(n for n, step in enumerate(steps) if step[-1][0] >= q and step[0][0] <= q) for q in range(TB)]
        for steps in STEPS]
BASE = [0, BG * len(GLOBAL_STEPS)]
ON_POOL = [[n % 4 == 3 for n in range(len(steps))] for steps in STEPS]
CL = 77
CH = H // 2
CS = 2 * U
FMAX = float(np.finfo(np.float32).max)
E, FI = 8, 1024
FC = FI // P
FP = FC // 2
BLK = 256
BA = BLK // P
NBLK = 2 * T // BLK + E
NJ = T // BLK
THIRD = DC * FI
START = 5


def build_decoder(nc, x, wq0, kvdT, kvup, wo0, wq1, wk1, wv1, wo1, n1, n2, rope, tri,
                  ctxT, mask, xwq, xwk, xwv, xwo, xbq, xbk, xbv, xbo, router, experts, small, out):
    ctx = ExitStack()
    with ctx:
        def sb(name, shape, dt=F32):
            return ctx.enter_context(nc.sbuf_tensor(name, shape, dt))

        def sem(name):
            return ctx.enter_context(nc.semaphore(name))

        X = sb("X", [P, NT, D])
        tri_sb = sb("tri_sb", [P, 4, P])
        identF = tri_sb[:, 3, :]
        eps = sb("eps", [P, 2])
        root = sb("root", [P, NT])
        rstd = sb("rstd", [P, NT])

        small_sb = sb("small_sb", [P, 16 + E * NJ + NBLK + P])
        ST = sb("ST", [P, NT, 6])
        MV = sb("MV", [P, NT, 2])
        EB = sb("EB", [P, NBLK], mybir.dt.int32)
        SLOT = sb("SLOT", [P, 2, NT], mybir.dt.uint32)
        CO = sb("CO", [P, 2, NT])
        ONES = sb("ONES", [P, P])
        middle = ExitStack()

        def mb(name, shape, dt=F32):
            return middle.enter_context(nc.sbuf_tensor(name, shape, dt))

        ssq = mb("ssq", [P, NT])
        XN = mb("XN", [P, U, D])
        XT = mb("XT", [P, U, DC, P])
        WX = mb("WX", [P, 4, DC, D])
        ctx_sb = mb("ctx_sb", [P, DC, NB * CL])
        xb = mb("xb", [P, 2, DC])
        BV = mb("BV", [CL, D])
        BO = mb("BO", [P, D])
        KZ = mb("KZ", [P, NB, DC, CH, CL])
        VX = mb("VX", [CL, NB, H, HD + 1])
        MF = mb("MF", [P, NT, CL])
        RW = mb("RW", [P, DC, E])
        LG = mb("LG", [P, NT, E])
        early = ExitStack()

        def eb(name, shape, dt=F32):
            return early.enter_context(nc.sbuf_tensor(name, shape, dt))

        OA = eb("OA", [P, NT, D])
        W = [eb(f"W{l}", [P, DC, QKV]) for l in range(2)]
        WO = [eb(f"WO{l}", [P, DC, D]) for l in range(2)]
        kvd_sb = eb("kvd_sb", [LAT, D])
        kvup_sb = eb("kvup_sb", [LAT, 2 * G * HD])
        nw = eb("nw", [P, 2, DC])
        rope_sb = eb("rope_sb", [P, 2, 2, NT, HD])
        identH = eb("identH", [P, P], F16)
        identB = eb("identB", [P, P], BF16)
        hide = eb("hide", [P, 3, HG, P], BF16)
        KB = eb("KB", [P, DC, NB * CL])
        RS = eb("RS", [P, 2, U, QKH * HD])
        RAW, SQ = RS[:, 0], RS[:, 1]
        R1 = eb("R1", [P, U, QKH * HD])
        R2 = eb("R2", [P, U, QKH * HD])
        ss = eb("ss", [P, U * QKH])
        sr = eb("sr", [P, U * QKH])
        rn = eb("rn", [P, U * QKH])
        RQ = eb("RQ", [P, U * H, HD])
        RK = eb("RK", [P, U * G, HD])
        QS = eb("QS", [P, U * H, 4, HD], F16)
        KS = eb("KS", [P, U * G, 8, HD], F16)
        QT = eb("QT", [P, H // 2, T], F16)
        KT = eb("KT", [P, 2 * G, T], F16)
        VA = eb("VA", [P, NT * G, HD])
        VL1, VL2 = (r[:].rearrange("p u n -> p (u n)")[:, 0:NT * G * HD].rearrange("p (n d) -> p n d", d=HD) for r in (R1, R2))
        VS = eb("VS", [P, NT * G, VW], BF16)
        PF = RS[:].rearrange("p a u n -> p (a u n)")[:, 0:2 * 1024].rearrange("p (s n) -> p s n", s=2)
        PL = QS[:].rearrange("p n c d -> p (n c d)")[:, 0:2 * 1024].rearrange("p (s n) -> p s n", s=2)
        OS = eb("OS", [P, 2, HG, HD])
        OR = eb("OR", [P, 2, HG, 1])
        early.close()
        cross = ExitStack()

        def cb(name, shape, dt=F32):
            return cross.enter_context(nc.sbuf_tensor(name, shape, dt))

        XM = cb("XM", [P, DC, U * P])
        QC = cb("QC", [P, DC, U * P])
        CLG = cb("CLG", [P, 2, CH, CL])
        CMX = cb("CMX", [P, 2, CH, 1])
        CPX = cb("CPX", [P, 2, CH, CL])
        CPT = cb("CPT", [CL, CH, P])
        CR = cb("CR", [P, 2, CH, 1])
        OX = cb("OX", [P, U, D])
        rt = {n: cb(f"rt_{n}", [P, NT, E]) for n in
              ("eq1", "code1", "one1", "left", "eq2", "code2", "one2", "w1", "w2", "pfa", "pfb", "slot", "t1", "t2")}
        rc = {n: cb(f"rc_{n}", [P, NT]) for n in ("m1", "i1", "m2", "i2", "d", "e", "den", "r", "p2")}
        re = {n: cb(f"re_{n}", [P, E]) for n in ("cnt", "sumw", "nb", "bba", "bbb", "end", "one", "inv", "mean")}
        SW = cb("SW", [P, NT, 2 * E])
        TOT = cb("TOT", [P, NT, 2 * E])
        GTJ = cb("GTJ", [P, E, NJ])
        LEB = cb("LEB", [P, NBLK, E])
        EBF = cb("EBF", [P, NBLK])
        POSF = cb("POSF", [P, 2, NT])
        cross.close()
        middle.close()
        RAWW = sb("RAWW", [P, 3, THIRD])
        WH = [sb(f"WH{a}", [P, 3, THIRD], F32R) for a in range(2)]
        WL = [sb(f"WL{a}", [P, 3, THIRD], F32R) for a in range(2)]
        XR = sb("XR", [P, 2, BA, D])
        XH = [sb(f"XH{a}", [P, DC, BLK], F32R) for a in range(2)]
        XL = [sb(f"XL{a}", [P, DC, BLK], F32R) for a in range(2)]
        SG = sb("SG", [P, 2, 2, BLK])
        HF = sb("HF", [P, 2, 2, BLK])
        HH = [sb(f"HH{a}", [P, FC, BLK], F32R) for a in range(2)]
        HL = [sb(f"HL{a}", [P, FC, BLK], F32R) for a in range(2)]
        EO = sb("EO", [P, 2, BA, D])
        YB = RAWW[:].rearrange("p w n -> p (w n)")[:, 0:2 * 2 * U * D].rearrange("p (s k u d) -> p s k u d", s=2, k=2, u=U)
        XG = nc.dram_tensor("XG", [NBLK * BLK, D], F32).ap()
        YG = nc.dram_tensor("YG", [NBLK * BLK, D], F32).ap()

        PS = ctx.enter_context(nc.psum_tensor("PS", [P, 8, 512], F32))
        ps_x = PS[:, 0:2, :].rearrange("p a (u n) -> p (a u) n", u=2)
        ps_p = PS[:, 2:6, :]
        ps_q = PS[:, 6, :].bitcast(F16).rearrange("p (h n) -> p h n", h=H // 2)
        ps_k = PS[:, 7, 0:256].bitcast(F16).rearrange("p (g n) -> p g n", g=G)
        ps_s = PS[:, 0:4, :].rearrange("p (a b) n -> p a (b n)", a=2)
        ps_o = PS[:, 4:6, 0:HG * VW].rearrange("p a (h v) -> p a h v", h=HG)

        s_loadx = sem("s_loadx")
        s_loadw = sem("s_loadw")
        s_fuse = sem("s_fuse")
        s_weights = sem("s_weights")
        s_const = sem("s_const")
        s_square = sem("s_square")
        s_ssq = sem("s_ssq")
        s_root = sem("s_root")
        s_rstd = sem("s_rstd")
        s_xn = sem("s_xn")
        s_xt = sem("s_xt")
        s_xte = sem("s_xte")
        s_proj = sem("s_proj")
        s_raw = sem("s_raw")
        s_rot2 = sem("s_rot2")
        s_dve = sem("s_dve")
        s_hss = sem("s_hss")
        s_hroot = sem("s_hroot")
        s_split = sem("s_split")
        s_stack = sem("s_stack")
        s_vs = sem("s_vs")
        s_qkt = sem("s_qkt")
        s_qe = sem("s_qe")
        s_ke = sem("s_ke")
        s_score = sem("s_score")
        s_exp = sem("s_exp")
        s_low = sem("s_low")
        s_lowp = sem("s_lowp")
        s_pv = sem("s_pv")
        s_osum = sem("s_osum")
        s_on = sem("s_on")
        s_oproj = sem("s_oproj")
        s_res = sem("s_res")
        s_x0 = sem("s_x0")
        s_cload = sem("s_cload")
        s_ckv = sem("s_ckv")
        s_ckb = sem("s_ckb")
        s_ckz = sem("s_ckz")
        s_bn = sem("s_bn")
        s_stat = sem("s_stat")
        s_mv = sem("s_mv")
        s_xb = sem("s_xb")
        s_cq = sem("s_cq")
        s_cqe = sem("s_cqe")
        s_cs = sem("s_cs")
        s_clog = sem("s_clog")
        s_cmax = sem("s_cmax")
        s_csub = sem("s_csub")
        s_cexp = sem("s_cexp")
        s_cpt = sem("s_cpt")
        s_cpe = sem("s_cpe")
        s_cpv = sem("s_cpv")
        s_crec = sem("s_crec")
        s_con = sem("s_con")
        s_cwo = sem("s_cwo")
        s_cres = sem("s_cres")
        s_rl = sem("s_rl")
        s_rle = sem("s_rle")
        s_route = sem("s_route")
        s_gap = sem("s_gap")
        s_tot = sem("s_tot")
        s_zero = sem("s_zero")
        s_clear = sem("s_clear")
        s_scat = sem("s_scat")
        s_wl = [sem(f"s_wl{w}") for w in range(3)]
        s_wh = sem("s_wh")
        s_wlo = sem("s_wlo")
        s_xbl = [sem(f"s_xbl{a}") for a in range(2)]
        s_bt = sem("s_bt")
        s_bh = sem("s_bh")
        s_bl = sem("s_bl")
        s_gu = sem("s_gu")
        s_silu = sem("s_silu")
        s_hm = sem("s_hm")
        s_hh = sem("s_hh")
        s_hl = sem("s_hl")
        s_down = sem("s_down")
        s_eo = sem("s_eo")
        s_yg = sem("s_yg")
        s_eof = sem("s_eof")
        s_gat = [sem(f"s_gat{a}") for a in range(2)]
        s_mix = sem("s_mix")
        s_fin = sem("s_fin")
        s_out = sem("s_out")

        xv = x.rearrange("(t p) d -> p t d", p=P)
        ov = out.rearrange("(t p) d -> p t d", p=P)
        NLOAD = 12 * 16
        NCLOAD = 13 * 16
        NSHARES = 19
        NROUTE = 51
        KZf = KZ[:].rearrange("p b c h k -> p (b c h k)")
        VXf = VX[:].rearrange("k b h d -> k (b h d)")
        own = small_sb[:, 0:CH]
        expert_no = small_sb[:, 8:16]
        block_rows = small_sb[:, 16:16 + E * NJ]
        block_no = small_sb[:, 16 + E * NJ:16 + E * NJ + NBLK]
        before = small_sb[:, 16 + E * NJ + NBLK:]
        NDVE = 5
        NVS = 5
        KTf = KT[:].rearrange("p a t -> p (a t)")
        VSf = VS[:].rearrange("p n v -> p (n v)")
        KS2 = KS[:].rearrange("p n a d -> p n (a d)")
        QS2 = QS[:].rearrange("p (n e) a d -> p n (e a d)", e=2)
        block = ctx.enter_context(nc.Block())

        @block.sync
        def _(sp):
            for i in range(NI):
                sp.dma_start(X[:, U * i:U * i + U, :], xv[:, U * i:U * i + U, :]).then_inc(s_loadx, 16)
            for l, wq in enumerate((wq0, wq1)):
                sp.dma_start(W[l][:, :, 0:D], wq.rearrange("(c p) n -> p c n", p=P)).then_inc(s_loadw, 16)
            sp.dma_start(W[1][:, :, D:D + 64], wk1.rearrange("(c p) n -> p c n", p=P)).then_inc(s_loadw, 16)
            sp.dma_start(W[1][:, :, D + 64:D + 128], wv1.rearrange("(c p) n -> p c n", p=P)).then_inc(s_loadw, 16)
            sp.dma_start(kvd_sb[:], kvdT).then_inc(s_loadw, 16)
            sp.dma_start(kvup_sb[:], kvup).then_inc(s_loadw, 16)
            sp.dma_start(nw[:, 0, :], n1).then_inc(s_loadw, 16)
            sp.dma_start(nw[:, 1, :], n2).then_inc(s_loadw, 16)
            sp.dma_start(rope_sb[:], rope).then_inc(s_loadw, 16)
            sp.dma_start(tri_sb[:], tri).then_inc(s_loadw, 16)
            for l, wo in enumerate((wo0, wo1)):
                sp.dma_start(WO[l][:], wo.rearrange("(c p) n -> p c n", p=P)).then_inc(s_loadw, 16)
            for n, w in enumerate((xwq, xwk, xwv, xwo)):
                sp.dma_start(WX[:, n], w.rearrange("(c p) n -> p c n", p=P)).then_inc(s_cload, 16)
            sp.dma_start(ctx_sb[:], ctxT.rearrange("(c p) n -> p c n", p=P)).then_inc(s_cload, 16)
            sp.dma_start(xb[:, 0, :], xbq).then_inc(s_cload, 16)
            sp.dma_start(xb[:, 1, :], xbk).then_inc(s_cload, 16)
            sp.dma_start(BV[:], xbv.to_broadcast([CL, D])).then_inc(s_cload, 16)
            sp.dma_start(BO[:], xbo.to_broadcast([P, D])).then_inc(s_cload, 16)
            for b in range(NB):
                sp.dma_start(MF[:, b * TB:(b + 1) * TB, :], mask.rearrange("(t p) k -> p t k", p=P)).then_inc(s_cload, 16)
            sp.dma_start(small_sb[:], small).then_inc(s_cload, 16)
            sp.dma_start(RW[:], router.rearrange("(c p) e -> p c e", p=P)).then_inc(s_cload, 16)
            sp.wait_ge(s_zero, 1)
            for n in range(NBLK):
                sp.dma_start(XG[n * BLK:(n + 1) * BLK, :].rearrange("(p a) d -> p (a d)", p=P // 2),
                             KT[P // 2:P, 0, :].bitcast(F32)).then_inc(s_clear, 16)
            for i in range(NI):
                sp.wait_ge(s_xn, START + 3 * NI + i + 1)
                sp.dma_start(OA[:, U * i:U * i + U, :], xv[:, U * i:U * i + U, :]).then_inc(s_x0, 16)

            def load_block(m, par, half):
                e = sp.value_load(EB[0:1, ds(m, 1)], min_val=0, max_val=E - 1)
                for w in range(3):
                    sp.wait_ge(s_wlo, START + m * 3 + w - 2)
                    sp.dma_start(RAWW[:, w, :], experts[ds(e, 1), :, w * THIRD:(w + 1) * THIRD]
                                 .rearrange("a p n -> p (a n)")).then_inc(s_wl[w], 16)
                sp.wait_ge(s_bt, START + m - 1)
                sp.dma_start(XR[:, par], XG[ds(m * BLK, BLK), :].rearrange("(a p) d -> p a d", p=P)).then_inc(s_xbl[par], 16)

            sp.wait_ge(s_route, NROUTE)
            sp.wait_ge(s_scat, 32 * NT)
            with sp.Fori(0, NBLK // 2) as j:
                for par in range(2):
                    load_block(j * 2 + par, par, j)
            for i in range(NI):
                sp.wait_ge(s_fin, i + 1)
                sp.dma_start(ov[:, U * i:U * i + U, :], X[:, U * i:U * i + U, :]).then_inc(s_out, 16)
            sp.wait_ge(s_out, 16 * NI)

        @block.gpsimd
        def _(pool):
            pool.sem_inc(s_rot2, START)
            pool.sem_inc(s_stack, START)
            pool.sem_inc(s_lowp, START)
            pool.memset(eps[:, 0:1], EPS_RMS)
            pool.memset(eps[:, 1:2], EPS_LN)
            pool.memset(VS[:, :, 3 * HD:VW], 1.0).then_inc(s_const, 1)
            pool.memset(ONES[:], 1.0)
            pool.wait_ge(s_loadw, NLOAD)
            pool.tensor_copy(identH[:], identF)
            pool.tensor_copy(identB[:], identF)
            pool.tensor_copy(hide[:], tri_sb[:, 0:3, :].unsqueeze(2).to_broadcast([P, 3, HG, P])).then_inc(s_const, 1)

            def rotate_and_stack(l, i):
                n = l * NI + i
                pool.wait_ge(s_raw, START + n * U + U)
                rv = RAW.rearrange("p u (h d e) -> p u h d e", h=QKH, e=2)
                r2 = R2[:].rearrange("p u (h d e) -> p u h d e", h=QKH, e=2)
                sv = rope_sb[:, l, 1, ds(i * U, U), :].rearrange("p t (d e) -> p t d e", e=2)
                for e in range(2):
                    last = pool.tensor_tensor(
                        r2[:, :, :, :, e], rv[:, :, :, :, 1 - e],
                        sv[:, :, :, e].unsqueeze(2).to_broadcast([P, U, QKH, HD // 2]), ALU.mult)
                last.then_inc(s_rot2, 1)
                pool.wait_ge(s_split, START + n + 1)
                pool.tensor_tensor(QS[:, :, 3, :], RQ[:], QS[:, :, 0, :], ALU.subtract)
                pool.tensor_copy(QS[:, :, 1, :], QS[:, :, 0, :])
                k2 = KS[:].rearrange("p n (r c) d -> p n r (c d)", r=4)
                pool.tensor_copy(k2[:, :, 1:4, :], k2[:, :, 0:1, :].to_broadcast([P, U * G, 3, 2 * HD])).then_inc(s_stack, 1)

            def split_values(l):
                part = [VS[:, :, c * HD:(c + 1) * HD] for c in range(3)]
                pool.wait_ge(s_split, START + (l + 1) * NI)
                pool.tensor_copy(part[0], VA[:]).then_inc(s_vs, 1)
                pool.wait_ge(s_vs, l * NVS + 1)
                pool.tensor_tensor(VL1, VA[:], part[0], ALU.subtract).then_inc(s_vs, 1)
                pool.wait_ge(s_vs, l * NVS + 2)
                pool.tensor_copy(part[1], VL1).then_inc(s_vs, 1)
                pool.wait_ge(s_vs, l * NVS + 3)
                pool.tensor_tensor(VL2, VL1, part[1], ALU.subtract).then_inc(s_vs, 1)
                pool.wait_ge(s_vs, l * NVS + 4)
                pool.tensor_copy(part[2], VL2).then_inc(s_vs, 1)

            def low_parts(l, it):
                for n, step in enumerate(STEPS[l]):
                    if ON_POOL[l][n]:
                        at = BASE[l] + it * len(STEPS[l]) + n
                        cols = sum(HG * w for _, _, w in step)
                        pool.wait_ge(s_exp, START + at + 1)
                        pool.wait_ge(s_pv, START + at - 1)
                        pf = PF[:, n % 2, 0:cols]
                        pool.tensor_tensor(PL[:, n % 2, 0:cols], pf, high_part(pf), ALU.subtract).then_inc(s_lowp, 1)

            for l in range(2):
                with pool.Fori(0, NI) as i:
                    rotate_and_stack(l, i)
                split_values(l)
                with pool.Fori(0, BG) as it:
                    low_parts(l, it)
                pool.wait_ge(s_on, START + (l + 1) * BG * TB)
                with pool.Fori(0, NI) as i:
                    pool.wait_ge(s_xt, START + ((2 * l + 1) * NI + i) * XB)
                    pool.tensor_copy(XN[:], OA[:, ds(i * U, U), :]).then_inc(s_xn, 1)
            pool.sem_inc(s_xb, START)
            with pool.Fori(0, NI) as i:
                pool.wait_ge(s_xn, START + 4 * NI + i + 1)
                pool.tensor_tensor(X[:, ds(i * U, U), :], XN[:], BO[:].unsqueeze(1).to_broadcast([P, U, D]),
                                   ALU.add).then_inc(s_xb, 1)
            pool.wait_ge(s_route, NROUTE)
            pool.wait_ge(s_clear, 16 * (NBLK))
            for k in range(2):
                for t in range(NT):
                    pool.indirect_dma_start(XG[:, :], bass.IndirectOffsetOnAxis(SLOT[:, k, t:t + 1], 0),
                                            X[:, t, :], None).then_inc(s_scat, 16)
            pool.sem_inc(s_eof, START)
            with pool.Fori(0, NBLK // 2) as j:
                for par in range(2):
                    m = j * 2 + par
                    pool.wait_ge(s_eo, START + m + 1)
                    pool.dma_start(YG[ds(m * BLK, BLK), :].rearrange("(a p) d -> p a d", p=P), EO[:, par]).then_inc(s_yg, 16)
                    pool.wait_ge(s_yg, 16 * m + 16)
                    pool.sem_inc(s_eof, 1)
            pool.wait_ge(s_yg, 16 * NBLK)
            for i in range(NI):
                if i >= 2:
                    pool.wait_ge(s_stat, 2 * NI + i - 1)
                for k in range(2):
                    for u in range(U):
                        pool.indirect_dma_start(YB[:, i % 2, k, u, :], None, YG[:, :],
                                                bass.IndirectOffsetOnAxis(SLOT[:, k, i * U + u:i * U + u + 1], 0)
                                                ).then_inc(s_gat[i % 2], 16)

        @block.scalar
        def _(act):
            act.sem_inc(s_square, START)
            act.sem_inc(s_root, START)
            act.sem_inc(s_xte, START)
            act.sem_inc(s_raw, START)
            act.sem_inc(s_hroot, START)
            act.sem_inc(s_qe, START)
            act.sem_inc(s_exp, START)
            for s in (s_cqe, s_cexp, s_cpe, s_rle, s_wh, s_bh, s_silu, s_hh, s_eo):
                act.sem_inc(s, START)

            def squares(n, i):
                act.wait_ge(s_ssq, START + n)
                act.activation(RAW.rearrange("p u n -> p (u n)")[:, 0:U * D],
                               X[:, ds(i * U, U), :].rearrange("p u n -> p (u n)"), ACT.Square).then_inc(s_square, 1)

            def tiles_out(k, i):
                for v in range(XB):
                    act.wait_ge(s_xt, START + (k * NI + i) * XB + v + 1)
                    act.copy(XT[:, 2 * v:2 * v + 2].rearrange("p u c n -> p (u c n)"), PS[:, v, :]).then_inc(s_xte, 1)

            def project(l, i):
                n = l * NI + i
                tiles_out(2 * l, i)
                for u in range(U):
                    act.wait_ge(s_proj, START + n * U + u + 1)
                    if u == 0:
                        act.wait_ge(s_split, START + n)
                    act.copy(RAW[:, u, :], ps_p[:, u, 0:QKH * HD])
                    act.copy(VA[:, ds((i * U + u) * G, G), :], ps_p[:, u, QKH * HD:QKV])
                    act.activation(SQ[:, u, :], ps_p[:, u, 0:QKH * HD], ACT.Square).then_inc(s_raw, 1)
                act.wait_ge(s_hss, START + n + 1)
                act.activation(sr[:], ss[:], ACT.Sqrt, bias=eps[:, 0:1], scale=1.0 / HD).then_inc(s_hroot, 1)

            def stacks_out(l, i):
                for u in range(U):
                    act.wait_ge(s_qkt, START + (l * NI + i) * U + u + 1)
                    act.copy(QT[:, :, ds((i * U + u) * P, P)], ps_q).then_inc(s_qe, 1)

            def exponentials(l, it):
                for n, step in enumerate(STEPS[l]):
                    at = BASE[l] + it * len(STEPS[l]) + n
                    cols = sum(HG * w for _, _, w in step)
                    act.wait_ge(s_score, START + at + 1)
                    act.wait_ge(s_pv, START + at - 1)
                    act.activation(PF[:, n % 2, 0:cols], ps_s[:, n % 2, 0:cols], ACT.Exp, scale=SCALE).then_inc(s_exp, 1)

            act.wait_ge(s_const, 1)
            act.wait_ge(s_loadx, 16 * NI)
            with act.Fori(0, NI) as i:
                squares(i, i)
            for l in range(2):
                act.wait_ge(s_ssq, START + (l + 1) * NI)
                act.activation(root[:], ssq[:], ACT.Sqrt, bias=eps[:, 0:1], scale=1.0 / D).then_inc(s_root, 1)
                project(l, 0)
                with act.Fori(1, NI) as i:
                    project(l, i)
                    stacks_out(l, i - 1)
                stacks_out(l, NI - 1)
                with act.Fori(0, BG) as it:
                    exponentials(l, it)
                with act.Fori(0, NI) as i:
                    tiles_out(2 * l + 1, i)
                    for u in range(U):
                        act.wait_ge(s_oproj, START + (l * NI + i) * U + u + 1)
                    if l == 0:
                        act.wait_ge(s_res, START + i + 1)
                        squares(i + NI, i)

            def roots(n):
                act.wait_ge(s_mv, n)
                act.activation(root[:], MV[:, :, 1], ACT.Sqrt, bias=eps[:, 1:2]).then_inc(s_root, 1)

            def chunks_out(n):
                for v in range(XB):
                    act.wait_ge(s_xt, START + n * XB + v + 1)
                    act.copy(XM[:].rearrange("p c (u n) -> p u c n", u=U)[:, 2 * v:2 * v + 2],
                             PS[:, v, :].rearrange("p (u c n) -> p u c n", u=2, c=DC)).then_inc(s_xte, 1)

            roots(1)
            with act.Fori(0, NI) as i:
                chunks_out(4 * NI + i * 2)
                for o in range(DC):
                    act.wait_ge(s_cq, START + i * DC + o + 1)
                    act.activation(QC[:, o, :], PS[:, 2 + o, :], ACT.Identity, bias=xb[:, 0, o:o + 1]).then_inc(s_cqe, 1)
                for m in range(CS):
                    at = i * CS + m
                    act.wait_ge(s_csub, START + at + 1)
                    act.wait_ge(s_cpt, START + at - 1)
                    act.activation(CPX[:, m % 2], CLG[:, m % 2], ACT.Exp).then_inc(s_cexp, 1)
                    act.wait_ge(s_cpt, START + at + 1)
                    act.copy(CPT[:].rearrange("k h n -> k (h n)"), PS[0:CL, 0:2, :].rearrange("k a n -> k (a n)")).then_inc(s_cpe, 1)
                n = 4 * NI + i * 2 + 1
                for v in range(XB):
                    act.wait_ge(s_xt, START + n * XB + v + 1)
                    act.copy(XT[:, 2 * v:2 * v + 2].rearrange("p u c n -> p (u c n)"), PS[:, v, :]).then_inc(s_xte, 1)
            roots(2)
            with act.Fori(0, NI) as i:
                tiles_out(6, i)
                act.wait_ge(s_rl, START + i + 1)
                act.copy(LG[:, ds(i * U, U), :], PS[:, 2, 0:U * E].rearrange("p (u e) -> p u e", e=E)).then_inc(s_rle, 1)
            act.wait_ge(s_route, 12)
            act.activation(rc["e"][:], rc["d"][:], ACT.Exp).then_inc(s_gap, 1)

            def high_weights(m, par, w):
                act.wait_ge(s_wl[w], 16 * m + 16)
                if w == 0:
                    act.wait_ge(s_gu, START + (m - 1) * FP)
                if w == 2:
                    act.wait_ge(s_down, START + m - 1)
                act.copy(WH[par][:, w, :], RAWW[:, w, :]).then_inc(s_wh, 1)

            def high_rows(m, par):
                act.wait_ge(s_bt, START + m + 1)
                act.copy(XH[par][:].rearrange("p c n -> p (c n)"), PS[:, 7, :]).then_inc(s_bh, 1)

            def expert_block(m, par, first=False, last=False):
                for q in range(FP):
                    at = m * FP + q
                    act.wait_ge(s_gu, START + at + 1)
                    act.wait_ge(s_hm, START + at - 1)
                    act.activation(SG[:, q % 2], PS[:, 2 * (q % 2):2 * (q % 2) + 2, 0:BLK], ACT.Silu).then_inc(s_silu, 1)
                    if not last and q != 2:
                        high_weights(m + 1, 1 - par, {0: 0, 1: 1, 3: 2}[q])
                    if q == 2 and not first:
                        block_out(m - 1, 1 - par)
                    act.wait_ge(s_hm, START + at + 1)
                    if q == 0:
                        act.wait_ge(s_down, START + m - 1)
                    act.copy(HH[par][:, 2 * q:2 * q + 2, :], HF[:, q % 2]).then_inc(s_hh, 1)
                    if q == 2 and not last:
                        high_rows(m + 1, 1 - par)

            def block_out(m, par):
                act.wait_ge(s_down, START + m + 1)
                act.wait_ge(s_eof, START + m - 1)
                act.copy(EO[:, par].rearrange("p a d -> p (a d)"), PS[:, 4 + par, :]).then_inc(s_eo, 1)

            for w in range(3):
                high_weights(0, 0, w)
            high_rows(0, 0)
            expert_block(0, 0, first=True)
            with act.Fori(0, NBLK // 2 - 1) as j:
                expert_block(j * 2 + 1, 1)
                expert_block(j * 2 + 2, 0)
            expert_block(NBLK - 1, 1, last=True)
            block_out(NBLK - 1, 1)
            roots(3)

        @block.vector
        def _(dve):
            dve.sem_inc(s_ssq, START)
            dve.sem_inc(s_rstd, START)
            dve.sem_inc(s_xn, START)
            dve.sem_inc(s_dve, START)
            dve.sem_inc(s_hss, START)
            dve.sem_inc(s_split, START)
            dve.sem_inc(s_ke, START)
            dve.sem_inc(s_low, START)
            dve.sem_inc(s_osum, START)
            dve.sem_inc(s_on, START)
            dve.sem_inc(s_res, START)
            for s in (s_bn, s_clog, s_cmax, s_csub, s_crec, s_con, s_cres, s_wlo, s_bl, s_hm, s_hl):
                dve.sem_inc(s, START)

            def sums(n, i):
                dve.wait_ge(s_square, START + n + 1)
                dve.tensor_reduce(ssq[:, ds(i * U, U)], RAW.rearrange("p u n -> p (u n)")[:, 0:U * D]
                                  .rearrange("p (u n) -> p u n", u=U), AX.X, ALU.add).then_inc(s_ssq, 1)

            def normalise(l, i):
                dve.wait_ge(s_xt, START + (2 * l * NI + i) * XB)
                dve.tensor_tensor(XN[:], X[:, ds(i * U, U), :],
                                  rstd[:, ds(i * U, U)].unsqueeze(2).to_broadcast([P, U, D]), ALU.mult).then_inc(s_xn, 1)

            def rotate(l, i):
                n = l * NI + i
                step = START + n * NDVE
                dve.wait_ge(s_raw, START + n * U + U)
                four = lambda a: a[:].rearrange("p u (h d) -> p u h d", h=QKH)
                dve.tensor_tensor(four(R1), RAW.rearrange("p u (h d) -> p u h d", h=QKH),
                                  rope_sb[:, l, 0, ds(i * U, U), :].unsqueeze(2).to_broadcast([P, U, QKH, HD]),
                                  ALU.mult).then_inc(s_dve, 1)
                dve.tensor_reduce(ss[:], SQ.rearrange("p u (h d) -> p (u h) d", d=HD), AX.X, ALU.add).then_inc(s_hss, 1)
                dve.wait_ge(s_rot2, START + n + 1)
                dve.wait_ge(s_dve, step + 1)
                dve.tensor_tensor(R1[:], R1[:], R2[:], ALU.add).then_inc(s_dve, 1)
                dve.wait_ge(s_hroot, START + n + 1)
                dve.reciprocal(rn[:], sr[:]).then_inc(s_dve, 1)
                dve.wait_ge(s_dve, step + 3)
                r = four(R1)
                inv = rn[:].rearrange("p (u h) -> p u h", u=U)
                for dst, a, b in ((RQ, 0, H), (RK, H, QKH)):
                    last = dve.tensor_tensor(dst[:].rearrange("p (u h) d -> p u h d", u=U), r[:, :, a:b, :],
                                             inv[:, :, a:b].unsqueeze(3).to_broadcast([P, U, b - a, HD]), ALU.mult)
                last.then_inc(s_dve, 1)

            def split(l, i):
                n = l * NI + i
                step = START + n * NDVE
                dve.wait_ge(s_qkt, START + n * U)
                dve.wait_ge(s_dve, step + 4)
                dve.tensor_copy(QS[:, :, 0, :], RQ[:])
                dve.tensor_copy(KS[:, :, 0, :], RK[:]).then_inc(s_dve, 1)
                dve.wait_ge(s_dve, step + 5)
                dve.tensor_tensor(QS[:, :, 2, :], RQ[:], QS[:, :, 0, :], ALU.subtract)
                dve.tensor_tensor(KS[:, :, 1, :], RK[:], KS[:, :, 0, :], ALU.subtract).then_inc(s_split, 1)

            def stacks_out(l, i):
                k4 = KT[:].rearrange("p (g e) t -> p g e t", e=2)
                for u in range(U):
                    t = ds((i * U + u) * P, P)
                    dve.wait_ge(s_qkt, START + (l * NI + i) * U + u + 1)
                    dve.tensor_copy(k4[0:64, :, 0, t], ps_k[0:64])
                    dve.tensor_copy(k4[64:P, :, 1, t], ps_k[64:P]).then_inc(s_ke, 1)

            def attend(l, b, g):
                it = b * G + g
                steps = STEPS[l]
                for n, step in enumerate(steps):
                    at = BASE[l] + it * len(steps) + n
                    if not ON_POOL[l][n]:
                        cols = sum(HG * w for _, _, w in step)
                        dve.wait_ge(s_exp, START + at + 1)
                        dve.wait_ge(s_pv, START + at - 1)
                        pf = PF[:, n % 2, 0:cols]
                        dve.tensor_tensor(PL[:, n % 2, 0:cols], pf, high_part(pf), ALU.subtract).then_inc(s_low, 1)
                    for q in range(TB):
                        if DONE[l][q] == n - 1:
                            finish(l, b, g, it, q)
                finish(l, b, g, it, TB - 1)

            def finish(l, b, g, it, q):
                a, k = q % 2, l * BG * TB + it * TB + q
                dve.wait_ge(s_pv, START + BASE[l] + it * len(STEPS[l]) + DONE[l][q] + 1)
                dve.reciprocal(OR[:, a], ps_o[:, a, :, 3 * HD:VW])
                dve.tensor_reduce(OS[:, a], ps_o[:, a, :, 0:3 * HD].rearrange("p h (c d) -> p h d c", c=3),
                                  AX.X, ALU.add).then_inc(s_osum, 1)
                dve.wait_ge(s_osum, START + k + 1)
                dve.tensor_tensor(OA[:, ds(b * TB + q, 1), ds(g * HG * HD, HG * HD)].rearrange("p a (h d) -> p (a h) d", h=HG),
                                  OS[:, a], OR[:, a].to_broadcast([P, HG, HD]), ALU.mult).then_inc(s_on, 1)

            k4 = KT[:].rearrange("p (g e) t -> p g e t", e=2)
            dve.memset(k4[64:P, :, 0, :], 0.0)
            dve.memset(k4[0:64, :, 1, :], 0.0).then_inc(s_zero, 1)
            dve.wait_ge(s_loadw, NLOAD)
            dve.wait_ge(s_fuse, 1)
            for c in range(DC):
                dve.tensor_scalar(W[0][:, c, D:QKV], PS[:, 6 + c, 0:P], nw[:, 0, c:c + 1], None, ALU.mult)
                dve.tensor_scalar(W[0][:, c, 0:D], W[0][:, c, 0:D], nw[:, 0, c:c + 1], None, ALU.mult)
                last = dve.tensor_scalar(W[1][:, c, :], W[1][:, c, :], nw[:, 1, c:c + 1], None, ALU.mult)
            last.then_inc(s_weights, 1)
            dve.wait_ge(s_cload, NCLOAD)
            dve.wait_ge(s_ckv, 1)
            for o in range(DC):
                last = dve.tensor_scalar(KB[:, o, :], PS[:, 4 + o, 0:NB * CL], xb[:, 1, o:o + 1], None, ALU.add)
            for b in range(NB):
                last = dve.tensor_tensor(VX[:, b, :, 0:HD], PS[0:CL, 2 + b, 0:D].rearrange("k (h d) -> k h d", h=H),
                                         BV[:].rearrange("k (h d) -> k h d", h=H), ALU.add)
            last.then_inc(s_ckb, 1)
            dve.wait_ge(s_ckb, 1)
            for b in range(NB):
                for o in range(DC):
                    last = dve.tensor_tensor(KZ[:, b, o], KB[:, o, b * CL:(b + 1) * CL].unsqueeze(1).to_broadcast([P, CH, CL]),
                                             own.unsqueeze(2).to_broadcast([P, CH, CL]), ALU.mult)
            dve.tensor_scalar(MF[:], MF[:], FMAX, None, ALU.mult)
            last = dve.memset(VX[:, :, :, HD:HD + 1], 1.0)
            last.then_inc(s_ckz, 1)
            with dve.Fori(0, NI) as i:
                sums(i, i)
            for l in range(2):
                dve.wait_ge(s_root, START + l + 1)
                dve.reciprocal(rstd[:], root[:]).then_inc(s_rstd, 1)
                dve.wait_ge(s_rstd, START + l + 1)
                normalise(l, 0)
                rotate(l, 0)
                split(l, 0)
                with dve.Fori(1, NI) as i:
                    normalise(l, i)
                    rotate(l, i)
                    stacks_out(l, i - 1)
                    split(l, i)
                stacks_out(l, NI - 1)
                with dve.Fori(0, NB) as b:
                    with dve.Fori(0, G) as g:
                        attend(l, b, g)
                with dve.Fori(0, NI) as i:
                    dve.wait_ge(s_oproj, START + (l * NI + i) * U + U)
                    xs = X[:, ds(i * U, U), :]
                    dve.tensor_tensor(xs, xs, ps_p[:, :, 0:D], ALU.add).then_inc(s_res, 1)
                    if l == 0:
                        sums(i + NI, i)

            def means(n):
                dve.wait_ge(s_stat, n * NI)
                for t in range(NT):
                    last = dve.bn_aggr(MV[:, t, :], ST[:, t, :])
                last.then_inc(s_mv, 1)
                dve.wait_ge(s_root, START + 2 + n)
                dve.reciprocal(rstd[:], root[:]).then_inc(s_rstd, 1)
                dve.wait_ge(s_rstd, START + 2 + n)
                dve.wait_ge(s_mv, n)

            def rows(dst, i, u):
                t = i * U + u
                return dve.tensor_scalar(dst, X[:, ds(t, 1), :].rearrange("p a d -> p (a d)"),
                                         MV[:, ds(t, 1), 0], rstd[:, ds(t, 1)], ALU.subtract, ALU.mult)

            def statistics(i):
                for u in range(U):
                    last = dve.bn_stats(ST[:, ds(i * U + u, 1), :].rearrange("p a s -> p (a s)"),
                                        X[:, ds(i * U + u, 1), :].rearrange("p a d -> p (a d)"))
                last.then_inc(s_stat, 1)

            dve.wait_ge(s_x0, 16 * NI)
            dve.wait_ge(s_res, START + 2 * NI)
            with dve.Fori(0, NI) as i:
                xs = X[:, ds(i * U, U), :]
                dve.tensor_tensor(xs, xs, OA[:, ds(i * U, U), :], ALU.add).then_inc(s_bn, 1)
                dve.wait_ge(s_bn, START + i + 1)
                statistics(i)
            means(1)
            with dve.Fori(0, NI) as i:
                dve.wait_ge(s_xt, START + (4 * NI + i * 2) * XB)
                for u in range(U):
                    last = rows(XN[:, u, :], i, u)
                last.then_inc(s_xn, 1)

                def normalise_step(m):
                    u, o, a = m // DC, m % DC, m % 2
                    at = i * CS + m
                    dve.wait_ge(s_cpv, START + at + 1)
                    ps = PS[:, 2 + o, 0:CH * (HD + 1)].rearrange("p (h d) -> p h d", h=CH)
                    dve.reciprocal(CR[:, a], ps[:, :, HD:HD + 1]).then_inc(s_crec, 1)
                    dve.wait_ge(s_crec, START + at + 1)
                    dve.tensor_tensor(OX[:, u, o * P:(o + 1) * P].rearrange("p (h d) -> p h d", h=CH),
                                      ps[:, :, 0:HD], CR[:, a].to_broadcast([P, CH, HD]), ALU.mult).then_inc(s_con, 1)

                for m in range(CS):
                    u, o, a = m // DC, m % DC, m % 2
                    at = i * CS + m
                    dve.wait_ge(s_cs, START + at + 1)
                    dve.wait_ge(s_cexp, START + at - 1)
                    ps = PS[:, 4 + 2 * a:6 + 2 * a, 0:CH // 2 * CL].rearrange("p b (h k) -> p b h k", h=CH // 2)
                    lg = CLG[:, a].rearrange("p (b h) k -> p b h k", b=2)
                    mf = MF[:, ds(i * U + u, 1), :]
                    dve.tensor_tensor(lg, ps, mf.unsqueeze(1).to_broadcast([P, 2, CH // 2, CL]), ALU.subtract).then_inc(s_clog, 1)
                    dve.wait_ge(s_clog, START + at + 1)
                    dve.tensor_reduce(CMX[:, a], CLG[:, a], AX.X, ALU.max).then_inc(s_cmax, 1)
                    dve.wait_ge(s_cmax, START + at + 1)
                    dve.tensor_tensor(CLG[:, a], CLG[:, a], CMX[:, a].to_broadcast([P, CH, CL]), ALU.subtract).then_inc(s_csub, 1)
                    if m:
                        normalise_step(m - 1)
                normalise_step(CS - 1)
                dve.wait_ge(s_cwo, START + i * XB + XB)
                dve.wait_ge(s_xb, START + i + 1)
                xs = X[:, ds(i * U, U), :]
                dve.tensor_tensor(xs, xs, PS[:, 2:4, :].rearrange("p b (u d) -> p (b u) d", u=2), ALU.add).then_inc(s_cres, 1)
                dve.wait_ge(s_cres, START + i + 1)
                statistics(i)
            means(2)
            with dve.Fori(0, NI) as i:
                dve.wait_ge(s_xt, START + (6 * NI + i) * XB)
                for u in range(U):
                    rows(XN[:, u, :], i, u)
                    last = rows(X[:, ds(i * U + u, 1), :].rearrange("p a d -> p (a d)"), i, u)
                last.then_inc(s_xn, 1)

            count = [0]

            def then(ins):
                count[0] += 1
                ins.then_inc(s_route, 1)
                dve.wait_ge(s_route, count[0])

            te = [P, NT, E]
            dve.wait_ge(s_rle, START + NI)
            wide = lambda a: a.unsqueeze(2).to_broadcast(te)
            each = lambda a: a.unsqueeze(1).to_broadcast(te)
            first_of = []
            for k, logits in (("1", LG[:]), ("2", rt["left"][:])):
                if k == "2":
                    then(dve.scalar_tensor_tensor(out=rt["left"][:], in0=rt["one1"][:], scalar=-FMAX, in1=LG[:],
                                                  op0=ALU.mult, op1=ALU.add))
                then(dve.tensor_reduce(rc["m" + k][:], logits, AX.X, ALU.max))
                then(dve.tensor_tensor(rt["eq" + k][:], logits, wide(rc["m" + k][:]), ALU.is_equal))
                then(dve.scalar_tensor_tensor(out=rt["code" + k][:], in0=rt["eq" + k][:], scalar=-float(E),
                                              in1=each(expert_no), op0=ALU.mult, op1=ALU.add))
                then(dve.tensor_reduce(rc["i" + k][:], rt["code" + k][:], AX.X, ALU.min))
                then(dve.tensor_tensor(rt["one" + k][:], rt["code" + k][:], wide(rc["i" + k][:]), ALU.is_equal))
            then(dve.tensor_tensor(rc["d"][:], rc["m2"][:], rc["m1"][:], ALU.subtract))
            then(dve.tensor_tensor(SW[:, :, 0:E], rt["one1"][:], rt["one2"][:], ALU.add))
            dve.wait_ge(s_gap, 1)
            then(dve.tensor_scalar(rc["den"][:], rc["e"][:], 1.0, None, ALU.add))
            then(dve.reciprocal(rc["r"][:], rc["den"][:]))
            then(dve.tensor_tensor(rc["p2"][:], rc["e"][:], rc["r"][:], ALU.mult))
            then(dve.tensor_tensor(rt["w1"][:], rt["one1"][:], wide(rc["r"][:]), ALU.mult))
            then(dve.tensor_tensor(rt["w2"][:], rt["one2"][:], wide(rc["p2"][:]), ALU.mult))
            then(dve.tensor_tensor(SW[:, :, E:2 * E], rt["w1"][:], rt["w2"][:], ALU.add))
            assert count[0] == NSHARES
            dve.wait_ge(s_tot, 1)
            then(dve.tensor_copy(TOT[:].rearrange("p t e -> p (t e)"), PS[:, 3, 0:NT * 2 * E]))
            dve.memset(rt["pfa"][:, 0:1, :], 0.0)
            then(dve.tensor_copy(rt["pfa"][:, 1:NT, :], TOT[:, 0:NT - 1, 0:E]))
            a, b = rt["pfa"], rt["pfb"]
            for d in (1, 2, 4, 8):
                dve.tensor_copy(b[:, 0:d, :], a[:, 0:d, :])
                then(dve.tensor_tensor(b[:, d:NT, :], a[:, d:NT, :], a[:, 0:NT - d, :], ALU.add))
                a, b = b, a
            then(dve.tensor_tensor(rt["t1"][:], a[:], PS[:, 4, 0:NT * E].rearrange("p (t e) -> p t e", e=E), ALU.add))
            then(dve.tensor_tensor(re["cnt"][:], a[:, NT - 1, :], TOT[:, NT - 1, 0:E], ALU.add))
            then(dve.tensor_tensor(GTJ[:], re["cnt"][:].unsqueeze(2).to_broadcast([P, E, NJ]),
                                   block_rows.rearrange("p (e j) -> p e j", e=E), ALU.is_gt))
            then(dve.tensor_reduce(re["nb"][:], GTJ[:], AX.X, ALU.add))
            dve.memset(re["bba"][:, 0:1], 0.0)
            then(dve.tensor_copy(re["bba"][:, 1:E], re["nb"][:, 0:E - 1]))
            a, b = re["bba"], re["bbb"]
            for d in (1, 2, 4):
                dve.tensor_copy(b[:, 0:d], a[:, 0:d])
                then(dve.tensor_tensor(b[:, d:E], a[:, d:E], a[:, 0:E - d], ALU.add))
                a, b = b, a
            then(dve.tensor_tensor(re["end"][:], a[:], re["nb"][:], ALU.add))
            then(dve.tensor_tensor(LEB[:], re["end"][:].unsqueeze(1).to_broadcast([P, NBLK, E]),
                                   block_no.unsqueeze(2).to_broadcast([P, NBLK, E]), ALU.is_le))
            then(dve.tensor_reduce(EBF[:], LEB[:], AX.X, ALU.add))
            then(dve.tensor_scalar(EB[:], EBF[:], float(E - 1), None, ALU.min))
            then(dve.scalar_tensor_tensor(out=rt["slot"][:], in0=each(a[:]), scalar=float(BLK), in1=rt["t1"][:],
                                          op0=ALU.mult, op1=ALU.add))
            for k in range(2):
                then(dve.tensor_tensor(rt["t2"][:], rt[f"one{k + 1}"][:], rt["slot"][:], ALU.mult))
                then(dve.tensor_reduce(POSF[:, k], rt["t2"][:], AX.X, ALU.add))
            then(dve.tensor_copy(SLOT[:], POSF[:]))
            then(dve.tensor_reduce(re["sumw"][:], TOT[:, :, E:2 * E].rearrange("p t e -> p e t"), AX.X, ALU.add))
            then(dve.tensor_scalar(re["one"][:], re["cnt"][:], 1.0, None, ALU.max))
            then(dve.reciprocal(re["inv"][:], re["one"][:]))
            then(dve.tensor_tensor(re["mean"][:], re["sumw"][:], re["inv"][:], ALU.mult))
            for k in range(2):
                then(dve.tensor_tensor(rt["t2"][:], rt[f"one{k + 1}"][:], each(re["mean"][:]), ALU.mult))
                then(dve.tensor_reduce(CO[:, k], rt["t2"][:], AX.X, ALU.add))
            assert count[0] == NROUTE

            def low_weights(m, par, w):
                dve.wait_ge(s_wh, START + m * 3 + w + 1)
                if w == 2:
                    dve.wait_ge(s_down, START + m - 1)
                dve.tensor_tensor(WL[par][:, w, :], RAWW[:, w, :], WH[par][:, w, :].bitcast(F32), ALU.subtract).then_inc(s_wlo, 1)

            def low_rows(m, par):
                dve.wait_ge(s_bh, START + m + 1)
                dve.tensor_tensor(XL[par][:].rearrange("p c n -> p (c n)"), PS[:, 7, :],
                                  XH[par][:].rearrange("p c n -> p (c n)").bitcast(F32), ALU.subtract).then_inc(s_bl, 1)

            def expert_block(m, par, last=False):
                for q in range(FP):
                    at = m * FP + q
                    dve.wait_ge(s_silu, START + at + 1)
                    dve.wait_ge(s_hh, START + at - 1)
                    dve.tensor_tensor(HF[:, q % 2], SG[:, q % 2], PS[:, 2 * (q % 2):2 * (q % 2) + 2, BLK:2 * BLK],
                                      ALU.mult).then_inc(s_hm, 1)
                    if not last and q != 2:
                        low_weights(m + 1, 1 - par, {0: 0, 1: 1, 3: 2}[q])
                    dve.wait_ge(s_hh, START + at + 1)
                    if q == 0:
                        dve.wait_ge(s_down, START + m - 1)
                    dve.tensor_tensor(HL[par][:, 2 * q:2 * q + 2, :], HF[:, q % 2],
                                      HH[par][:, 2 * q:2 * q + 2, :].bitcast(F32), ALU.subtract).then_inc(s_hl, 1)
                    if q == 2 and not last:
                        low_rows(m + 1, 1 - par)

            for w in range(3):
                low_weights(0, 0, w)
            low_rows(0, 0)
            expert_block(0, 0)
            with dve.Fori(0, NBLK // 2 - 1) as j:
                expert_block(j * 2 + 1, 1)
                expert_block(j * 2 + 2, 0)
            expert_block(NBLK - 1, 1, last=True)

            for i in range(NI):
                dve.wait_ge(s_gat[i % 2], 2 * U * 16 * (i // 2 + 1))
                for k in range(2):
                    for u in range(U):
                        t = i * U + u
                        last = dve.scalar_tensor_tensor(out=X[:, t, :], in0=YB[:, i % 2, k, u, :], scalar=CO[:, k, t:t + 1],
                                                        in1=X[:, t, :], op0=ALU.mult, op1=ALU.add)
                    last.then_inc(s_mix, 1)
                    dve.wait_ge(s_mix, 2 * i + k + 1)
                statistics(i)
            means(3)
            for i in range(NI):
                for u in range(U):
                    last = rows(X[:, i * U + u, :], i, u)
                last.then_inc(s_fin, 1)

        @block.tensor
        def _(pe):
            pe.sem_inc(s_xt, START)
            pe.sem_inc(s_proj, START)
            pe.sem_inc(s_qkt, START)
            pe.sem_inc(s_score, START)
            pe.sem_inc(s_pv, START)
            pe.sem_inc(s_oproj, START)
            for s in (s_cq, s_cs, s_cpt, s_cpv, s_cwo, s_rl, s_bt, s_gu, s_down):
                pe.sem_inc(s, START)

            pe.wait_ge(s_loadw, NLOAD)
            for c in range(DC):
                last = pe.matmul(PS[:, 6 + c, 0:P], kvd_sb[:, c * P:(c + 1) * P], kvup_sb[:], start=True, stop=True)
            last.then_inc(s_fuse, 1)
            pe.wait_ge(s_cload, NCLOAD)
            for o in range(DC):
                for c in range(DC):
                    pe.matmul(PS[:, 4 + o, 0:NB * CL], WX[:, 1, c, o * P:(o + 1) * P], ctx_sb[:, c, :],
                              start=(c == 0), stop=(c == DC - 1))
            for b in range(NB):
                for c in range(DC):
                    last = pe.matmul(PS[0:CL, 2 + b, 0:D], ctx_sb[:, c, b * CL:(b + 1) * CL], WX[:, 2, c, :],
                                     start=(c == 0), stop=(c == DC - 1))
            last.then_inc(s_ckv, 1)
            pe.wait_ge(s_ckb, 1)

            def transposes(k, i):
                pe.wait_ge(s_xn, START + k * NI + i + 1)
                transpose_group(k * NI + i, XN)

            def transpose_group(n, rows):
                pe.wait_ge(s_xte, START + n * XB)
                for v in range(XB):
                    for u in (2 * v, 2 * v + 1):
                        for c in range(DC):
                            last = pe.transpose(ps_x[:, u, c * P:(c + 1) * P], rows[:, u, c * P:(c + 1) * P], identF)
                    last.then_inc(s_xt, 1)

            def products(k, i, w, cols, s_done, done, s_free, free):
                for u in range(U):
                    if u % 2 == 0:
                        pe.wait_ge(s_xte, START + (k * NI + i) * XB + u // 2 + 1)
                    if u == 0:
                        pe.wait_ge(s_free, START + free)
                    for c in range(DC):
                        last = pe.matmul(ps_p[:, u, 0:cols], XT[:, u, c, :], w[:, c, 0:cols],
                                         start=(c == 0), stop=(c == DC - 1))
                    last.then_inc(s_done, 1)

            def stack_transposes(l, i):
                n = l * NI + i
                pe.wait_ge(s_stack, START + n + 1)
                for u in range(U):
                    pe.wait_ge(s_qe, START + n * U + u)
                    pe.wait_ge(s_ke, START + n * U + u)
                    for h in range(H // 2):
                        pe.transpose(ps_q[:, h, :], QS2[:, u * H // 2 + h, :], identH[:])
                    for g in range(G):
                        last = pe.transpose(ps_k[:, g, :], KS2[:, u * G + g, :], identH[:])
                    last.then_inc(s_qkt, 1)

            def scores(l, b, g, n):
                it = b * G + g
                at = BASE[l] + it * len(STEPS[l]) + n
                pe.wait_ge(s_exp, START + at - 1)
                col = 0
                for q, k, w in STEPS[l][n]:
                    into = ps_s[:, n % 2, col:col + HG * w]
                    table = None if k < q and l == 0 else 0 if l == 0 else 1 if k == q else 2
                    if table is not None:
                        pe.matmul(into, identB[:], hide[:, table, :, 0:w], start=True, stop=False, skip_group_check=True)
                    for e in range(2):
                        last = pe.matmul(into[:, e * 2 * w:(e + 1) * 2 * w], KTf[:, ds((g * 2 + e) * T + b * S + k * P, P)],
                                         QT[:, ds(g * 2, 2), ds(b * S + q * P, w)],
                                         start=(table is None and e == 0), stop=(e == 1), skip_group_check=True)
                    col += HG * w
                last.then_inc(s_score, 1)

            def values(l, b, g, n):
                it = b * G + g
                at = BASE[l] + it * len(STEPS[l]) + n
                share = ON_POOL[l]
                per = [sum(share), len(share) - sum(share)]
                before = [sum(share[:n + 1]), n + 1 - sum(share[:n + 1])]
                pe.wait_ge(s_exp, START + at + 1)
                base = [BG * sum(ON_POOL[0]) * l, BG * (len(ON_POOL[0]) - sum(ON_POOL[0])) * l]
                if share[n]:
                    pe.wait_ge(s_lowp, START + base[0] + it * per[0] + before[0])
                else:
                    pe.wait_ge(s_low, START + base[1] + it * per[1] + before[1])
                col = 0
                for q, k, w in STEPS[l][n]:
                    first = k == 0 if l == 0 else k == q
                    if first:
                        pe.wait_ge(s_on, START + l * BG * TB + it * TB + q - 1)
                    vs = VSf[:, ds(((b * TB + k) * G + g) * VW, VW)]
                    for h in range(HG):
                        at_h = head_column(h, w) + col
                        pf = high_part(PF[:, n % 2, at_h:at_h + w])
                        pl = PL[:, n % 2, at_h:at_h + w]
                        for part, p in enumerate((pf, pl)):
                            last = pe.matmul(ps_o[0:w, q % 2, h, :], p, vs, start=(first and h == 0 and part == 0),
                                             stop=True, skip_group_check=True)
                    col += HG * w
                last.then_inc(s_pv, 1)

            def head_column(h, w):
                return ((h % 2) * 2 + h // 2) * w

            pe.wait_ge(s_const, 2)
            pe.wait_ge(s_weights, 1)
            for l in range(2):
                def project(i):
                    transposes(2 * l, i)
                    products(2 * l, i, W[l], QKV, s_proj, None, s_raw, (l * NI + i) * U)
                project(0)
                with pe.Fori(1, NI) as i:
                    project(i)
                    stack_transposes(l, i - 1)
                stack_transposes(l, NI - 1)
                pe.wait_ge(s_qe, START + (l + 1) * NT)
                pe.wait_ge(s_ke, START + (l + 1) * NT)
                pe.wait_ge(s_vs, (l + 1) * NVS)
                with pe.Fori(0, NB) as b:
                    with pe.Fori(0, G) as g:
                        for n in range(len(STEPS[l])):
                            scores(l, b, g, n)
                            if n:
                                values(l, b, g, n - 1)
                        values(l, b, g, len(STEPS[l]) - 1)
                with pe.Fori(0, NI) as i:
                    transposes(2 * l + 1, i)
                    products(2 * l + 1, i, WO[l], D, s_oproj, None, s_res, l * NI + i)

            def cross_scores(b, at, m):
                u, o, a = m // DC, m % DC, m % 2
                if m < DC:
                    pe.wait_ge(s_cqe, START + (b * (NI // NB) + at) * DC + o + 1)
                n = (b * (NI // NB) + at) * CS + m
                pe.wait_ge(s_clog, START + n - 1)
                for j in range(2):
                    w = CH // 2 * CL
                    last = pe.matmul(PS[:, 4 + 2 * a + j, 0:w], QC[:, o, u * P:(u + 1) * P],
                                     KZf[:, ds(((b * DC + o) * 2 + j) * w, w)], start=True, stop=True)
                last.then_inc(s_cs, 1)

            def cross_values(b, at, m):
                o, a = m % DC, m % 2
                n = (b * (NI // NB) + at) * CS + m
                pe.wait_ge(s_cexp, START + n + 1)
                for h in range(CH):
                    last = pe.transpose(PS[0:CL, h // 4, (h % 4) * P:(h % 4 + 1) * P], CPX[:, a, h, :], identF)
                last.then_inc(s_cpt, 1)
                pe.wait_ge(s_cpe, START + n + 1)
                pe.wait_ge(s_con, START + n - 1)
                for h in range(CH):
                    last = pe.matmul(PS[:, 2 + o, h * (HD + 1):(h + 1) * (HD + 1)], CPT[:, h, :],
                                     VXf[:, ds(((b * H) + o * CH + h) * (HD + 1), HD + 1)], start=True, stop=True)
                last.then_inc(s_cpv, 1)

            pe.wait_ge(s_ckz, 1)
            with pe.Fori(0, NB) as b:
                with pe.Fori(0, NI // NB) as gi:
                    i = b * (NI // NB) + gi
                    pe.wait_ge(s_xn, START + 4 * NI + i + 1)
                    transpose_group(4 * NI + i * 2, XN)
                    pe.wait_ge(s_xte, START + (4 * NI + i * 2 + 1) * XB)
                    pe.wait_ge(s_cres, START + i)
                    for o in range(DC):
                        for c in range(DC):
                            last = pe.matmul(PS[:, 2 + o, :], WX[:, 0, c, o * P:(o + 1) * P], XM[:, c, :],
                                             start=(c == 0), stop=(c == DC - 1))
                        last.then_inc(s_cq, 1)
                    for m in range(CS):
                        cross_scores(b, gi, m)
                        if m:
                            cross_values(b, gi, m - 1)
                    cross_values(b, gi, CS - 1)
                    pe.wait_ge(s_con, START + i * CS + CS)
                    transpose_group(4 * NI + i * 2 + 1, OX)
                    for u in range(U):
                        if u % 2 == 0:
                            pe.wait_ge(s_xte, START + (4 * NI + i * 2 + 1) * XB + u // 2 + 1)
                        for c in range(DC):
                            last = pe.matmul(PS[:, 2 + u // 2, (u % 2) * D:(u % 2 + 1) * D], XT[:, u, c, :], WX[:, 3, c, :],
                                             start=(c == 0), stop=(c == DC - 1))
                        if u % 2:
                            last.then_inc(s_cwo, 1)

            with pe.Fori(0, NI) as i:
                pe.wait_ge(s_xn, START + 5 * NI + i + 1)
                transpose_group(6 * NI + i, XN)
                pe.wait_ge(s_xte, START + (6 * NI + i + 1) * XB)
                pe.wait_ge(s_rle, START + i)
                for u in range(U):
                    for c in range(DC):
                        last = pe.matmul(PS[:, 2, u * E:(u + 1) * E], XT[:, u, c, :], RW[:, c, :],
                                         start=(c == 0), stop=(c == DC - 1))
                last.then_inc(s_rl, 1)
            pe.wait_ge(s_route, NSHARES)
            pe.matmul(PS[:, 3, 0:NT * 2 * E], ONES[:], SW[:].rearrange("p t e -> p (t e)"), start=True, stop=True)
            pe.matmul(PS[:, 4, 0:NT * E], before, SW[:, :, 0:E], start=True, stop=True).then_inc(s_tot, 1)

            def three(into, hs, ls, hm, lm, start, stop):
                pe.matmul(into, hs, hm, start=start, stop=False, skip_group_check=True)
                pe.matmul(into, hs, lm, start=False, stop=False, skip_group_check=True)
                return pe.matmul(into, ls, hm, start=False, stop=stop, skip_group_check=True)

            def block_rows_in(m, par, half):
                pe.wait_ge(s_xbl[par], 16 * half + 16)
                pe.wait_ge(s_bl, START + m)
                for c in range(DC):
                    for a in range(BA):
                        last = pe.transpose(PS[:, 7, (c * BA + a) * P:(c * BA + a + 1) * P],
                                            XR[:, par, a, c * P:(c + 1) * P], identF)
                last.then_inc(s_bt, 1)

            def down(m, par):
                pe.wait_ge(s_hl, START + m * FP + FP)
                pe.wait_ge(s_wlo, START + m * 3 + 3)
                pe.wait_ge(s_eo, START + m - 1)
                for a in range(BA):
                    for f in range(FC):
                        last = three(PS[:, 4 + par, a * D:(a + 1) * D],
                                     HH[par][:, f, a * P:(a + 1) * P], HL[par][:, f, a * P:(a + 1) * P],
                                     WH[par][:, 2, f * D:(f + 1) * D], WL[par][:, 2, f * D:(f + 1) * D],
                                     start=(a == 0 and f == 0), stop=(f == FC - 1))
                last.then_inc(s_down, 1)

            def expert_block(m, par, half, first=False, last=False):
                pe.wait_ge(s_bl, START + m + 1)
                pe.wait_ge(s_wlo, START + m * 3 + 2)
                for q in range(FP):
                    pe.wait_ge(s_hm, START + m * FP + q - 1)
                    for f in (2 * q, 2 * q + 1):
                        for w in range(2):
                            for c in range(DC):
                                at = c * FI + f * P
                                done = three(PS[:, 2 * (q % 2) + f % 2, w * BLK:(w + 1) * BLK],
                                             WH[par][:, w, at:at + P], WL[par][:, w, at:at + P],
                                             XH[par][:, c, :], XL[par][:, c, :],
                                             start=(w == 0 and c == 0), stop=(c == DC - 1))
                    done.then_inc(s_gu, 1)
                    if q == 1 and not first:
                        down(m - 1, 1 - par)
                    if q == 2 and not last:
                        block_rows_in(m + 1, 1 - par, half if par == 0 else half + 1)

            block_rows_in(0, 0, 0)
            expert_block(0, 0, 0, first=True)
            with pe.Fori(0, NBLK // 2 - 1) as j:
                expert_block(j * 2 + 1, 1, j)
                expert_block(j * 2 + 2, 0, j + 1)
            expert_block(NBLK - 1, 1, NBLK // 2 - 1, last=True)
            down(NBLK - 1, 1)


def high_part(a):
    return a.bitcast(BF16).rearrange("p (n two) -> p n two", two=2)[:, :, 1]


def constants():
    f = np.float32
    rope = np.zeros((P, 2, 2, NT, HD), f)
    for l, base in enumerate((1000000.0, 10000.0)):
        inv = f(1.0) / np.power(f(base), np.arange(0, HD, 2, dtype=f) / f(HD)).astype(f)
        ang = (np.arange(S, dtype=f)[:, None] * inv[None, :]).astype(f)
        c, s = np.cos(ang).astype(f), np.sin(ang).astype(f)
        both = np.stack([np.repeat(c, 2, 1), np.stack([-s, s], -1).reshape(S, HD)])
        both = np.tile(both.reshape(2, TB, P, HD), (1, NB, 1, 1))
        rope[:, l] = both.transpose(2, 0, 1, 3)
    small = np.zeros((P, 16 + E * NJ + NBLK + P), f)
    small[:, 0:CH] = SCALE * (np.arange(P)[:, None] // HD == np.arange(CH)[None, :])
    small[:, 8:16] = np.arange(E)
    small[:, 16:16 + E * NJ] = np.tile(np.arange(NJ) * BLK, E)
    small[:, 16 + E * NJ:16 + E * NJ + NBLK] = np.arange(NBLK)
    small[:, 16 + E * NJ + NBLK:] = np.arange(P)[:, None] < np.arange(P)[None, :]
    tri = np.zeros((P, 4, P), f)
    k, q = np.arange(P)[:, None], np.arange(P)[None, :]
    tri[:, 0] = np.where(q >= k, 0.0, HIDE)
    tri[:, 1] = np.where((q >= k) & (q - k < WIN), 0.0, HIDE)
    tri[:, 2] = np.where(P + q - k < WIN, 0.0, HIDE)
    tri[:, 3] = np.eye(P)
    return rope, tri, small


_OUT = (NB, S, D)


def kernel(**inputs):
    import numpy as _np
    import concourse.bacc as _bacc
    from concourse import mybir as _mybir
    from concourse.bass_utils import run_bass_kernel_spmd as _run

    a = {k.replace("L0_", ""): _np.asarray(v) for k, v in inputs.items()}
    rope, tri, small = constants()
    column = lambda v: v.reshape(DC, P).T
    chunked = lambda w: w.reshape(E, -1, P, w.shape[-1]).transpose(0, 2, 1, 3).reshape(E, P, THIRD)
    gate, up = (chunked(a[f"ffn_{n}_w"].transpose(0, 2, 1)) for n in ("gate", "up"))
    lower = chunked(a["ffn_down_w"].transpose(0, 2, 1))
    arrays = {
        "x": a["x"].reshape(T, D),
        "wq0": a["attn_g_wq"], "kvdT": a["attn_g_kv_down"].T,
        "kvup": _np.concatenate([a["attn_g_k_up"], a["attn_g_v_up"]], 1), "wo0": a["attn_g_wo"],
        "wq1": a["attn_l_wq"], "wk1": a["attn_l_wk"], "wv1": a["attn_l_wv"], "wo1": a["attn_l_wo"],
        "n1": column(a["attn_norm1_w"]), "n2": column(a["attn_norm2_w"]), "rope": rope, "tri": tri,
        "ctxT": a["ctx_1024"].reshape(NB * CL, D).T, "mask": a["mask_1x1xSxS2_ff0"].reshape(S, CL),
        "xwq": a["xattn_Wq"], "xwk": a["xattn_Wk"], "xwv": a["xattn_Wv"], "xwo": a["xattn_Wo"],
        "xbq": column(a["xattn_bq"]), "xbk": column(a["xattn_bk"]),
        "xbv": a["xattn_bv"].reshape(1, D), "xbo": a["xattn_bo"].reshape(1, D),
        "router": a["ffn_router_w"].T, "experts": _np.concatenate([gate, up, lower], 2), "small": small,
    }
    arrays = {f"in_{n}": _np.ascontiguousarray(v) for n, v in arrays.items()}
    nc = _bacc.Bacc("TRN2", target_bir_lowering=False, num_devices=1)
    args = [nc.dram_tensor(n, v.shape, _mybir.dt.from_np(v.dtype), kind="ExternalInput").ap() for n, v in arrays.items()]
    args.append(nc.dram_tensor("out_0", (T, D), F32, kind="ExternalOutput").ap())
    build_decoder(nc, *args)
    r = _run(nc, [arrays], core_ids=[0])
    return r.results[0]["out_0"].reshape(_OUT)
```

```python
from contextlib import ExitStack

import numpy as np
import concourse.bass as bass
from concourse import mybir

P = 128
NB, S, D = 2, 1024, 256
T = NB * S
NT = T // P
TB = S // P
DC = D // P
H, G, HD = 16, 4, 16
HG = H // G
LAT = 64
WIN = 64
U = 4
NI = NT // U
XB = U // 2
QKV = (H + 2 * G) * HD
QKH = H + G
VW = 3 * HD + 1
BG = NB * G
EPS_RMS, EPS_LN = 1e-6, 1e-5
SCALE = float(HD) ** -0.5
HIDE = -30000.0

F32, F32R = mybir.dt.float32, mybir.dt.float32r
BF16, F16 = mybir.dt.bfloat16, mybir.dt.float16
ALU = mybir.AluOpType
ACT = mybir.ActivationFunctionType
AX = mybir.AxisListType
ds = bass.ds

GLOBAL_UNITS = [(q, k) for q in range(TB) for k in range(q + 1)]
GLOBAL_STEPS = [[(q, k, P) for q, k in GLOBAL_UNITS[n:n + 2]] for n in range(0, len(GLOBAL_UNITS), 2)]
LOCAL_STEPS = [[(q, q, P)] + [(q, q - 1, WIN)] * (q > 0) for q in range(TB)]
STEPS = [GLOBAL_STEPS, LOCAL_STEPS]
DONE = [[max(n for n, step in enumerate(steps) if step[-1][0] >= q and step[0][0] <= q) for q in range(TB)]
        for steps in STEPS]
BASE = [0, BG * len(GLOBAL_STEPS)]
SLOTS = 3
REUSE = [[next(d for d in range(1, 9) if (n - d) % len(steps) % SLOTS == n % SLOTS) for n in range(len(steps))]
         for steps in STEPS]
CL = 77
CH = H // 2
CS = 2 * U
CLS = 4
LATE = 3
FMAX = float(np.finfo(np.float32).max)
E, FI = 8, 1024
FC = FI // P
FP = FC // 2
BLK = 256
BA = BLK // P
NBLK = (2 * T + E * (BLK - 1)) // BLK
NJ = T // BLK
THIRD = DC * FI
START = CS + 1


def build_decoder(nc, x, wq0, kvdT, kvup, wo0, wq1, wk1, wv1, wo1, n1, n2, rope, tri,
                  ctxT, mask, xwq, xwk, xwv, xwo, xbq, xbk, xbv, xbo, router, experts, small, out):
    ctx = ExitStack()
    with ctx:
        def sb(name, shape, dt=F32):
            return ctx.enter_context(nc.sbuf_tensor(name, shape, dt))

        def sem(name):
            return ctx.enter_context(nc.semaphore(name))

        X = sb("X", [P, NT, D])
        tri_sb = sb("tri_sb", [P, 4, P])
        identF = tri_sb[:, 3, :]
        eps = sb("eps", [P, 2])
        root = sb("root", [P, NT])
        rstd = sb("rstd", [P, NT])

        small_sb = sb("small_sb", [P, 16 + E * NJ + NBLK + P])
        ST = sb("ST", [P, NT, 6])
        MV = sb("MV", [P, NT, 2])
        EB = sb("EB", [P, NBLK], mybir.dt.int32)
        SLOT = sb("SLOT", [P, 2, NT], mybir.dt.uint32)
        CO = sb("CO", [P, 2, NT])
        ONES = sb("ONES", [P, P])
        middle = ExitStack()

        def mb(name, shape, dt=F32):
            return middle.enter_context(nc.sbuf_tensor(name, shape, dt))

        ssq = mb("ssq", [P, NT])
        XN = mb("XN", [P, U, D])
        XT = mb("XT", [P, U, DC, P])
        WX = mb("WX", [P, 4, DC, D])
        ctx_sb = mb("ctx_sb", [P, DC, NB * CL])
        xb = mb("xb", [P, 2, DC])
        BV = mb("BV", [CL, D])
        BO = mb("BO", [P, D])
        KZ = mb("KZ", [P, NB, DC, CH, CL])
        VX = mb("VX", [CL, NB, H, HD + 1])
        MF = mb("MF", [P, NT, CL])
        RW = mb("RW", [P, DC, E])
        LG = mb("LG", [P, NT, E])
        early = ExitStack()

        def eb(name, shape, dt=F32):
            return early.enter_context(nc.sbuf_tensor(name, shape, dt))

        OA = eb("OA", [P, NT, D])
        W = [eb(f"W{l}", [P, DC, QKV]) for l in range(2)]
        WO = [eb(f"WO{l}", [P, DC, D]) for l in range(2)]
        kvd_sb = eb("kvd_sb", [LAT, D])
        kvup_sb = eb("kvup_sb", [LAT, 2 * G * HD])
        nw = eb("nw", [P, 2, DC])
        rope_sb = eb("rope_sb", [P, 2, 2, NT, HD])
        identH = eb("identH", [P, P], F16)
        identB = eb("identB", [P, P], BF16)
        hide = eb("hide", [P, 3, HG, P], BF16)
        KB = eb("KB", [P, DC, NB * CL])
        RSF = eb("RSF", [P, SLOTS * 1024])
        RS = RSF[:, 0:2 * U * QKH * HD].rearrange("p (a u n) -> p a u n", a=2, u=U)
        RAW, SQ = RS[:, 0], RS[:, 1]
        R1 = eb("R1", [P, U, QKH * HD])
        R2 = eb("R2", [P, U, QKH * HD])
        ss = eb("ss", [P, U * QKH])
        sr = eb("sr", [P, U * QKH])
        rn = eb("rn", [P, U * QKH])
        RQ = eb("RQ", [P, U * H, HD])
        RK = eb("RK", [P, U * G, HD])
        QS = eb("QS", [P, U * H, 4, HD], F16)
        KS = eb("KS", [P, U * G, 8, HD], F16)
        QT = eb("QT", [P, H // 2, T], F16)
        KT = eb("KT", [P, 2 * G, T], F16)
        VA = eb("VA", [P, U * G, HD])
        VL = eb("VL", [P, U * G, HD])
        VS = eb("VS", [P, NT * G, VW], BF16)
        PF = RSF[:].rearrange("p (s n) -> p s n", s=SLOTS)
        PL = QS[:].rearrange("p n c d -> p (n c d)")[:, 0:SLOTS * 1024].rearrange("p (s n) -> p s n", s=SLOTS)
        OS = eb("OS", [P, 2, HG, HD])
        OR = eb("OR", [P, 2, HG, 1])
        early.close()
        cross = ExitStack()

        def cb(name, shape, dt=F32):
            return cross.enter_context(nc.sbuf_tensor(name, shape, dt))

        XS = cb("XS", [P, 2, U, D])
        XM = cb("XM", [P, 2, DC, U * P])
        QC = cb("QC", [P, DC, T])
        QG = cb("QG", [P, DC, U * P])
        CLG = cb("CLG", [P, CLS, CH, CL])
        CMX = cb("CMX", [P, 2, CH, 1])
        CPX = cb("CPX", [P, 2, CH, CL])
        CPT = cb("CPT", [CL, CH, P])
        CR = cb("CR", [P, 2, CH, 1])
        OX = cb("OX", [P, NT, D])
        rt = {n: cb(f"rt_{n}", [P, NT, E]) for n in
              ("eq1", "code1", "one1", "left", "eq2", "code2", "one2", "w1", "w2", "pfa", "pfb", "slot", "t1", "t2")}
        rc = {n: cb(f"rc_{n}", [P, NT]) for n in ("m1", "i1", "m2", "i2", "d", "e", "den", "r", "p2")}
        re = {n: cb(f"re_{n}", [P, E]) for n in ("cnt", "sumw", "nb", "bba", "bbb", "end", "one", "inv", "mean")}
        SW = cb("SW", [P, NT, 2 * E])
        TOT = cb("TOT", [P, NT, 2 * E])
        GTJ = cb("GTJ", [P, E, NJ])
        LEB = cb("LEB", [P, NBLK, E])
        EBF = cb("EBF", [P, NBLK])
        POSF = cb("POSF", [P, 2, NT])
        cross.close()
        middle.close()
        RAWW = sb("RAWW", [P, 3, THIRD])
        WH = [sb(f"WH{a}", [P, 3, THIRD], F32R) for a in range(2)]
        WL = [sb(f"WL{a}", [P, 3, THIRD], F32R) for a in range(2)]
        XR = sb("XR", [P, 2, BA, D])
        XH = [sb(f"XH{a}", [P, DC, BLK], F32R) for a in range(2)]
        XL = [sb(f"XL{a}", [P, DC, BLK], F32R) for a in range(2)]
        SG = sb("SG", [P, 2, 2, BLK])
        HF = sb("HF", [P, 2, 2, BLK])
        HH = [sb(f"HH{a}", [P, FC, BLK], F32R) for a in range(2)]
        HL = [sb(f"HL{a}", [P, FC, BLK], F32R) for a in range(2)]
        EO = sb("EO", [P, 2, BA, D])
        YB = RAWW[:].rearrange("p w n -> p (w n)")[:, 0:2 * 2 * U * D].rearrange("p (s k u d) -> p s k u d", s=2, k=2, u=U)
        XG = nc.dram_tensor("XG", [NBLK * BLK, D], F32).ap()
        YG = nc.dram_tensor("YG", [NBLK * BLK, D], F32).ap()

        PS = ctx.enter_context(nc.psum_tensor("PS", [P, 8, 512], F32))
        ps_x = PS[:, 0:2, :].rearrange("p a (u n) -> p (a u) n", u=2)
        ps_p = PS[:, 2:6, :]
        ps_q = [PS[:, a, :].bitcast(F16).rearrange("p (h n) -> p h n", h=H // 2) for a in (0, 6)]
        ps_k = [PS[:, a, 0:256].bitcast(F16).rearrange("p (g n) -> p g n", g=G) for a in (1, 7)]
        ps_s = PS[:, 0:2 * SLOTS, :].rearrange("p (a b) n -> p a (b n)", a=SLOTS)
        ps_o = PS[:, 6:8, 0:HG * VW].rearrange("p a (h v) -> p a h v", h=HG)

        s_loadx = sem("s_loadx")
        s_loadw = sem("s_loadw")
        s_fuse = sem("s_fuse")
        s_weights = sem("s_weights")
        s_const = sem("s_const")
        s_square = sem("s_square")
        s_ssq = sem("s_ssq")
        s_root = sem("s_root")
        s_rstd = sem("s_rstd")
        s_xn = sem("s_xn")
        s_xt = sem("s_xt")
        s_xte = sem("s_xte")
        s_proj = sem("s_proj")
        s_raw = sem("s_raw")
        s_rot2 = sem("s_rot2")
        s_dve = sem("s_dve")
        s_hss = sem("s_hss")
        s_hroot = sem("s_hroot")
        s_split = sem("s_split")
        s_rest = sem("s_rest")
        s_stack = sem("s_stack")
        s_dup = sem("s_dup")
        s_vs = sem("s_vs")
        s_qkt = sem("s_qkt")
        s_qe = sem("s_qe")
        s_ke = sem("s_ke")
        s_score = sem("s_score")
        s_exp = sem("s_exp")
        s_low = sem("s_low")
        s_lowp = sem("s_lowp")
        s_pv = sem("s_pv")
        s_osum = sem("s_osum")
        s_on = sem("s_on")
        s_oproj = sem("s_oproj")
        s_res = sem("s_res")
        s_x0 = sem("s_x0")
        s_cload = sem("s_cload")
        s_ckv = sem("s_ckv")
        s_ckb = sem("s_ckb")
        s_ckz = sem("s_ckz")
        s_bn = sem("s_bn")
        s_stat = sem("s_stat")
        s_mv = sem("s_mv")
        s_xb = sem("s_xb")
        s_cq = sem("s_cq")
        s_cqe = sem("s_cqe")
        s_qg = sem("s_qg")
        s_ostage = sem("s_ostage")
        s_cs = sem("s_cs")
        s_clog = sem("s_clog")
        s_cmax = sem("s_cmax")
        s_csub = sem("s_csub")
        s_cexp = sem("s_cexp")
        s_cpt = sem("s_cpt")
        s_cpe = sem("s_cpe")
        s_cpv = sem("s_cpv")
        s_crec = sem("s_crec")
        s_con = sem("s_con")
        s_cwo = sem("s_cwo")
        s_cres = sem("s_cres")
        s_rl = sem("s_rl")
        s_rle = sem("s_rle")
        s_route = sem("s_route")
        s_gap = sem("s_gap")
        s_tot = sem("s_tot")
        s_zero = sem("s_zero")
        s_clear = sem("s_clear")
        s_scat = sem("s_scat")
        s_wl = [sem(f"s_wl{w}") for w in range(3)]
        s_wh = sem("s_wh")
        s_wlo = sem("s_wlo")
        s_xbl = [sem(f"s_xbl{a}") for a in range(2)]
        s_bt = sem("s_bt")
        s_bh = sem("s_bh")
        s_bl = sem("s_bl")
        s_gu = sem("s_gu")
        s_silu = sem("s_silu")
        s_hm = sem("s_hm")
        s_hh = sem("s_hh")
        s_hl = sem("s_hl")
        s_down = sem("s_down")
        s_eo = sem("s_eo")
        s_yg = sem("s_yg")
        s_eof = sem("s_eof")
        s_gat = [sem(f"s_gat{a}") for a in range(2)]
        s_mix = sem("s_mix")
        s_fin = sem("s_fin")
        s_out = sem("s_out")

        xv = x.rearrange("(t p) d -> p t d", p=P)
        ov = out.rearrange("(t p) d -> p t d", p=P)
        NLOAD = 12 * 16
        NCLOAD = 13 * 16
        NSHARES = 19
        NROUTE = 51
        KZf = KZ[:].rearrange("p b c h k -> p (b c h k)")
        VXf = VX[:].rearrange("k b h d -> k (b h d)")
        own = small_sb[:, 0:CH]
        expert_no = small_sb[:, 8:16]
        block_rows = small_sb[:, 16:16 + E * NJ]
        block_no = small_sb[:, 16 + E * NJ:16 + E * NJ + NBLK]
        before = small_sb[:, 16 + E * NJ + NBLK:]
        NDVE = 5
        NVS = 4
        KTf = KT[:].rearrange("p a t -> p (a t)")
        VSf = VS[:].rearrange("p n v -> p (n v)")
        KS2 = KS[:].rearrange("p n a d -> p n (a d)")
        QS2 = QS[:].rearrange("p (n e) a d -> p n (e a d)", e=2)
        block = ctx.enter_context(nc.Block())

        @block.sync
        def _(sp):
            for i in range(NI):
                sp.dma_start(X[:, U * i:U * i + U, :], xv[:, U * i:U * i + U, :]).then_inc(s_loadx, 16)
            for l, wq in enumerate((wq0, wq1)):
                sp.dma_start(W[l][:, :, 0:D], wq.rearrange("(c p) n -> p c n", p=P)).then_inc(s_loadw, 16)
            sp.dma_start(W[1][:, :, D:D + 64], wk1.rearrange("(c p) n -> p c n", p=P)).then_inc(s_loadw, 16)
            sp.dma_start(W[1][:, :, D + 64:D + 128], wv1.rearrange("(c p) n -> p c n", p=P)).then_inc(s_loadw, 16)
            sp.dma_start(kvd_sb[:], kvdT).then_inc(s_loadw, 16)
            sp.dma_start(kvup_sb[:], kvup).then_inc(s_loadw, 16)
            sp.dma_start(nw[:, 0, :], n1).then_inc(s_loadw, 16)
            sp.dma_start(nw[:, 1, :], n2).then_inc(s_loadw, 16)
            sp.dma_start(rope_sb[:], rope).then_inc(s_loadw, 16)
            sp.dma_start(tri_sb[:], tri).then_inc(s_loadw, 16)
            for l, wo in enumerate((wo0, wo1)):
                sp.dma_start(WO[l][:], wo.rearrange("(c p) n -> p c n", p=P)).then_inc(s_loadw, 16)
            for n, w in enumerate((xwq, xwk, xwv, xwo)):
                sp.dma_start(WX[:, n], w.rearrange("(c p) n -> p c n", p=P)).then_inc(s_cload, 16)
            sp.dma_start(ctx_sb[:], ctxT.rearrange("(c p) n -> p c n", p=P)).then_inc(s_cload, 16)
            sp.dma_start(xb[:, 0, :], xbq).then_inc(s_cload, 16)
            sp.dma_start(xb[:, 1, :], xbk).then_inc(s_cload, 16)
            sp.dma_start(BV[:], xbv.to_broadcast([CL, D])).then_inc(s_cload, 16)
            sp.dma_start(BO[:], xbo.to_broadcast([P, D])).then_inc(s_cload, 16)
            for b in range(NB):
                sp.dma_start(MF[:, b * TB:(b + 1) * TB, :], mask.rearrange("(t p) k -> p t k", p=P)).then_inc(s_cload, 16)
            sp.dma_start(small_sb[:], small).then_inc(s_cload, 16)
            sp.dma_start(RW[:], router.rearrange("(c p) e -> p c e", p=P)).then_inc(s_cload, 16)
            sp.wait_ge(s_zero, 1)
            for n in range(NBLK):
                sp.dma_start(XG[n * BLK:(n + 1) * BLK, :].rearrange("(p a) d -> p (a d)", p=P // 2),
                             KT[P // 2:P, 0, :].bitcast(F32)).then_inc(s_clear, 16)
            for i in range(NI):
                sp.wait_ge(s_xn, START + 3 * NI + i + 1)
                sp.dma_start(OA[:, U * i:U * i + U, :], xv[:, U * i:U * i + U, :]).then_inc(s_x0, 16)

            def load_block(m, par):
                e = sp.value_load(EB[0:1, ds(m, 1)], min_val=0, max_val=E - 1)
                for w in range(3):
                    sp.wait_ge(s_wlo, START + m * 3 + w - 2)
                    sp.dma_start(RAWW[:, w, :], experts[ds(e, 1), :, w * THIRD:(w + 1) * THIRD]
                                 .rearrange("a p n -> p (a n)")).then_inc(s_wl[w], 16)
                sp.wait_ge(s_bt, START + m - 1)
                sp.dma_start(XR[:, par], XG[ds(m * BLK, BLK), :].rearrange("(a p) d -> p a d", p=P)).then_inc(s_xbl[par], 16)

            sp.wait_ge(s_route, NROUTE)
            sp.wait_ge(s_scat, 32 * NT)
            with sp.Fori(0, NBLK // 2) as j:
                for par in range(2):
                    load_block(j * 2 + par, par)
            load_block(NBLK - 1, 0)
            for i in range(NI):
                sp.wait_ge(s_fin, i + 1)
                sp.dma_start(ov[:, U * i:U * i + U, :], X[:, U * i:U * i + U, :]).then_inc(s_out, 16)
            sp.wait_ge(s_out, 16 * NI)

        @block.gpsimd
        def _(pool):
            pool.sem_inc(s_rot2, START)
            pool.sem_inc(s_stack, START)
            pool.sem_inc(s_vs, START)
            pool.sem_inc(s_lowp, START)
            pool.memset(eps[:, 0:1], EPS_RMS)
            pool.memset(eps[:, 1:2], EPS_LN)
            pool.memset(VS[:, :, 3 * HD:VW], 1.0).then_inc(s_const, 1)
            pool.memset(ONES[:], 1.0)
            pool.wait_ge(s_loadw, NLOAD)
            pool.tensor_copy(identH[:], identF)
            pool.tensor_copy(identB[:], identF)
            pool.tensor_copy(hide[:], tri_sb[:, 0:3, :].unsqueeze(2).to_broadcast([P, 3, HG, P])).then_inc(s_const, 1)

            def rotate_and_stack(l, i):
                n = l * NI + i
                pool.wait_ge(s_raw, START + n * U + U)
                pool.wait_ge(s_dve, START + (n - 1) * NDVE + 2)
                rv = RAW.rearrange("p u (h d e) -> p u h d e", h=QKH, e=2)
                r2 = R2[:].rearrange("p u (h d e) -> p u h d e", h=QKH, e=2)
                sv = rope_sb[:, l, 1, ds(i * U, U), :].rearrange("p t (d e) -> p t d e", e=2)
                for e in range(2):
                    last = pool.tensor_tensor(
                        r2[:, :, :, :, e], rv[:, :, :, :, 1 - e],
                        sv[:, :, :, e].unsqueeze(2).to_broadcast([P, U, QKH, HD // 2]), ALU.mult)
                last.then_inc(s_rot2, 1)
                group = ds(i * (U * G), U * G)
                part = [VS[:, group, c * HD:(c + 1) * HD] for c in range(3)]
                pool.tensor_copy(part[0], VA[:]).then_inc(s_vs, 1)
                pool.wait_ge(s_vs, START + n * NVS + 1)
                pool.wait_ge(s_dve, START + n * NDVE + 5)
                pool.tensor_tensor(QS[:, :, 3, :], RQ[:], QS[:, :, 0, :], ALU.subtract).then_inc(s_stack, 1)
                pool.tensor_tensor(VL[:], VA[:], part[0], ALU.subtract).then_inc(s_vs, 1)
                pool.wait_ge(s_vs, START + n * NVS + 2)
                pool.tensor_copy(part[1], VL[:]).then_inc(s_vs, 1)
                pool.wait_ge(s_vs, START + n * NVS + 3)
                pool.tensor_tensor(part[2], VL[:], part[1], ALU.subtract).then_inc(s_vs, 1)

            def low_parts(l, it):
                for n, step in enumerate(STEPS[l]):
                    at = BASE[l] + it * len(STEPS[l]) + n
                    cut, cols = low_share(step)
                    pool.wait_ge(s_exp, START + at + 1)
                    pool.wait_ge(s_pv, START + at - REUSE[l][n] + 1)
                    pf = PF[:, n % SLOTS, cut:cols]
                    pool.tensor_tensor(PL[:, n % SLOTS, cut:cols], pf, high_part(pf), ALU.subtract).then_inc(s_lowp, 1)

            for l in range(2):
                with pool.Fori(0, NI) as i:
                    rotate_and_stack(l, i)
                with pool.Fori(0, BG) as it:
                    low_parts(l, it)
                pool.wait_ge(s_on, START + (l + 1) * BG * TB)
                with pool.Fori(0, NI) as i:
                    pool.wait_ge(s_xt, START + ((2 * l + 1) * NI + i) * XB)
                    pool.tensor_copy(XN[:], OA[:, ds(i * U, U), :]).then_inc(s_xn, 1)
            pool.sem_inc(s_xb, START)
            pool.sem_inc(s_qg, START)
            pool.sem_inc(s_ostage, START)
            with pool.Fori(0, NI // 2) as j:
                for a in range(2):
                    i = j * 2 + a
                    pool.wait_ge(s_xn, START + 4 * NI + i + 1)
                    pool.tensor_tensor(X[:, ds(i * U, U), :], XS[:, a], BO[:].unsqueeze(1).to_broadcast([P, U, D]),
                                       ALU.add).then_inc(s_xb, 1)
            pool.wait_ge(s_cqe, START + NI * DC)
            with pool.Fori(0, NI) as i:
                for u in range(U):
                    pool.wait_ge(s_cs, START + (i - 1) * CS + (u + 1) * DC)
                    pool.tensor_copy(QG[:, :, u * P:(u + 1) * P], QC[:, :, ds((i * U + u) * P, P)]).then_inc(s_qg, 1)
            with pool.Fori(0, NI // 2) as j:
                for a in range(2):
                    i = j * 2 + a
                    pool.wait_ge(s_con, START + (i + 1) * CS)
                    pool.wait_ge(s_xt, START + (5 * NI + i - 1) * XB)
                    pool.tensor_copy(XS[:, a], OX[:, ds(i * U, U), :]).then_inc(s_ostage, 1)
            pool.wait_ge(s_route, NROUTE)
            pool.wait_ge(s_clear, 16 * (NBLK))
            for k in range(2):
                for t in range(NT):
                    pool.indirect_dma_start(XG[:, :], bass.IndirectOffsetOnAxis(SLOT[:, k, t:t + 1], 0),
                                            X[:, t, :], None).then_inc(s_scat, 16)
            pool.sem_inc(s_eof, START)

            def store_block(m, par):
                pool.wait_ge(s_eo, START + m + 1)
                pool.dma_start(YG[ds(m * BLK, BLK), :].rearrange("(a p) d -> p a d", p=P), EO[:, par]).then_inc(s_yg, 16)
                pool.wait_ge(s_yg, 16 * m + 16)
                pool.sem_inc(s_eof, 1)

            with pool.Fori(0, NBLK // 2) as j:
                for par in range(2):
                    store_block(j * 2 + par, par)
            store_block(NBLK - 1, 0)
            pool.wait_ge(s_yg, 16 * NBLK)
            for i in range(NI):
                if i >= 2:
                    pool.wait_ge(s_stat, 2 * NI + i - 1)
                for k in range(2):
                    for u in range(U):
                        pool.indirect_dma_start(YB[:, i % 2, k, u, :], None, YG[:, :],
                                                bass.IndirectOffsetOnAxis(SLOT[:, k, i * U + u:i * U + u + 1], 0)
                                                ).then_inc(s_gat[i % 2], 16)

        @block.scalar
        def _(act):
            act.sem_inc(s_square, START)
            act.sem_inc(s_root, START)
            act.sem_inc(s_xte, START)
            act.sem_inc(s_raw, START)
            act.sem_inc(s_hroot, START)
            act.sem_inc(s_dup, START)
            act.sem_inc(s_qe, START)
            act.sem_inc(s_exp, START)
            for s in (s_cqe, s_cexp, s_cpe, s_rle, s_wh, s_bh, s_silu, s_hh, s_eo):
                act.sem_inc(s, START)

            def squares(n, i):
                act.wait_ge(s_ssq, START + n)
                act.activation(RAW.rearrange("p u n -> p (u n)")[:, 0:U * D],
                               X[:, ds(i * U, U), :].rearrange("p u n -> p (u n)"), ACT.Square).then_inc(s_square, 1)

            def tiles_out(k, i):
                for v in range(XB):
                    act.wait_ge(s_xt, START + (k * NI + i) * XB + v + 1)
                    act.copy(XT[:, 2 * v:2 * v + 2].rearrange("p u c n -> p (u c n)"), PS[:, v, :]).then_inc(s_xte, 1)

            def project(l, i, tiles):
                n = l * NI + i
                for u in tiles:
                    act.wait_ge(s_proj, START + n * U + u + 1)
                    if u == 0:
                        act.wait_ge(s_rot2, START + n)
                        act.wait_ge(s_hss, START + n)
                        act.wait_ge(s_vs, START + n * NVS)
                    act.copy(RAW[:, u, :], ps_p[:, u, 0:QKH * HD])
                    act.copy(VA[:, u * G:(u + 1) * G, :], ps_p[:, u, QKH * HD:QKV])
                    act.activation(SQ[:, u, :], ps_p[:, u, 0:QKH * HD], ACT.Square).then_inc(s_raw, 1)

            def head_roots(l, i):
                act.wait_ge(s_hss, START + l * NI + i + 1)
                act.activation(sr[:], ss[:], ACT.Sqrt, bias=eps[:, 0:1], scale=1.0 / HD).then_inc(s_hroot, 1)

            def copies(l, i):
                n = l * NI + i
                act.wait_ge(s_dve, START + n * NDVE + 5)
                act.copy(QS[:, :, 1, :], QS[:, :, 0, :])
                act.wait_ge(s_split, START + n + 1)
                k2 = KS[:].rearrange("p n (r c) d -> p n r (c d)", r=4)
                act.copy(k2[:, :, 1:4, :], k2[:, :, 0:1, :].to_broadcast([P, U * G, 3, 2 * HD])).then_inc(s_dup, 1)

            def stacks_out(l, i, tiles):
                for u in tiles:
                    act.wait_ge(s_qkt, START + (l * NI + i) * U + u + 1)
                    act.copy(QT[:, :, ds((i * U + u) * P, P)], ps_q[u % 2]).then_inc(s_qe, 1)

            def group_step(l, i, stacks=True, before=True, this=True):
                if stacks:
                    stacks_out(l, i - 2, (0, 1))
                if before:
                    head_roots(l, i - 1)
                if stacks:
                    stacks_out(l, i - 2, (2, 3))
                if this:
                    tiles_out(2 * l, i)
                    project(l, i, (0, 1))
                if before:
                    copies(l, i - 1)
                if this:
                    project(l, i, (2, 3))

            def exponentials(l, it):
                for n, step in enumerate(STEPS[l]):
                    at = BASE[l] + it * len(STEPS[l]) + n
                    cols = sum(HG * w for _, _, w in step)
                    act.wait_ge(s_score, START + at + 1)
                    act.wait_ge(s_pv, START + at - REUSE[l][n] + 1)
                    act.activation(PF[:, n % SLOTS, 0:cols], ps_s[:, n % SLOTS, 0:cols], ACT.Exp, scale=SCALE).then_inc(s_exp, 1)

            act.wait_ge(s_const, 1)
            act.wait_ge(s_loadx, 16 * NI)
            with act.Fori(0, NI) as i:
                squares(i, i)
            for l in range(2):
                act.wait_ge(s_ssq, START + (l + 1) * NI)
                act.activation(root[:], ssq[:], ACT.Sqrt, bias=eps[:, 0:1], scale=1.0 / D).then_inc(s_root, 1)
                group_step(l, 0, stacks=False, before=False)
                group_step(l, 1, stacks=False)
                with act.Fori(2, NI) as i:
                    group_step(l, i)
                group_step(l, NI, this=False)
                group_step(l, NI + 1, this=False, before=False)
                nc.scalar.preload_act_table(ACT.Exp)
                with act.Fori(0, BG) as it:
                    exponentials(l, it)
                with act.Fori(0, NI) as i:
                    tiles_out(2 * l + 1, i)
                    for u in range(U):
                        act.wait_ge(s_oproj, START + (l * NI + i) * U + u + 1)
                    if l == 0:
                        act.wait_ge(s_res, START + i + 1)
                        squares(i + NI, i)

            def roots(n):
                act.wait_ge(s_mv, n)
                act.activation(root[:], MV[:, :, 1], ACT.Sqrt, bias=eps[:, 1:2]).then_inc(s_root, 1)

            roots(1)
            with act.Fori(0, NI // 2) as j:
                for a in range(2):
                    i = j * 2 + a
                    act.wait_ge(s_cq, START + (i - 1) * DC)
                    for v in range(XB):
                        act.wait_ge(s_xt, START + (4 * NI + i) * XB + v + 1)
                        act.copy(XM[:, a].rearrange("p c (u n) -> p u c n", u=U)[:, 2 * v:2 * v + 2],
                                 PS[:, v, :].rearrange("p (u c n) -> p u c n", u=2, c=DC)).then_inc(s_xte, 1)
                    for o in range(DC):
                        act.wait_ge(s_cq, START + i * DC + o + 1)
                        act.activation(QC[:, o, ds(i * (U * P), U * P)], PS[:, 2 + o, :], ACT.Identity,
                                       bias=xb[:, 0, o:o + 1]).then_inc(s_cqe, 1)

            def transposed_out(at):
                act.wait_ge(s_cpt, START + at + 1)
                act.copy(CPT[:].rearrange("k h n -> k (h n)"), PS[0:CL, 0:2, :].rearrange("k a n -> k (a n)")).then_inc(s_cpe, 1)

            def cross_group(i, first=False):
                for m in range(CS):
                    at = i * CS + m
                    if not (first and m < LATE - 1):
                        transposed_out(at - LATE + 1)
                    act.wait_ge(s_csub, START + at + 1)
                    act.wait_ge(s_cpt, START + at - 1)
                    act.activation(CPX[:, m % 2], CLG[:, m % CLS], ACT.Exp).then_inc(s_cexp, 1)

            nc.scalar.preload_act_table(ACT.Exp)
            cross_group(0, first=True)
            with act.Fori(1, NI) as i:
                cross_group(i)
            for m in range(LATE - 1):
                transposed_out(NI * CS - LATE + 1 + m)
            with act.Fori(0, NI) as i:
                tiles_out(5, i)
            roots(2)
            with act.Fori(0, NI) as i:
                tiles_out(6, i)
                act.wait_ge(s_rl, START + i + 1)
                act.copy(LG[:, ds(i * U, U), :], PS[:, 2, 0:U * E].rearrange("p (u e) -> p u e", e=E)).then_inc(s_rle, 1)
            act.wait_ge(s_route, 12)
            act.activation(rc["e"][:], rc["d"][:], ACT.Exp).then_inc(s_gap, 1)

            def high_weights(m, par, w):
                act.wait_ge(s_wl[w], 16 * m + 16)
                if w == 0:
                    act.wait_ge(s_gu, START + (m - 1) * FP)
                if w == 2:
                    act.wait_ge(s_down, START + m - 1)
                act.copy(WH[par][:, w, :], RAWW[:, w, :]).then_inc(s_wh, 1)

            def high_rows(m, par):
                act.wait_ge(s_bt, START + m + 1)
                act.copy(XH[par][:].rearrange("p c n -> p (c n)"), PS[:, 7, :]).then_inc(s_bh, 1)

            def expert_block(m, par, first=False, last=False):
                for q in range(FP):
                    at = m * FP + q
                    act.wait_ge(s_gu, START + at + 1)
                    act.wait_ge(s_hm, START + at - 1)
                    act.activation(SG[:, q % 2], PS[:, 2 * (q % 2):2 * (q % 2) + 2, 0:BLK], ACT.Silu).then_inc(s_silu, 1)
                    if not last and q != 2:
                        high_weights(m + 1, 1 - par, {0: 0, 1: 1, 3: 2}[q])
                    if q == 2 and not first:
                        block_out(m - 1, 1 - par)
                    act.wait_ge(s_hm, START + at + 1)
                    if q == 0:
                        act.wait_ge(s_down, START + m - 1)
                    act.copy(HH[par][:, 2 * q:2 * q + 2, :], HF[:, q % 2]).then_inc(s_hh, 1)
                    if q == 2 and not last:
                        high_rows(m + 1, 1 - par)

            def block_out(m, par):
                act.wait_ge(s_down, START + m + 1)
                act.wait_ge(s_eof, START + m - 1)
                act.copy(EO[:, par].rearrange("p a d -> p (a d)"), PS[:, 4 + par, :]).then_inc(s_eo, 1)

            for w in range(3):
                high_weights(0, 0, w)
            high_rows(0, 0)
            expert_block(0, 0, first=True)
            with act.Fori(0, NBLK // 2 - 1) as j:
                expert_block(j * 2 + 1, 1)
                expert_block(j * 2 + 2, 0)
            expert_block(NBLK - 2, 1)
            expert_block(NBLK - 1, 0, last=True)
            block_out(NBLK - 1, 0)
            roots(3)

        @block.vector
        def _(dve):
            dve.sem_inc(s_ssq, START)
            dve.sem_inc(s_rstd, START)
            dve.sem_inc(s_xn, START)
            dve.sem_inc(s_dve, START)
            dve.sem_inc(s_hss, START)
            dve.sem_inc(s_split, START)
            dve.sem_inc(s_rest, START)
            dve.sem_inc(s_ke, START)
            dve.sem_inc(s_low, START)
            dve.sem_inc(s_osum, START)
            dve.sem_inc(s_on, START)
            dve.sem_inc(s_res, START)
            for s in (s_bn, s_clog, s_cmax, s_csub, s_crec, s_con, s_cres, s_wlo, s_bl, s_hm, s_hl):
                dve.sem_inc(s, START)

            def sums(n, i):
                dve.wait_ge(s_square, START + n + 1)
                dve.tensor_reduce(ssq[:, ds(i * U, U)], RAW.rearrange("p u n -> p (u n)")[:, 0:U * D]
                                  .rearrange("p (u n) -> p u n", u=U), AX.X, ALU.add).then_inc(s_ssq, 1)

            def normalise(l, i):
                dve.wait_ge(s_xt, START + (2 * l * NI + i) * XB)
                dve.tensor_tensor(XN[:], X[:, ds(i * U, U), :],
                                  rstd[:, ds(i * U, U)].unsqueeze(2).to_broadcast([P, U, D]), ALU.mult).then_inc(s_xn, 1)

            def rotate(l, i, stacks=True):
                n = l * NI + i
                step = START + n * NDVE
                out = (lambda u: stack_out(l, i - 1, u)) if stacks else (lambda u: None)
                dve.wait_ge(s_raw, START + n * U + U)
                four = lambda a: a[:].rearrange("p u (h d) -> p u h d", h=QKH)
                out(0)
                dve.tensor_tensor(four(R1), RAW.rearrange("p u (h d) -> p u h d", h=QKH),
                                  rope_sb[:, l, 0, ds(i * U, U), :].unsqueeze(2).to_broadcast([P, U, QKH, HD]),
                                  ALU.mult).then_inc(s_dve, 1)
                out(1)
                out(2)
                dve.tensor_reduce(ss[:], SQ.rearrange("p u (h d) -> p (u h) d", d=HD), AX.X, ALU.add).then_inc(s_hss, 1)
                out(3)
                dve.wait_ge(s_rot2, START + n + 1)
                dve.wait_ge(s_dve, step + 1)
                dve.tensor_tensor(R1[:], R1[:], R2[:], ALU.add).then_inc(s_dve, 1)
                dve.wait_ge(s_hroot, START + n + 1)
                dve.reciprocal(rn[:], sr[:]).then_inc(s_dve, 1)
                dve.wait_ge(s_dve, step + 3)
                dve.wait_ge(s_stack, START + n)
                r = four(R1)
                inv = rn[:].rearrange("p (u h) -> p u h", u=U)
                for dst, a, b in ((RQ, 0, H), (RK, H, QKH)):
                    last = dve.tensor_tensor(dst[:].rearrange("p (u h) d -> p u h d", u=U), r[:, :, a:b, :],
                                             inv[:, :, a:b].unsqueeze(3).to_broadcast([P, U, b - a, HD]), ALU.mult)
                last.then_inc(s_dve, 1)

            def split(l, i):
                n = l * NI + i
                step = START + n * NDVE
                dve.wait_ge(s_qkt, START + n * U)
                dve.wait_ge(s_dve, step + 4)
                dve.tensor_copy(KS[:, :, 0, :], RK[:])
                dve.tensor_copy(QS[:, :, 0, :], RQ[:]).then_inc(s_dve, 1)
                dve.wait_ge(s_dve, step + 5)
                dve.tensor_tensor(KS[:, :, 1, :], RK[:], KS[:, :, 0, :], ALU.subtract).then_inc(s_split, 1)
                dve.tensor_tensor(QS[:, :, 2, :], RQ[:], QS[:, :, 0, :], ALU.subtract).then_inc(s_rest, 1)

            def stack_out(l, i, u):
                k4 = KT[:].rearrange("p (g e) t -> p g e t", e=2)
                t = ds((i * U + u) * P, P)
                dve.wait_ge(s_qkt, START + (l * NI + i) * U + u + 1)
                dve.tensor_copy(k4[0:64, :, 0, t], ps_k[u % 2][0:64])
                dve.tensor_copy(k4[64:P, :, 1, t], ps_k[u % 2][64:P]).then_inc(s_ke, 1)

            def attend(l, it, first=False):
                for n, step in enumerate(STEPS[l]):
                    at = BASE[l] + it * len(STEPS[l]) + n
                    cut, cols = low_share(step)
                    dve.wait_ge(s_exp, START + at + 1)
                    dve.wait_ge(s_pv, START + at - REUSE[l][n] + 1)
                    pf = PF[:, n % SLOTS, 0:cut]
                    dve.tensor_tensor(PL[:, n % SLOTS, 0:cut], pf, high_part(pf), ALU.subtract).then_inc(s_low, 1)
                    for q in range(TB):
                        if DONE[l][q] == n - 2:
                            finish(l, it, q)
                        elif DONE[l][q] == n - 2 + len(STEPS[l]) and not first:
                            finish(l, it - 1, q)

            def finish(l, it, q):
                a, k = q % 2, l * BG * TB + it * TB + q
                dve.wait_ge(s_pv, START + BASE[l] + it * len(STEPS[l]) + DONE[l][q] + 1)
                dve.reciprocal(OR[:, a], ps_o[:, a, :, 3 * HD:VW])
                dve.tensor_reduce(OS[:, a], ps_o[:, a, :, 0:3 * HD].rearrange("p h (c d) -> p h d c", c=3),
                                  AX.X, ALU.add).then_inc(s_osum, 1)
                dve.wait_ge(s_osum, START + k + 1)
                dve.tensor_tensor(OA[:, ds(it // G * TB + q, 1), ds(it % G * (HG * HD), HG * HD)]
                                  .rearrange("p a (h d) -> p (a h) d", h=HG),
                                  OS[:, a], OR[:, a].to_broadcast([P, HG, HD]), ALU.mult).then_inc(s_on, 1)

            k4 = KT[:].rearrange("p (g e) t -> p g e t", e=2)
            dve.memset(k4[64:P, :, 0, :], 0.0)
            dve.memset(k4[0:64, :, 1, :], 0.0).then_inc(s_zero, 1)
            dve.wait_ge(s_loadw, NLOAD)
            dve.wait_ge(s_fuse, 1)
            for c in range(DC):
                dve.tensor_scalar(W[0][:, c, D:QKV], PS[:, 6 + c, 0:P], nw[:, 0, c:c + 1], None, ALU.mult)
                dve.tensor_scalar(W[0][:, c, 0:D], W[0][:, c, 0:D], nw[:, 0, c:c + 1], None, ALU.mult)
                last = dve.tensor_scalar(W[1][:, c, :], W[1][:, c, :], nw[:, 1, c:c + 1], None, ALU.mult)
            last.then_inc(s_weights, 1)
            dve.wait_ge(s_cload, NCLOAD)
            dve.wait_ge(s_ckv, 1)
            for o in range(DC):
                last = dve.tensor_scalar(KB[:, o, :], PS[:, 4 + o, 0:NB * CL], xb[:, 1, o:o + 1], None, ALU.add)
            for b in range(NB):
                last = dve.tensor_tensor(VX[:, b, :, 0:HD], PS[0:CL, 2 + b, 0:D].rearrange("k (h d) -> k h d", h=H),
                                         BV[:].rearrange("k (h d) -> k h d", h=H), ALU.add)
            last.then_inc(s_ckb, 1)
            dve.wait_ge(s_ckb, 1)
            for b in range(NB):
                for o in range(DC):
                    last = dve.tensor_tensor(KZ[:, b, o], KB[:, o, b * CL:(b + 1) * CL].unsqueeze(1).to_broadcast([P, CH, CL]),
                                             own.unsqueeze(2).to_broadcast([P, CH, CL]), ALU.mult)
            dve.tensor_scalar(MF[:], MF[:], FMAX, None, ALU.mult)
            last = dve.memset(VX[:, :, :, HD:HD + 1], 1.0)
            last.then_inc(s_ckz, 1)
            with dve.Fori(0, NI) as i:
                sums(i, i)
            for l in range(2):
                dve.wait_ge(s_root, START + l + 1)
                dve.reciprocal(rstd[:], root[:]).then_inc(s_rstd, 1)
                dve.wait_ge(s_rstd, START + l + 1)
                normalise(l, 0)
                normalise(l, 1)
                rotate(l, 0, stacks=False)
                split(l, 0)
                with dve.Fori(2, NI) as i:
                    normalise(l, i)
                    rotate(l, i - 1)
                    split(l, i - 1)
                rotate(l, NI - 1)
                split(l, NI - 1)
                for u in range(U):
                    stack_out(l, NI - 1, u)
                attend(l, 0, first=True)
                with dve.Fori(1, BG) as it:
                    attend(l, it)
                for q in range(TB):
                    if DONE[l][q] >= len(STEPS[l]) - 2:
                        finish(l, BG - 1, q)
                with dve.Fori(0, NI) as i:
                    dve.wait_ge(s_oproj, START + (l * NI + i) * U + U)
                    xs = X[:, ds(i * U, U), :]
                    dve.tensor_tensor(xs, xs, ps_p[:, :, 0:D], ALU.add).then_inc(s_res, 1)
                    if l == 0:
                        sums(i + NI, i)

            def means(n):
                dve.wait_ge(s_stat, n * NI)
                for t in range(NT):
                    last = dve.bn_aggr(MV[:, t, :], ST[:, t, :])
                last.then_inc(s_mv, 1)
                dve.wait_ge(s_root, START + 2 + n)
                dve.reciprocal(rstd[:], root[:]).then_inc(s_rstd, 1)
                dve.wait_ge(s_rstd, START + 2 + n)
                dve.wait_ge(s_mv, n)

            def rows(dst, i, u):
                t = i * U + u
                return dve.tensor_scalar(dst, X[:, ds(t, 1), :].rearrange("p a d -> p (a d)"),
                                         MV[:, ds(t, 1), 0], rstd[:, ds(t, 1)], ALU.subtract, ALU.mult)

            def statistics(i):
                for u in range(U):
                    last = dve.bn_stats(ST[:, ds(i * U + u, 1), :].rearrange("p a s -> p (a s)"),
                                        X[:, ds(i * U + u, 1), :].rearrange("p a d -> p (a d)"))
                last.then_inc(s_stat, 1)

            dve.wait_ge(s_x0, 16 * NI)
            dve.wait_ge(s_res, START + 2 * NI)
            with dve.Fori(0, NI) as i:
                xs = X[:, ds(i * U, U), :]
                dve.tensor_tensor(xs, xs, OA[:, ds(i * U, U), :], ALU.add).then_inc(s_bn, 1)
                dve.wait_ge(s_bn, START + i + 1)
                statistics(i)
            means(1)
            with dve.Fori(0, NI // 2) as j:
                for a in range(2):
                    i = j * 2 + a
                    dve.wait_ge(s_xt, START + (4 * NI + i - 1) * XB)
                    dve.wait_ge(s_xb, START + i - 1)
                    for u in range(U):
                        last = rows(XS[:, a, u, :], i, u)
                    last.then_inc(s_xn, 1)

            def logits(i, m):
                u, a, c, at = m // DC, m % 2, m % CLS, i * CS + m
                dve.wait_ge(s_cs, START + at + 1)
                dve.wait_ge(s_cexp, START + at - CLS + 1)
                ps = PS[:, 4 + 2 * a:6 + 2 * a, 0:CH // 2 * CL].rearrange("p b (h k) -> p b h k", h=CH // 2)
                lg = CLG[:, c].rearrange("p (b h) k -> p b h k", b=2)
                mf = MF[:, ds(i * U + u, 1), :]
                dve.tensor_tensor(lg, ps, mf.unsqueeze(1).to_broadcast([P, 2, CH // 2, CL]), ALU.subtract).then_inc(s_clog, 1)
                dve.wait_ge(s_clog, START + at + 1)
                dve.tensor_reduce(CMX[:, a], CLG[:, c], AX.X, ALU.max).then_inc(s_cmax, 1)
                dve.wait_ge(s_cmax, START + at + 1)
                dve.tensor_tensor(CLG[:, c], CLG[:, c], CMX[:, a].to_broadcast([P, CH, CL]), ALU.subtract).then_inc(s_csub, 1)

            def normalise_step(i, m):
                u, o, a, at = m // DC, m % DC, m % 2, i * CS + m
                dve.wait_ge(s_cpv, START + at + 1)
                ps = PS[:, 2 + o, 0:CH * (HD + 1)].rearrange("p (h d) -> p h d", h=CH)
                dve.reciprocal(CR[:, a], ps[:, :, HD:HD + 1]).then_inc(s_crec, 1)
                dve.wait_ge(s_crec, START + at + 1)
                dve.tensor_tensor(OX[:, ds(i * U + u, 1), o * P:(o + 1) * P].rearrange("p a (h d) -> p (a h) d", h=CH),
                                  ps[:, :, 0:HD], CR[:, a].to_broadcast([P, CH, HD]), ALU.mult).then_inc(s_con, 1)

            def cross_group(i, first=False):
                for m in range(CS):
                    logits(i, m)
                    if m >= LATE:
                        normalise_step(i, m - LATE)
                    elif not first:
                        normalise_step(i - 1, m - LATE + CS)

            cross_group(0, first=True)
            with dve.Fori(1, NI) as i:
                cross_group(i)
            for m in range(CS - LATE, CS):
                normalise_step(NI - 1, m)
            with dve.Fori(0, NI // 2) as j:
                for a in range(2):
                    i = j * 2 + a
                    dve.wait_ge(s_cwo, START + i * XB + XB)
                    xs = X[:, ds(i * U, U), :]
                    dve.tensor_tensor(xs, xs, PS[:, 2 + 2 * a:4 + 2 * a, :].rearrange("p b (u d) -> p (b u) d", u=2),
                                      ALU.add).then_inc(s_cres, 1)
                    dve.wait_ge(s_cres, START + i + 1)
                    statistics(i)
            means(2)
            with dve.Fori(0, NI) as i:
                dve.wait_ge(s_xt, START + (6 * NI + i) * XB)
                for u in range(U):
                    rows(XN[:, u, :], i, u)
                    last = rows(X[:, ds(i * U + u, 1), :].rearrange("p a d -> p (a d)"), i, u)
                last.then_inc(s_xn, 1)

            count = [0]

            def then(ins):
                count[0] += 1
                ins.then_inc(s_route, 1)
                dve.wait_ge(s_route, count[0])

            te = [P, NT, E]
            dve.wait_ge(s_rle, START + NI)
            wide = lambda a: a.unsqueeze(2).to_broadcast(te)
            each = lambda a: a.unsqueeze(1).to_broadcast(te)
            for k, logits in (("1", LG[:]), ("2", rt["left"][:])):
                if k == "2":
                    then(dve.scalar_tensor_tensor(out=rt["left"][:], in0=rt["one1"][:], scalar=-FMAX, in1=LG[:],
                                                  op0=ALU.mult, op1=ALU.add))
                then(dve.tensor_reduce(rc["m" + k][:], logits, AX.X, ALU.max))
                then(dve.tensor_tensor(rt["eq" + k][:], logits, wide(rc["m" + k][:]), ALU.is_equal))
                then(dve.scalar_tensor_tensor(out=rt["code" + k][:], in0=rt["eq" + k][:], scalar=-float(E),
                                              in1=each(expert_no), op0=ALU.mult, op1=ALU.add))
                then(dve.tensor_reduce(rc["i" + k][:], rt["code" + k][:], AX.X, ALU.min))
                then(dve.tensor_tensor(rt["one" + k][:], rt["code" + k][:], wide(rc["i" + k][:]), ALU.is_equal))
            then(dve.tensor_tensor(rc["d"][:], rc["m2"][:], rc["m1"][:], ALU.subtract))
            then(dve.tensor_tensor(SW[:, :, 0:E], rt["one1"][:], rt["one2"][:], ALU.add))
            dve.wait_ge(s_gap, 1)
            then(dve.tensor_scalar(rc["den"][:], rc["e"][:], 1.0, None, ALU.add))
            then(dve.reciprocal(rc["r"][:], rc["den"][:]))
            then(dve.tensor_tensor(rc["p2"][:], rc["e"][:], rc["r"][:], ALU.mult))
            then(dve.tensor_tensor(rt["w1"][:], rt["one1"][:], wide(rc["r"][:]), ALU.mult))
            then(dve.tensor_tensor(rt["w2"][:], rt["one2"][:], wide(rc["p2"][:]), ALU.mult))
            then(dve.tensor_tensor(SW[:, :, E:2 * E], rt["w1"][:], rt["w2"][:], ALU.add))
            assert count[0] == NSHARES
            dve.wait_ge(s_tot, 1)
            then(dve.tensor_copy(TOT[:].rearrange("p t e -> p (t e)"), PS[:, 3, 0:NT * 2 * E]))
            dve.memset(rt["pfa"][:, 0:1, :], 0.0)
            then(dve.tensor_copy(rt["pfa"][:, 1:NT, :], TOT[:, 0:NT - 1, 0:E]))
            a, b = rt["pfa"], rt["pfb"]
            for d in (1, 2, 4, 8):
                dve.tensor_copy(b[:, 0:d, :], a[:, 0:d, :])
                then(dve.tensor_tensor(b[:, d:NT, :], a[:, d:NT, :], a[:, 0:NT - d, :], ALU.add))
                a, b = b, a
            then(dve.tensor_tensor(rt["t1"][:], a[:], PS[:, 4, 0:NT * E].rearrange("p (t e) -> p t e", e=E), ALU.add))
            then(dve.tensor_tensor(re["cnt"][:], a[:, NT - 1, :], TOT[:, NT - 1, 0:E], ALU.add))
            then(dve.tensor_tensor(GTJ[:], re["cnt"][:].unsqueeze(2).to_broadcast([P, E, NJ]),
                                   block_rows.rearrange("p (e j) -> p e j", e=E), ALU.is_gt))
            then(dve.tensor_reduce(re["nb"][:], GTJ[:], AX.X, ALU.add))
            dve.memset(re["bba"][:, 0:1], 0.0)
            then(dve.tensor_copy(re["bba"][:, 1:E], re["nb"][:, 0:E - 1]))
            a, b = re["bba"], re["bbb"]
            for d in (1, 2, 4):
                dve.tensor_copy(b[:, 0:d], a[:, 0:d])
                then(dve.tensor_tensor(b[:, d:E], a[:, d:E], a[:, 0:E - d], ALU.add))
                a, b = b, a
            then(dve.tensor_tensor(re["end"][:], a[:], re["nb"][:], ALU.add))
            then(dve.tensor_tensor(LEB[:], re["end"][:].unsqueeze(1).to_broadcast([P, NBLK, E]),
                                   block_no.unsqueeze(2).to_broadcast([P, NBLK, E]), ALU.is_le))
            then(dve.tensor_reduce(EBF[:], LEB[:], AX.X, ALU.add))
            then(dve.tensor_scalar(EB[:], EBF[:], float(E - 1), None, ALU.min))
            then(dve.scalar_tensor_tensor(out=rt["slot"][:], in0=each(a[:]), scalar=float(BLK), in1=rt["t1"][:],
                                          op0=ALU.mult, op1=ALU.add))
            for k in range(2):
                then(dve.tensor_tensor(rt["t2"][:], rt[f"one{k + 1}"][:], rt["slot"][:], ALU.mult))
                then(dve.tensor_reduce(POSF[:, k], rt["t2"][:], AX.X, ALU.add))
            then(dve.tensor_copy(SLOT[:], POSF[:]))
            then(dve.tensor_reduce(re["sumw"][:], TOT[:, :, E:2 * E].rearrange("p t e -> p e t"), AX.X, ALU.add))
            then(dve.tensor_scalar(re["one"][:], re["cnt"][:], 1.0, None, ALU.max))
            then(dve.reciprocal(re["inv"][:], re["one"][:]))
            then(dve.tensor_tensor(re["mean"][:], re["sumw"][:], re["inv"][:], ALU.mult))
            for k in range(2):
                then(dve.tensor_tensor(rt["t2"][:], rt[f"one{k + 1}"][:], each(re["mean"][:]), ALU.mult))
                then(dve.tensor_reduce(CO[:, k], rt["t2"][:], AX.X, ALU.add))
            assert count[0] == NROUTE

            def low_weights(m, par, w):
                dve.wait_ge(s_wh, START + m * 3 + w + 1)
                if w == 2:
                    dve.wait_ge(s_down, START + m - 1)
                dve.tensor_tensor(WL[par][:, w, :], RAWW[:, w, :], WH[par][:, w, :].bitcast(F32), ALU.subtract).then_inc(s_wlo, 1)

            def low_rows(m, par):
                dve.wait_ge(s_bh, START + m + 1)
                dve.tensor_tensor(XL[par][:].rearrange("p c n -> p (c n)"), PS[:, 7, :],
                                  XH[par][:].rearrange("p c n -> p (c n)").bitcast(F32), ALU.subtract).then_inc(s_bl, 1)

            def expert_block(m, par, last=False):
                for q in range(FP):
                    at = m * FP + q
                    dve.wait_ge(s_silu, START + at + 1)
                    dve.wait_ge(s_hh, START + at - 1)
                    dve.tensor_tensor(HF[:, q % 2], SG[:, q % 2], PS[:, 2 * (q % 2):2 * (q % 2) + 2, BLK:2 * BLK],
                                      ALU.mult).then_inc(s_hm, 1)
                    if not last and q != 2:
                        low_weights(m + 1, 1 - par, {0: 0, 1: 1, 3: 2}[q])
                    dve.wait_ge(s_hh, START + at + 1)
                    if q == 0:
                        dve.wait_ge(s_down, START + m - 1)
                    dve.tensor_tensor(HL[par][:, 2 * q:2 * q + 2, :], HF[:, q % 2],
                                      HH[par][:, 2 * q:2 * q + 2, :].bitcast(F32), ALU.subtract).then_inc(s_hl, 1)
                    if q == 2 and not last:
                        low_rows(m + 1, 1 - par)

            for w in range(3):
                low_weights(0, 0, w)
            low_rows(0, 0)
            expert_block(0, 0)
            with dve.Fori(0, NBLK // 2 - 1) as j:
                expert_block(j * 2 + 1, 1)
                expert_block(j * 2 + 2, 0)
            expert_block(NBLK - 2, 1)
            expert_block(NBLK - 1, 0, last=True)

            for i in range(NI):
                dve.wait_ge(s_gat[i % 2], 2 * U * 16 * (i // 2 + 1))
                for k in range(2):
                    for u in range(U):
                        t = i * U + u
                        last = dve.scalar_tensor_tensor(out=X[:, t, :], in0=YB[:, i % 2, k, u, :], scalar=CO[:, k, t:t + 1],
                                                        in1=X[:, t, :], op0=ALU.mult, op1=ALU.add)
                    last.then_inc(s_mix, 1)
                    dve.wait_ge(s_mix, 2 * i + k + 1)
                statistics(i)
            means(3)
            for i in range(NI):
                for u in range(U):
                    last = rows(X[:, i * U + u, :], i, u)
                last.then_inc(s_fin, 1)

        @block.tensor
        def _(pe):
            pe.sem_inc(s_xt, START)
            pe.sem_inc(s_proj, START)
            pe.sem_inc(s_qkt, START)
            pe.sem_inc(s_score, START)
            pe.sem_inc(s_pv, START)
            pe.sem_inc(s_oproj, START)
            for s in (s_cq, s_cs, s_cpt, s_cpv, s_cwo, s_rl, s_bt, s_gu, s_down):
                pe.sem_inc(s, START)

            pe.wait_ge(s_loadw, NLOAD)
            for c in range(DC):
                last = pe.matmul(PS[:, 6 + c, 0:P], kvd_sb[:, c * P:(c + 1) * P], kvup_sb[:], start=True, stop=True)
            last.then_inc(s_fuse, 1)
            pe.wait_ge(s_cload, NCLOAD)
            for o in range(DC):
                for c in range(DC):
                    pe.matmul(PS[:, 4 + o, 0:NB * CL], WX[:, 1, c, o * P:(o + 1) * P], ctx_sb[:, c, :],
                              start=(c == 0), stop=(c == DC - 1))
            for b in range(NB):
                for c in range(DC):
                    last = pe.matmul(PS[0:CL, 2 + b, 0:D], ctx_sb[:, c, b * CL:(b + 1) * CL], WX[:, 2, c, :],
                                     start=(c == 0), stop=(c == DC - 1))
            last.then_inc(s_ckv, 1)
            pe.wait_ge(s_ckb, 1)

            def transposes(k, i):
                pe.wait_ge(s_xn, START + k * NI + i + 1)
                transpose_group(k * NI + i, XN)

            def transpose_group(n, rows):
                pe.wait_ge(s_xte, START + n * XB)
                for v in range(XB):
                    for u in (2 * v, 2 * v + 1):
                        for c in range(DC):
                            last = pe.transpose(ps_x[:, u, c * P:(c + 1) * P], rows[:, u, c * P:(c + 1) * P], identF)
                    last.then_inc(s_xt, 1)

            def products(k, i, w, cols, s_done, s_free, free):
                for u in range(U):
                    if u % 2 == 0:
                        pe.wait_ge(s_xte, START + (k * NI + i) * XB + u // 2 + 1)
                    if u == 0:
                        pe.wait_ge(s_free, START + free)
                    for c in range(DC):
                        last = pe.matmul(ps_p[:, u, 0:cols], XT[:, u, c, :], w[:, c, 0:cols],
                                         start=(c == 0), stop=(c == DC - 1))
                    last.then_inc(s_done, 1)

            def stack_transposes(l, i):
                n = l * NI + i
                pe.wait_ge(s_stack, START + n + 1)
                pe.wait_ge(s_rest, START + n + 1)
                pe.wait_ge(s_dup, START + n + 1)
                for u in range(U):
                    pe.wait_ge(s_qe, START + n * U + u - 1)
                    pe.wait_ge(s_ke, START + n * U + u - 1)
                    for h in range(H // 2):
                        pe.transpose(ps_q[u % 2][:, h, :], QS2[:, u * H // 2 + h, :], identH[:])
                    for g in range(G):
                        last = pe.transpose(ps_k[u % 2][:, g, :], KS2[:, u * G + g, :], identH[:])
                    last.then_inc(s_qkt, 1)

            def scores(l, it, n):
                at = BASE[l] + it * len(STEPS[l]) + n
                b, g = it // G, it % G
                pe.wait_ge(s_exp, START + at - REUSE[l][n] + 1)
                col = 0
                for q, k, w in STEPS[l][n]:
                    into = ps_s[:, n % SLOTS, col:col + HG * w]
                    table = None if k < q and l == 0 else 0 if l == 0 else 1 if k == q else 2
                    if table is not None:
                        pe.matmul(into, identB[:], hide[:, table, :, 0:w], start=True, stop=False, skip_group_check=True)
                    for e in range(2):
                        last = pe.matmul(into[:, e * 2 * w:(e + 1) * 2 * w], KTf[:, ds((g * 2 + e) * T + b * S + k * P, P)],
                                         QT[:, ds(g * 2, 2), ds(b * S + q * P, w)],
                                         start=(table is None and e == 0), stop=(e == 1), skip_group_check=True)
                    col += HG * w
                last.then_inc(s_score, 1)

            def values(l, it, n):
                at = BASE[l] + it * len(STEPS[l]) + n
                b, g = it // G, it % G
                pe.wait_ge(s_exp, START + at + 1)
                pe.wait_ge(s_low, START + at + 1)
                pe.wait_ge(s_lowp, START + at + 1)
                col = 0
                for q, k, w in STEPS[l][n]:
                    first = k == 0 if l == 0 else k == q
                    if first:
                        pe.wait_ge(s_on, START + l * BG * TB + it * TB + q - 1)
                    vs = VSf[:, ds(((b * TB + k) * G + g) * VW, VW)]
                    for h in range(HG):
                        at_h = head_column(h, w) + col
                        pf = high_part(PF[:, n % SLOTS, at_h:at_h + w])
                        pl = PL[:, n % SLOTS, at_h:at_h + w]
                        for part, p in enumerate((pf, pl)):
                            last = pe.matmul(ps_o[0:w, q % 2, h, :], p, vs, start=(first and h == 0 and part == 0),
                                             stop=True, skip_group_check=True)
                    col += HG * w
                last.then_inc(s_pv, 1)

            def attend(l, it, last=False):
                for n in range(len(STEPS[l])):
                    if n + 2 < len(STEPS[l]):
                        scores(l, it, n + 2)
                    elif not last:
                        scores(l, it + 1, n + 2 - len(STEPS[l]))
                    values(l, it, n)

            def head_column(h, w):
                return ((h % 2) * 2 + h // 2) * w

            pe.wait_ge(s_const, 2)
            pe.wait_ge(s_weights, 1)
            for l in range(2):
                def project(i):
                    pe.wait_ge(s_qe, START + (l * NI + i - 1) * U - 1)
                    pe.wait_ge(s_ke, START + (l * NI + i - 1) * U - 1)
                    transposes(2 * l, i)
                    products(2 * l, i, W[l], QKV, s_proj, s_raw, (l * NI + i) * U)
                project(0)
                project(1)
                with pe.Fori(2, NI) as i:
                    pe.wait_ge(s_xte, START + (2 * l * NI + i) * XB)
                    stack_transposes(l, i - 2)
                    project(i)
                pe.wait_ge(s_xte, START + (2 * l + 1) * NI * XB)
                stack_transposes(l, NI - 2)
                stack_transposes(l, NI - 1)
                pe.wait_ge(s_qe, START + (l + 1) * NT)
                pe.wait_ge(s_ke, START + (l + 1) * NT)
                pe.wait_ge(s_vs, START + (l + 1) * NI * NVS)
                scores(l, 0, 0)
                scores(l, 0, 1)
                with pe.Fori(0, BG - 1) as it:
                    attend(l, it)
                attend(l, BG - 1, last=True)
                with pe.Fori(0, NI) as i:
                    transposes(2 * l + 1, i)
                    products(2 * l + 1, i, WO[l], D, s_oproj, s_res, l * NI + i)

            def cross_scores(i, m):
                u, o, a, n = m // DC, m % DC, m % 2, i * CS + m
                if o == 0:
                    pe.wait_ge(s_qg, START + i * U + u + 1)
                pe.wait_ge(s_clog, START + n - 1)
                for j in range(2):
                    w = CH // 2 * CL
                    last = pe.matmul(PS[:, 4 + 2 * a + j, 0:w], QG[:, o, u * P:(u + 1) * P],
                                     KZf[:, ds(((i // (NI // NB) * DC + o) * 2 + j) * w, w)], start=True, stop=True)
                last.then_inc(s_cs, 1)

            def cross_transposes(i, m):
                n = i * CS + m
                pe.wait_ge(s_cexp, START + n + 1)
                for h in range(CH):
                    last = pe.transpose(PS[0:CL, h // 4, (h % 4) * P:(h % 4 + 1) * P], CPX[:, m % 2, h, :], identF)
                last.then_inc(s_cpt, 1)

            def cross_values(i, m):
                o, n = m % DC, i * CS + m
                pe.wait_ge(s_cpe, START + n + 1)
                pe.wait_ge(s_con, START + n - 1)
                for h in range(CH):
                    last = pe.matmul(PS[:, 2 + o, h * (HD + 1):(h + 1) * (HD + 1)], CPT[:, h, :],
                                     VXf[:, ds((i // (NI // NB) * H + o * CH + h) * (HD + 1), HD + 1)], start=True, stop=True)
                last.then_inc(s_cpv, 1)

            def cross_group(i, first=False):
                for m in range(CS):
                    if m >= LATE:
                        cross_transposes(i, m - LATE)
                    elif not first:
                        cross_transposes(i - 1, m - LATE + CS)
                    cross_scores(i, m)
                    if m >= LATE:
                        cross_values(i, m - LATE)
                    elif not first:
                        cross_values(i - 1, m - LATE + CS)

            pe.wait_ge(s_ckz, 1)
            with pe.Fori(0, NI // 2) as j:
                for a in range(2):
                    i = j * 2 + a
                    pe.wait_ge(s_xn, START + 4 * NI + i + 1)
                    transpose_group(4 * NI + i, XS[:, a])
                    pe.wait_ge(s_xte, START + (4 * NI + i + 1) * XB)
                    for o in range(DC):
                        pe.wait_ge(s_cqe, START + (i - 1) * DC + o + 1)
                        for c in range(DC):
                            last = pe.matmul(PS[:, 2 + o, :], WX[:, 0, c, o * P:(o + 1) * P], XM[:, a, c, :],
                                             start=(c == 0), stop=(c == DC - 1))
                        last.then_inc(s_cq, 1)
            cross_group(0, first=True)
            with pe.Fori(1, NI) as i:
                cross_group(i)
            for m in range(CS - LATE, CS):
                cross_transposes(NI - 1, m)
                cross_values(NI - 1, m)
            pe.wait_ge(s_con, START + NI * CS)
            with pe.Fori(0, NI // 2) as j:
                for a in range(2):
                    i = j * 2 + a
                    pe.wait_ge(s_ostage, START + i + 1)
                    transpose_group(5 * NI + i, XS[:, a])
                    pe.wait_ge(s_cres, START + i - 1)
                    for u in range(U):
                        if u % 2 == 0:
                            pe.wait_ge(s_xte, START + (5 * NI + i) * XB + u // 2 + 1)
                        for c in range(DC):
                            last = pe.matmul(PS[:, 2 + 2 * a + u // 2, (u % 2) * D:(u % 2 + 1) * D], XT[:, u, c, :], WX[:, 3, c, :],
                                             start=(c == 0), stop=(c == DC - 1))
                        if u % 2:
                            last.then_inc(s_cwo, 1)

            with pe.Fori(0, NI) as i:
                pe.wait_ge(s_xn, START + 5 * NI + i + 1)
                transpose_group(6 * NI + i, XN)
                pe.wait_ge(s_xte, START + (6 * NI + i + 1) * XB)
                pe.wait_ge(s_rle, START + i)
                for u in range(U):
                    for c in range(DC):
                        last = pe.matmul(PS[:, 2, u * E:(u + 1) * E], XT[:, u, c, :], RW[:, c, :],
                                         start=(c == 0), stop=(c == DC - 1))
                last.then_inc(s_rl, 1)
            pe.wait_ge(s_route, NSHARES)
            pe.matmul(PS[:, 3, 0:NT * 2 * E], ONES[:], SW[:].rearrange("p t e -> p (t e)"), start=True, stop=True)
            pe.matmul(PS[:, 4, 0:NT * E], before, SW[:, :, 0:E], start=True, stop=True).then_inc(s_tot, 1)

            def three(into, hs, ls, hm, lm, start, stop):
                pe.matmul(into, hs, hm, start=start, stop=False, skip_group_check=True)
                pe.matmul(into, hs, lm, start=False, stop=False, skip_group_check=True)
                return pe.matmul(into, ls, hm, start=False, stop=stop, skip_group_check=True)

            def block_rows_in(m, par, half):
                pe.wait_ge(s_xbl[par], 16 * half + 16)
                pe.wait_ge(s_bl, START + m)
                for c in range(DC):
                    for a in range(BA):
                        last = pe.transpose(PS[:, 7, (c * BA + a) * P:(c * BA + a + 1) * P],
                                            XR[:, par, a, c * P:(c + 1) * P], identF)
                last.then_inc(s_bt, 1)

            def down(m, par):
                pe.wait_ge(s_hl, START + m * FP + FP)
                pe.wait_ge(s_wlo, START + m * 3 + 3)
                pe.wait_ge(s_eo, START + m - 1)
                for a in range(BA):
                    for f in range(FC):
                        last = three(PS[:, 4 + par, a * D:(a + 1) * D],
                                     HH[par][:, f, a * P:(a + 1) * P], HL[par][:, f, a * P:(a + 1) * P],
                                     WH[par][:, 2, f * D:(f + 1) * D], WL[par][:, 2, f * D:(f + 1) * D],
                                     start=(a == 0 and f == 0), stop=(f == FC - 1))
                last.then_inc(s_down, 1)

            def expert_block(m, par, half, first=False, last=False):
                pe.wait_ge(s_bl, START + m + 1)
                pe.wait_ge(s_wlo, START + m * 3 + 2)
                for q in range(FP):
                    pe.wait_ge(s_hm, START + m * FP + q - 1)
                    for f in (2 * q, 2 * q + 1):
                        for w in range(2):
                            for c in range(DC):
                                at = c * FI + f * P
                                done = three(PS[:, 2 * (q % 2) + f % 2, w * BLK:(w + 1) * BLK],
                                             WH[par][:, w, at:at + P], WL[par][:, w, at:at + P],
                                             XH[par][:, c, :], XL[par][:, c, :],
                                             start=(w == 0 and c == 0), stop=(c == DC - 1))
                    done.then_inc(s_gu, 1)
                    if q == 1 and not first:
                        down(m - 1, 1 - par)
                    if q == 2 and not last:
                        block_rows_in(m + 1, 1 - par, half if par == 0 else half + 1)

            block_rows_in(0, 0, 0)
            expert_block(0, 0, 0, first=True)
            with pe.Fori(0, NBLK // 2 - 1) as j:
                expert_block(j * 2 + 1, 1, j)
                expert_block(j * 2 + 2, 0, j + 1)
            expert_block(NBLK - 2, 1, NBLK // 2 - 1)
            expert_block(NBLK - 1, 0, NBLK // 2, last=True)
            down(NBLK - 1, 0)


def low_share(step):
    cols = sum(HG * w for _, _, w in step)
    return cols * 5 // 8, cols


def high_part(a):
    return a.bitcast(BF16).rearrange("p (n two) -> p n two", two=2)[:, :, 1]


def constants():
    f = np.float32
    rope = np.zeros((P, 2, 2, NT, HD), f)
    for l, base in enumerate((1000000.0, 10000.0)):
        inv = f(1.0) / np.power(f(base), np.arange(0, HD, 2, dtype=f) / f(HD)).astype(f)
        ang = (np.arange(S, dtype=f)[:, None] * inv[None, :]).astype(f)
        c, s = np.cos(ang).astype(f), np.sin(ang).astype(f)
        both = np.stack([np.repeat(c, 2, 1), np.stack([-s, s], -1).reshape(S, HD)])
        both = np.tile(both.reshape(2, TB, P, HD), (1, NB, 1, 1))
        rope[:, l] = both.transpose(2, 0, 1, 3)
    small = np.zeros((P, 16 + E * NJ + NBLK + P), f)
    small[:, 0:CH] = SCALE * (np.arange(P)[:, None] // HD == np.arange(CH)[None, :])
    small[:, 8:16] = np.arange(E)
    small[:, 16:16 + E * NJ] = np.tile(np.arange(NJ) * BLK, E)
    small[:, 16 + E * NJ:16 + E * NJ + NBLK] = np.arange(NBLK)
    small[:, 16 + E * NJ + NBLK:] = np.arange(P)[:, None] < np.arange(P)[None, :]
    tri = np.zeros((P, 4, P), f)
    k, q = np.arange(P)[:, None], np.arange(P)[None, :]
    tri[:, 0] = np.where(q >= k, 0.0, HIDE)
    tri[:, 1] = np.where((q >= k) & (q - k < WIN), 0.0, HIDE)
    tri[:, 2] = np.where(P + q - k < WIN, 0.0, HIDE)
    tri[:, 3] = np.eye(P)
    return rope, tri, small


_OUT = (NB, S, D)


def kernel(**inputs):
    import numpy as _np
    import concourse.bacc as _bacc
    from concourse import mybir as _mybir
    from concourse.bass_utils import run_bass_kernel_spmd as _run

    a = {k.replace("L0_", ""): _np.asarray(v) for k, v in inputs.items()}
    rope, tri, small = constants()
    column = lambda v: v.reshape(DC, P).T
    chunked = lambda w: w.reshape(E, -1, P, w.shape[-1]).transpose(0, 2, 1, 3).reshape(E, P, THIRD)
    gate, up = (chunked(a[f"ffn_{n}_w"].transpose(0, 2, 1)) for n in ("gate", "up"))
    lower = chunked(a["ffn_down_w"].transpose(0, 2, 1))
    arrays = {
        "x": a["x"].reshape(T, D),
        "wq0": a["attn_g_wq"], "kvdT": a["attn_g_kv_down"].T,
        "kvup": _np.concatenate([a["attn_g_k_up"], a["attn_g_v_up"]], 1), "wo0": a["attn_g_wo"],
        "wq1": a["attn_l_wq"], "wk1": a["attn_l_wk"], "wv1": a["attn_l_wv"], "wo1": a["attn_l_wo"],
        "n1": column(a["attn_norm1_w"]), "n2": column(a["attn_norm2_w"]), "rope": rope, "tri": tri,
        "ctxT": a["ctx_1024"].reshape(NB * CL, D).T, "mask": a["mask_1x1xSxS2_ff0"].reshape(S, CL),
        "xwq": a["xattn_Wq"], "xwk": a["xattn_Wk"], "xwv": a["xattn_Wv"], "xwo": a["xattn_Wo"],
        "xbq": column(a["xattn_bq"]), "xbk": column(a["xattn_bk"]),
        "xbv": a["xattn_bv"].reshape(1, D), "xbo": a["xattn_bo"].reshape(1, D),
        "router": a["ffn_router_w"].T, "experts": _np.concatenate([gate, up, lower], 2), "small": small,
    }
    arrays = {f"in_{n}": _np.ascontiguousarray(v) for n, v in arrays.items()}
    nc = _bacc.Bacc("TRN2", target_bir_lowering=False, num_devices=1)
    args = [nc.dram_tensor(n, v.shape, _mybir.dt.from_np(v.dtype), kind="ExternalInput").ap() for n, v in arrays.items()]
    args.append(nc.dram_tensor("out_0", (T, D), F32, kind="ExternalOutput").ap())
    build_decoder(nc, *args)
    r = _run(nc, [arrays], core_ids=[0])
    return r.results[0]["out_0"].reshape(_OUT)
```

```python
from contextlib import ExitStack

import numpy as np
import concourse.bass as bass
from concourse import mybir

P = 128
NB, S, D = 2, 1024, 256
T = NB * S
NT = T // P
TB = S // P
DC = D // P
H, G, HD = 16, 4, 16
HG = H // G
LAT = 64
WIN = 64
U = 4
NI = NT // U
XB = U // 2
QKV = (H + 2 * G) * HD
QKH = H + G
VW = 3 * HD + 1
BG = NB * G
EPS_RMS, EPS_LN = 1e-6, 1e-5
SCALE = float(HD) ** -0.5
HIDE = -30000.0

F32, F32R = mybir.dt.float32, mybir.dt.float32r
BF16, F16 = mybir.dt.bfloat16, mybir.dt.float16
ALU = mybir.AluOpType
ACT = mybir.ActivationFunctionType
AX = mybir.AxisListType
ds = bass.ds

GLOBAL_UNITS = [(q, k) for q in range(TB) for k in range(q + 1)]
GLOBAL_STEPS = [[(q, k, P) for q, k in GLOBAL_UNITS[n:n + 2]] for n in range(0, len(GLOBAL_UNITS), 2)]
LOCAL_STEPS = [[(q, q, P)] + [(q, q - 1, WIN)] * (q > 0) for q in range(TB)]
STEPS = [GLOBAL_STEPS, LOCAL_STEPS]
DONE = [[max(n for n, step in enumerate(steps) if step[-1][0] >= q and step[0][0] <= q) for q in range(TB)]
        for steps in STEPS]
BASE = [0, BG * len(GLOBAL_STEPS)]
BANKS = 3
SLOTS = 4
RUNS = [[SLOTS, SLOTS, SLOTS, 3, 3], [SLOTS, SLOTS]]
SLOT_OF = [[m for run in runs for m in range(run)] for runs in RUNS]
BANK_OF = [[n % BANKS for n in range(len(steps))] for steps in STEPS]
since = lambda of: [next(d for d in range(1, 17) if of[(n - d) % len(of)] == of[n]) for n in range(len(of))]
BANK_REUSE, SLOT_REUSE = [since(of) for of in BANK_OF], [since(of) for of in SLOT_OF]
CL = 77
CH = H // 2
CS = 2 * U
CLS = 4
LATE = 3
LATER = 4
FMAX = float(np.finfo(np.float32).max)
E, FI = 8, 1024
FC = FI // P
FP = FC // 2
BLK = 256
BA = BLK // P
NBLK = (2 * T + E * (BLK - 1)) // BLK
NJ = T // BLK
NR = BA * NBLK
AT_BLOCK = 2 * CH + E * NJ
AT_BEFORE = AT_BLOCK + NBLK
AT_COUNT = AT_BEFORE + P
AT_SPARE = AT_COUNT + P
AT_ROW = AT_SPARE + NR
THIRD = DC * FI
START = CS + 1


def build_decoder(nc, x, wq0, kvdT, kvup, wo0, wq1, wk1, wv1, wo1, n1, n2, rope, tri,
                  ctxT, mask, xwq, xwk, xwv, xwo, xbq, xbk, xbv, xbo, router, experts, small, out):
    ctx = ExitStack()
    with ctx:
        def sb(name, shape, dt=F32):
            return ctx.enter_context(nc.sbuf_tensor(name, shape, dt))

        def sem(name):
            return ctx.enter_context(nc.semaphore(name))

        X = sb("X", [P, NT, D])
        tri_sb = sb("tri_sb", [P, 4, P])
        identF = tri_sb[:, 3, :]
        eps = sb("eps", [P, 2])
        root = sb("root", [P, NT])
        rstd = sb("rstd", [P, NT])
        shift = sb("shift", [P, NT])

        small_sb = sb("small_sb", [P, AT_ROW + 1])
        ST = sb("ST", [P, NT, 6])
        MV = sb("MV", [P, NT, 2])
        EB = sb("EB", [P, NBLK], mybir.dt.int32)
        SOURCE = sb("SOURCE", [P, NR], mybir.dt.uint32)
        TARGET = sb("TARGET", [P, NR], mybir.dt.uint32)
        NOW = sb("NOW", [P, 2, 2, BA], mybir.dt.uint32)
        CO = sb("CO", [P, 2, NT])
        ONES = sb("ONES", [P, P])
        middle = ExitStack()

        def mb(name, shape, dt=F32):
            return middle.enter_context(nc.sbuf_tensor(name, shape, dt))

        ssq = mb("ssq", [P, NT])
        XN = mb("XN", [P, U, D])
        XT = mb("XT", [P, U, DC, P])
        WX = mb("WX", [P, 4, DC, D])
        ctx_sb = mb("ctx_sb", [P, DC, NB * CL])
        xb = mb("xb", [P, 2, DC])
        BV = mb("BV", [CL, D])
        BO = mb("BO", [P, D])
        KZ = mb("KZ", [P, NB, DC, CH, CL])
        VX = mb("VX", [CL, NB * H, VW], BF16)
        MF = mb("MF", [P, NT, CL])
        RW = mb("RW", [P, DC, E])
        LG = mb("LG", [P, NT, E])
        early = ExitStack()

        def eb(name, shape, dt=F32):
            return early.enter_context(nc.sbuf_tensor(name, shape, dt))

        OA = eb("OA", [P, NT, D])
        W = [eb(f"W{l}", [P, DC, QKV]) for l in range(2)]
        WO = [eb(f"WO{l}", [P, DC, D]) for l in range(2)]
        kvd_sb = eb("kvd_sb", [LAT, D])
        kvup_sb = eb("kvup_sb", [LAT, 2 * G * HD])
        nw = eb("nw", [P, 2, DC])
        rope_sb = eb("rope_sb", [P, 2, 2, NT, HD])
        identH = eb("identH", [P, P], F16)
        identB = eb("identB", [P, P], BF16)
        hide = eb("hide", [P, 3, HG, P], BF16)
        KB = eb("KB", [P, DC, NB * CL])
        RS = eb("RS", [P, 4, U, QKH * HD])
        RAW, SQ = RS[:, 0], RS[:, 1]
        R1, R2 = RS[:, 2], RS[:, 3]
        ss = eb("ss", [P, U * QKH])
        sr = eb("sr", [P, U * QKH])
        rn = eb("rn", [P, U * QKH])
        RQ = eb("RQ", [P, U * H, HD])
        RK = eb("RK", [P, U * G, HD])
        QS = eb("QS", [P, U * H, 4, HD], F16)
        KS = eb("KS", [P, U * G, 8, HD], F16)
        QT = eb("QT", [P, H // 2, T], F16)
        KT = eb("KT", [P, 2 * G, T], F16)
        VA = eb("VA", [P, U * G, HD])
        VL = eb("VL", [P, U * G, HD])
        VS = eb("VS", [P, NT * G, VW], BF16)
        PF = RS[:].rearrange("p a u n -> p (a u n)")[:, 0:SLOTS * 1024].rearrange("p (s n) -> p s n", s=SLOTS)
        PL = QS[:].rearrange("p n c d -> p (n c d)")[:, 0:SLOTS * 1024].rearrange("p (s n) -> p s n", s=SLOTS)
        OS = eb("OS", [P, 2, HG, HD])
        OR = eb("OR", [P, 2, HG, 1])
        early.close()
        cross = ExitStack()

        def cb(name, shape, dt=F32):
            return cross.enter_context(nc.sbuf_tensor(name, shape, dt))

        XS = cb("XS", [P, 2, U, D])
        XM = cb("XM", [P, 2, DC, U * P])
        QC = cb("QC", [P, DC, T])
        QG = cb("QG", [P, DC, U * P])
        CLG = cb("CLG", [P, CLS, CH, CL])
        CMX = cb("CMX", [P, 2, CH, 1])
        CPX = cb("CPX", [P, 2, CH, CL])
        CPT = cb("CPT", [CL, 2, CH, P])
        CPL = cb("CPL", [CL, 2, CH, P], F16)
        CA = cb("CA", [P, 2, CH, HD])
        CR = cb("CR", [P, 2, CH, 1])
        OX = cb("OX", [P, NT, D])
        rt = {n: cb(f"rt_{n}", [P, NT, E]) for n in
              ("eq1", "code1", "one1", "left", "eq2", "code2", "one2", "w1", "w2", "pfa", "pfb", "slot", "t1", "t2")}
        rc = {n: cb(f"rc_{n}", [P, NT]) for n in ("m1", "i1", "m2", "i2", "d", "e", "den", "r", "p2")}
        re = {n: cb(f"re_{n}", [P, E]) for n in ("cnt", "sumw", "nb", "bba", "bbb", "end", "one", "inv", "mean")}
        SW = cb("SW", [P, NT, 2 * E])
        TOT = cb("TOT", [P, NT, 2 * E])
        GTJ = cb("GTJ", [P, E, NJ])
        LEB = cb("LEB", [P, NBLK, E])
        EBF = cb("EBF", [P, NBLK])
        POSF = cb("POSF", [P, 2, NT])
        SLOT = cb("SLOT", [P, 2, NT], mybir.dt.uint32)
        RUN = cb("RUN", [P, 2, 2, NT], mybir.dt.uint32)
        RUNF = cb("RUNF", [P, 2, 2 * NT])
        ISRUN = cb("ISRUN", [P, 2 * NT, NR], F16)
        WHO = cb("WHO", [P, 2 * NT, 2, NR], F16)
        PLACE = cb("PLACE", [P, 2 * NT, P], F16)
        inv = {n: cb(f"inv_{n}", [P, NR]) for n in ("of", "none", "spare", "token", "second")}
        cross.close()
        middle.close()
        RAWW = sb("RAWW", [P, 3, THIRD])
        WH = [sb(f"WH{a}", [P, 3, THIRD], F32R) for a in range(2)]
        WL = [sb(f"WL{a}", [P, 3, THIRD], F32R) for a in range(2)]
        XR = sb("XR", [P, 2, BA, D])
        XH = [sb(f"XH{a}", [P, DC, BLK], F32R) for a in range(2)]
        XL = [sb(f"XL{a}", [P, DC, BLK], F32R) for a in range(2)]
        SG = sb("SG", [P, 2, 2, BLK])
        HF = sb("HF", [P, 2, 2, BLK])
        HH = [sb(f"HH{a}", [P, FC, BLK], F32R) for a in range(2)]
        HL = [sb(f"HL{a}", [P, FC, BLK], F32R) for a in range(2)]
        EO = sb("EO", [P, 2, BA, D])
        YB = RAWW[:].rearrange("p w n -> p (w n)")[:, 0:2 * 2 * U * D].rearrange("p (s k u d) -> p s k u d", s=2, k=2, u=U)
        XD = nc.dram_tensor("XD", [T, D], F32).ap()
        YT = nc.dram_tensor("YT", [2 * T + NBLK * BLK, D], F32).ap()

        PS = ctx.enter_context(nc.psum_tensor("PS", [P, 8, 512], F32))
        ps_x = PS[:, 0:2, :].rearrange("p a (u n) -> p (a u) n", u=2)
        ps_p = PS[:, 2:6, :]
        ps_q = [PS[:, a, :].bitcast(F16).rearrange("p (h n) -> p h n", h=H // 2) for a in (0, 6)]
        ps_k = [PS[:, a, 0:256].bitcast(F16).rearrange("p (g n) -> p g n", g=G) for a in (1, 7)]
        ps_s = PS[:, 0:2 * BANKS, :].rearrange("p (a b) n -> p a (b n)", a=BANKS)
        ps_o = PS[:, 6:8, 0:HG * VW].rearrange("p a (h v) -> p a h v", h=HG)

        s_loadx = sem("s_loadx")
        s_loadw = sem("s_loadw")
        s_fuse = sem("s_fuse")
        s_weights = sem("s_weights")
        s_const = sem("s_const")
        s_square = sem("s_square")
        s_ssq = sem("s_ssq")
        s_root = sem("s_root")
        s_rstd = sem("s_rstd")
        s_xn = sem("s_xn")
        s_xt = sem("s_xt")
        s_xte = sem("s_xte")
        s_proj = sem("s_proj")
        s_raw = sem("s_raw")
        s_rot2 = sem("s_rot2")
        s_dve = sem("s_dve")
        s_hss = sem("s_hss")
        s_hroot = sem("s_hroot")
        s_split = sem("s_split")
        s_rest = sem("s_rest")
        s_stack = sem("s_stack")
        s_dup = sem("s_dup")
        s_vs = sem("s_vs")
        s_qkt = sem("s_qkt")
        s_qe = sem("s_qe")
        s_ke = sem("s_ke")
        s_score = sem("s_score")
        s_exp = sem("s_exp")
        s_low = sem("s_low")
        s_lowp = sem("s_lowp")
        s_pv = sem("s_pv")
        s_osum = sem("s_osum")
        s_on = sem("s_on")
        s_oproj = sem("s_oproj")
        s_res = sem("s_res")
        s_x0 = [sem(f"s_x0{a}") for a in range(2)]
        s_cload = sem("s_cload")
        s_ckv = sem("s_ckv")
        s_ckb = sem("s_ckb")
        s_ckz = sem("s_ckz")
        s_bn = sem("s_bn")
        s_stat = sem("s_stat")
        s_mv = sem("s_mv")
        s_xb = sem("s_xb")
        s_cq = sem("s_cq")
        s_cqe = sem("s_cqe")
        s_qg = sem("s_qg")
        s_ostage = sem("s_ostage")
        s_cs = sem("s_cs")
        s_clog = sem("s_clog")
        s_cmax = sem("s_cmax")
        s_csub = sem("s_csub")
        s_cexp = sem("s_cexp")
        s_cpt = sem("s_cpt")
        s_cpe = sem("s_cpe")
        s_cpl = sem("s_cpl")
        s_cpv = sem("s_cpv")
        s_crec = sem("s_crec")
        s_con = sem("s_con")
        s_cwo = sem("s_cwo")
        s_cres = sem("s_cres")
        s_keep = sem("s_keep")
        s_rl = sem("s_rl")
        s_rle = sem("s_rle")
        s_route = sem("s_route")
        s_gap = sem("s_gap")
        s_tot = sem("s_tot")
        s_xd = sem("s_xd")
        s_map = sem("s_map")
        s_now = sem("s_now")
        s_issue = sem("s_issue")
        s_wl = [sem(f"s_wl{w}") for w in range(3)]
        s_wh = sem("s_wh")
        s_wlo = sem("s_wlo")
        s_xbl = [sem(f"s_xbl{a}") for a in range(2)]
        s_bt = sem("s_bt")
        s_bh = sem("s_bh")
        s_bl = sem("s_bl")
        s_gu = sem("s_gu")
        s_silu = sem("s_silu")
        s_hm = sem("s_hm")
        s_hh = sem("s_hh")
        s_hl = sem("s_hl")
        s_down = sem("s_down")
        s_eo = sem("s_eo")
        s_yg = sem("s_yg")
        s_eof = sem("s_eof")
        s_gat = [sem(f"s_gat{a}") for a in range(2)]
        s_mix = sem("s_mix")
        s_shift = sem("s_shift")
        s_fin = sem("s_fin")
        s_out = sem("s_out")

        xv = x.rearrange("(t p) d -> p t d", p=P)
        ov = out.rearrange("(t p) d -> p t d", p=P)
        NLOAD = 12 * 16
        NCLOAD = 13 * 16
        NSHARES = 19
        NEXPERT = 37
        NSLOT = 53
        NROUTE = NSLOT + 16
        KZf = KZ[:].rearrange("p b c h k -> p (b c h k)")
        VXf = VX[:].rearrange("k n v -> k (n v)")
        VC, VC2 = (OA[0:CL, a:a + 2, :].rearrange("k b (h d) -> k (b h) d", h=H) for a in (0, 2))
        own = small_sb[:, 0:CH]
        expert_no = small_sb[:, 8:16]
        block_rows = small_sb[:, 2 * CH:AT_BLOCK]
        block_no = small_sb[:, AT_BLOCK:AT_BEFORE]
        counting = small_sb[:, AT_COUNT:AT_SPARE]
        spare = small_sb[:, AT_SPARE:AT_ROW]
        row_no = small_sb[:, AT_ROW:AT_ROW + 1]
        before = small_sb[:, AT_BEFORE:AT_COUNT]
        NDVE = 5
        NVS = 4
        KTf = KT[:].rearrange("p a t -> p (a t)")
        VSf = VS[:].rearrange("p n v -> p (n v)")
        KS2 = KS[:].rearrange("p n a d -> p n (a d)")
        QS2 = QS[:].rearrange("p (n e) a d -> p n (e a d)", e=2)
        block = ctx.enter_context(nc.Block())

        @block.sync
        def _(sp):
            for i in range(NI):
                sp.dma_start(X[:, U * i:U * i + U, :], xv[:, U * i:U * i + U, :]).then_inc(s_loadx, 16)
            for l, wq in enumerate((wq0, wq1)):
                sp.dma_start(W[l][:, :, 0:D], wq.rearrange("(c p) n -> p c n", p=P)).then_inc(s_loadw, 16)
            sp.dma_start(W[1][:, :, D:D + 64], wk1.rearrange("(c p) n -> p c n", p=P)).then_inc(s_loadw, 16)
            sp.dma_start(W[1][:, :, D + 64:D + 128], wv1.rearrange("(c p) n -> p c n", p=P)).then_inc(s_loadw, 16)
            sp.dma_start(kvd_sb[:], kvdT).then_inc(s_loadw, 16)
            sp.dma_start(kvup_sb[:], kvup).then_inc(s_loadw, 16)
            sp.dma_start(nw[:, 0, :], n1).then_inc(s_loadw, 16)
            sp.dma_start(nw[:, 1, :], n2).then_inc(s_loadw, 16)
            sp.dma_start(rope_sb[:], rope).then_inc(s_loadw, 16)
            sp.dma_start(tri_sb[:], tri).then_inc(s_loadw, 16)
            for l, wo in enumerate((wo0, wo1)):
                sp.dma_start(WO[l][:], wo.rearrange("(c p) n -> p c n", p=P)).then_inc(s_loadw, 16)
            for n, w in enumerate((xwq, xwk, xwv, xwo)):
                sp.dma_start(WX[:, n], w.rearrange("(c p) n -> p c n", p=P)).then_inc(s_cload, 16)
            sp.dma_start(ctx_sb[:], ctxT.rearrange("(c p) n -> p c n", p=P)).then_inc(s_cload, 16)
            sp.dma_start(xb[:, 0, :], xbq).then_inc(s_cload, 16)
            sp.dma_start(xb[:, 1, :], xbk).then_inc(s_cload, 16)
            sp.dma_start(BV[:], xbv.to_broadcast([CL, D])).then_inc(s_cload, 16)
            sp.dma_start(BO[:], xbo.to_broadcast([P, D])).then_inc(s_cload, 16)
            for b in range(NB):
                sp.dma_start(MF[:, b * TB:(b + 1) * TB, :], mask.rearrange("(t p) k -> p t k", p=P)).then_inc(s_cload, 16)
            sp.dma_start(small_sb[:], small).then_inc(s_cload, 16)
            sp.dma_start(RW[:], router.rearrange("(c p) e -> p c e", p=P)).then_inc(s_cload, 16)
            for i in range(NI):
                sp.wait_ge(s_xn, START + 3 * NI + i + 1)
                if i >= 2:
                    sp.wait_ge(s_bn, START + i - 1)
                sp.dma_start(OA[:, U * i:U * i + U, :], xv[:, U * i:U * i + U, :]).then_inc(s_x0[i % 2], 16)

            def load_weights(m):
                e = sp.value_load(EB[0:1, ds(m, 1)], min_val=0, max_val=E - 1)
                for w in range(3):
                    sp.wait_ge(s_wlo, START + m * 3 + w - 2)
                    sp.dma_start(RAWW[:, w, :], experts[ds(e, 1), :, w * THIRD:(w + 1) * THIRD]
                                 .rearrange("a p n -> p (a n)")).then_inc(s_wl[w], 16)

            for i in range(NI):
                sp.wait_ge(s_keep, START + i + 1)
                sp.dma_start(XD[i * U * P:(i + 1) * U * P, :].rearrange("(u p) d -> p u d", p=P),
                             X[:, U * i:U * i + U, :]).then_inc(s_xd, 16)
            sp.wait_ge(s_route, NEXPERT)
            with sp.Fori(0, NBLK) as m:
                load_weights(m)
            sp.wait_ge(s_yg, 16 * BA * NBLK)
            for i in range(NI):
                if i >= 2:
                    sp.wait_ge(s_stat, 2 * NI + i - 1)
                for k in range(2):
                    rows = YT[(k * NI + i) * U * P:(k * NI + i + 1) * U * P, :].rearrange("(u p) d -> p u d", p=P)
                    sp.dma_start(YB[:, i % 2, k], rows).then_inc(s_gat[i % 2], 16)
            for i in range(NI):
                sp.wait_ge(s_fin, i + 1)
                sp.dma_start(ov[:, U * i:U * i + U, :], X[:, U * i:U * i + U, :]).then_inc(s_out, 16)
            sp.wait_ge(s_out, 16 * NI)

        @block.gpsimd
        def _(pool):
            pool.sem_inc(s_rot2, START)
            pool.sem_inc(s_stack, START)
            pool.sem_inc(s_vs, START)
            pool.sem_inc(s_lowp, START)
            pool.memset(eps[:, 0:1], EPS_RMS)
            pool.memset(eps[:, 1:2], EPS_LN)
            pool.memset(VS[:, :, 3 * HD:VW], 1.0).then_inc(s_const, 1)
            pool.memset(ONES[:], 1.0)
            pool.wait_ge(s_loadw, NLOAD)
            pool.tensor_copy(identH[:], identF)
            pool.tensor_copy(identB[:], identF)
            pool.tensor_copy(hide[:], tri_sb[:, 0:3, :].unsqueeze(2).to_broadcast([P, 3, HG, P])).then_inc(s_const, 1)

            def rotate_and_stack(l, i):
                n = l * NI + i
                pool.wait_ge(s_raw, START + n * U + U)
                group = ds(i * (U * G), U * G)
                part = [VS[:, group, c * HD:(c + 1) * HD] for c in range(3)]
                pool.tensor_copy(part[0], VA[:]).then_inc(s_vs, 1)
                pool.wait_ge(s_vs, START + n * NVS + 1)
                pool.wait_ge(s_dve, START + (n - 1) * NDVE + 2)
                rv = RAW.rearrange("p u (h d e) -> p u h d e", h=QKH, e=2)
                r2 = R2.rearrange("p u (h d e) -> p u h d e", h=QKH, e=2)
                sv = rope_sb[:, l, 1, ds(i * U, U), :].rearrange("p t (d e) -> p t d e", e=2)
                for e in range(2):
                    last = pool.tensor_tensor(
                        r2[:, :, :, :, e], rv[:, :, :, :, 1 - e],
                        sv[:, :, :, e].unsqueeze(2).to_broadcast([P, U, QKH, HD // 2]), ALU.mult)
                last.then_inc(s_rot2, 1)
                pool.tensor_tensor(VL[:], VA[:], part[0], ALU.subtract).then_inc(s_vs, 1)
                pool.wait_ge(s_vs, START + n * NVS + 2)
                pool.tensor_copy(part[1], VL[:]).then_inc(s_vs, 1)
                pool.wait_ge(s_vs, START + n * NVS + 3)
                pool.tensor_tensor(part[2], VL[:], part[1], ALU.subtract).then_inc(s_vs, 1)
                pool.wait_ge(s_dve, START + n * NDVE + 5)
                pool.tensor_tensor(QS[:, :, 3, :], RQ[:], QS[:, :, 0, :], ALU.subtract).then_inc(s_stack, 1)

            def low_parts(l, it):
                for n, step in enumerate(STEPS[l]):
                    at = BASE[l] + it * len(STEPS[l]) + n
                    cut, cols = low_share(step)
                    pool.wait_ge(s_exp, START + at + 1)
                    pool.wait_ge(s_pv, START + at - SLOT_REUSE[l][n] + 1)
                    pf = PF[:, SLOT_OF[l][n], cut:cols]
                    pool.tensor_tensor(PL[:, SLOT_OF[l][n], cut:cols], pf, high_part(pf), ALU.subtract).then_inc(s_lowp, 1)

            for l in range(2):
                with pool.Fori(0, NI) as i:
                    rotate_and_stack(l, i)
                with pool.Fori(0, BG) as it:
                    low_parts(l, it)
            pool.sem_inc(s_xb, START)
            with pool.Fori(0, NI // 2) as j:
                for a in range(2):
                    i = j * 2 + a
                    pool.wait_ge(s_xn, START + 4 * NI + i + 1)
                    pool.tensor_tensor(X[:, ds(i * U, U), :], XS[:, a], BO[:].unsqueeze(1).to_broadcast([P, U, D]),
                                       ALU.add).then_inc(s_xb, 1)
            pool.sem_inc(s_cpl, START)
            with pool.Fori(0, NI) as i:
                for m in range(CS):
                    at, a = i * CS + m, m % 2
                    pool.wait_ge(s_cpe, START + at + 1)
                    pool.wait_ge(s_cpv, START + at - 1)
                    pool.tensor_tensor(CPL[:, a].rearrange("k h n -> k (h n)"), CPT[:, a].rearrange("k h n -> k (h n)"),
                                       high_part(CPT[:, a].rearrange("k h n -> k (h n)")), ALU.subtract).then_inc(s_cpl, 1)
            pool.sem_inc(s_eof, START)
            pool.sem_inc(s_now, START)
            pool.wait_ge(s_route, NROUTE)
            pool.wait_ge(s_xd, 16 * NI)

            def gather_block(m, par, n):
                pool.wait_ge(s_bt, START + m - 1)
                pool.tensor_copy(NOW[:, 0, par], SOURCE[:, ds(m * BA, BA)]).then_inc(s_now, 1)
                pool.wait_ge(s_now, START + n + 1)
                pool.sem_inc(s_issue, 1)
                for a in range(BA):
                    pool.indirect_dma_start(XR[:, par, a, :], None, XD[:, :],
                                            bass.IndirectOffsetOnAxis(NOW[:, 0, par, a:a + 1], 0)).then_inc(s_xbl[par], 16)

            def scatter_block(m, par, n):
                pool.wait_ge(s_eo, START + m + 1)
                pool.tensor_copy(NOW[:, 1, par], TARGET[:, ds(m * BA, BA)]).then_inc(s_now, 1)
                pool.wait_ge(s_now, START + n + 1)
                pool.sem_inc(s_issue, 1)
                for a in range(BA):
                    pool.indirect_dma_start(YT[:, :], bass.IndirectOffsetOnAxis(NOW[:, 1, par, a:a + 1], 0),
                                            EO[:, par, a, :], None).then_inc(s_yg, 16)

            def scattered(m):
                pool.wait_ge(s_yg, 16 * BA * (m + 1))
                pool.sem_inc(s_eof, 1)

            for m in range(3):
                gather_block(m, m % 2, m)
            with pool.Fori(0, (NBLK - 3) // 2) as j:
                for par in range(2):
                    m = j * 2 + par
                    gather_block(m + 3, 1 - par, 2 * m + 3)
                    scatter_block(m, par, 2 * m + 4)
                    scattered(m)
            for m in range(NBLK - 3, NBLK):
                scatter_block(m, m % 2, NBLK + m)
                scattered(m)

        @block.scalar
        def _(act):
            act.sem_inc(s_square, START)
            act.sem_inc(s_root, START)
            act.sem_inc(s_xte, START)
            act.sem_inc(s_raw, START)
            act.sem_inc(s_hroot, START)
            act.sem_inc(s_keep, START)
            act.sem_inc(s_dup, START)
            act.sem_inc(s_qg, START)
            act.sem_inc(s_ostage, START)
            act.sem_inc(s_qe, START)
            act.sem_inc(s_exp, START)
            for s in (s_cqe, s_cexp, s_cpe, s_rle, s_wh, s_bh, s_silu, s_hh, s_eo):
                act.sem_inc(s, START)

            def squares(n, i):
                act.wait_ge(s_ssq, START + n - 1)
                act.activation(RS[:, ds(i % 2, 1)].rearrange("p a u n -> p (a u n)")[:, 0:U * D],
                               X[:, ds(i * U, U), :].rearrange("p u n -> p (u n)"), ACT.Square).then_inc(s_square, 1)

            def stage(l, i):
                act.wait_ge(s_xt, START + ((2 * l + 1) * NI + i) * XB)
                act.copy(XN[:], OA[:, ds(i * U, U), :]).then_inc(s_xn, 1)

            def rms(l, i):
                act.wait_ge(s_ssq, START + l * NI + i + 1)
                act.activation(root[:, ds(i * U, U)], ssq[:, ds(i * U, U)], ACT.Sqrt, bias=eps[:, 0:1],
                               scale=1.0 / D).then_inc(s_root, 1)

            def squares_of_result(i):
                act.wait_ge(s_res, START + i + 1)
                squares(NI + i, i)

            def tiles_out(k, i):
                for v in range(XB):
                    act.wait_ge(s_xt, START + (k * NI + i) * XB + v + 1)
                    act.copy(XT[:, 2 * v:2 * v + 2].rearrange("p u c n -> p (u c n)"), PS[:, v, :]).then_inc(s_xte, 1)

            def project(l, i):
                n = l * NI + i
                for u in range(U):
                    act.wait_ge(s_proj, START + n * U + u + 1)
                    if u == 0:
                        act.wait_ge(s_rot2, START + n)
                        act.wait_ge(s_hss, START + n)
                        act.wait_ge(s_vs, START + n * NVS)
                    act.copy(RAW[:, u, :], ps_p[:, u, 0:QKH * HD])
                    act.copy(VA[:, u * G:(u + 1) * G, :], ps_p[:, u, QKH * HD:QKV])
                    act.activation(SQ[:, u, :], ps_p[:, u, 0:QKH * HD], ACT.Square).then_inc(s_raw, 1)

            def head_roots(l, i):
                act.wait_ge(s_hss, START + l * NI + i + 1)
                act.activation(sr[:], ss[:], ACT.Sqrt, bias=eps[:, 0:1], scale=1.0 / HD).then_inc(s_hroot, 1)

            def copies(l, i):
                act.wait_ge(s_dve, START + (l * NI + i) * NDVE + 5)
                act.copy(QS[:, :, 1, :], QS[:, :, 0, :]).then_inc(s_dup, 1)

            def stacks_out(l, i):
                for u in range(U):
                    act.wait_ge(s_qkt, START + (l * NI + i) * U + u + 1)
                    act.copy(QT[:, :, ds((i * U + u) * P, P)], ps_q[u % 2]).then_inc(s_qe, 1)

            def group_step(l, i, stacks=True, before=True, this=True, first=False):
                if stacks:
                    stacks_out(l, i - 2)
                if before:
                    head_roots(l, i - 1)
                if this:
                    tiles_out(2 * l, i)
                if l == 1 and first:
                    rms(1, NI - 1)
                if before:
                    copies(l, i - 1)
                if this:
                    project(l, i)

            def exponentials(l, it):
                for n, step in enumerate(STEPS[l]):
                    at = BASE[l] + it * len(STEPS[l]) + n
                    cols = sum(HG * w for _, _, w in step)
                    act.wait_ge(s_score, START + at + 1)
                    act.wait_ge(s_pv, START + at - SLOT_REUSE[l][n] + 1)
                    act.activation(PF[:, SLOT_OF[l][n], 0:cols], ps_s[:, BANK_OF[l][n], 0:cols], ACT.Exp, scale=SCALE).then_inc(s_exp, 1)

            act.wait_ge(s_const, 1)
            act.wait_ge(s_loadx, 16 * NI)
            nc.scalar.preload_act_table(ACT.Sqrt)
            squares(0, 0)
            for i in range(1, NI):
                squares(i, i)
                rms(0, i - 1)
            rms(0, NI - 1)
            for l in range(2):
                group_step(l, 0, stacks=False, before=False, first=True)
                group_step(l, 1, stacks=False)
                with act.Fori(2, NI) as i:
                    group_step(l, i)
                group_step(l, NI, this=False)
                nc.scalar.preload_act_table(ACT.Exp)
                group_step(l, NI + 1, this=False, before=False)
                with act.Fori(0, BG) as it:
                    exponentials(l, it)
                nc.scalar.preload_act_table(ACT.Sqrt)
                act.wait_ge(s_on, START + (l + 1) * BG * TB)
                stage(l, 0)
                tiles_out(2 * l + 1, 0)
                stage(l, 1)
                with act.Fori(1, NI - 1) as i:
                    tiles_out(2 * l + 1, i)
                    stage(l, i + 1)
                    if l == 0:
                        squares_of_result(i - 1)
                        rms(1, i - 1)
                tiles_out(2 * l + 1, NI - 1)
                if l == 0:
                    squares_of_result(NI - 2)
                    rms(1, NI - 2)
                    squares_of_result(NI - 1)

            def roots(n, i):
                act.wait_ge(s_mv, n * NI + i + 1)
                act.activation(root[:, i * U:i * U + U], MV[:, i * U:i * U + U, 1], ACT.Sqrt, bias=eps[:, 1:2]).then_inc(s_root, 1)

            for i in range(NI - 1):
                roots(0, i)
            for i in range(NI):
                a = i % 2
                act.wait_ge(s_cq, START + (i - 1) * DC)
                act.wait_ge(s_bn, START + NI - 1 + min(i, 1))
                for v in range(XB):
                    act.wait_ge(s_xt, START + (4 * NI + i) * XB + v + 1)
                    act.copy(XM[:, a].rearrange("p c (u n) -> p u c n", u=U)[:, 2 * v:2 * v + 2],
                             PS[:, v, :].rearrange("p (u c n) -> p u c n", u=2, c=DC)).then_inc(s_xte, 1)
                if i == 0:
                    roots(0, NI - 1)
                    nc.scalar.preload_act_table(ACT.Exp)
                for o in range(DC):
                    act.wait_ge(s_cq, START + i * DC + o + 1)
                    act.activation(QC[:, o, i * U * P:(i + 1) * U * P], PS[:, 2 + o, :], ACT.Identity,
                                   bias=xb[:, 0, o:o + 1]).then_inc(s_cqe, 1)

            def transposed_out(at, a):
                act.wait_ge(s_cpt, START + at + 1)
                act.wait_ge(s_cpv, START + at - 1)
                act.copy(CPT[:, a].rearrange("k h n -> k (h n)"), PS[0:CL, 0:2, :].rearrange("k a n -> k (a n)")).then_inc(s_cpe, 1)

            def queries(i, u):
                act.wait_ge(s_cs, START + (i - 1) * CS + (u + 1) * DC)
                act.copy(QG[:, :, u * P:(u + 1) * P], QC[:, :, ds((i * U + u) * P, P)]).then_inc(s_qg, 1)

            def outputs(i, a):
                act.copy(XS[:, ds(a, 1)].rearrange("p a u d -> p (a u) d"), OX[:, ds(i * U, U), :]).then_inc(s_ostage, 1)

            def cross_group(i, first=False, last=False):
                for m in range(CS):
                    at = i * CS + m
                    if m == LATER + 1 and not (first or last):
                        act.wait_ge(s_con, START + i * CS)
                        outputs(i - 1, (i - 1) % 2)
                    if m % DC == 0 and m >= DC and not last:
                        queries(i + 1, m // DC - 1)
                    if not (first and m < LATE - 1):
                        transposed_out(at - LATE + 1, (m - LATE + 1) % 2)
                    act.wait_ge(s_csub, START + at + 1)
                    act.wait_ge(s_cpt, START + at - 1)
                    act.activation(CPX[:, m % 2], CLG[:, m % CLS], ACT.Exp).then_inc(s_cexp, 1)

            for u in range(U):
                queries(0, u)
            cross_group(0, first=True)
            queries(1, U - 1)
            with act.Fori(1, NI - 1) as i:
                cross_group(i)
                queries(i + 1, U - 1)
            cross_group(NI - 1, last=True)
            for m in range(LATE - 1):
                transposed_out(NI * CS - LATE + 1 + m, (m - LATE + 1) % 2)
            nc.scalar.preload_act_table(ACT.Sqrt)
            act.wait_ge(s_con, START + NI * CS)
            for i in range(NI):
                tiles_out(5, i)
                if i + 2 < NI:
                    outputs(i + 2, i % 2)

            def rows_out(i, a):
                act.wait_ge(s_xn, START + 5 * NI + i + 1)
                act.copy(X[:, ds(i * U, U), :], XS[:, a]).then_inc(s_keep, 1)
                act.wait_ge(s_rl, START + i - 1)
                for v in range(XB):
                    act.wait_ge(s_xt, START + (6 * NI + i) * XB + v + 1)
                    act.copy(XM[:, a].rearrange("p c n -> p (c n)")[:, v * 2 * D:(v + 1) * 2 * D], PS[:, v, :]).then_inc(s_xte, 1)

            def router_out(i, a):
                act.wait_ge(s_rl, START + i + 1)
                act.copy(LG[:, ds(i * U, U), :], PS[:, 2 + a, 0:U * E].rearrange("p (u e) -> p u e", e=E)).then_inc(s_rle, 1)

            for i in range(NI - 1):
                roots(1, i)
            rows_out(0, 0)
            roots(1, NI - 1)
            nc.scalar.preload_act_table(ACT.Exp)
            rows_out(1, 1)
            router_out(0, 0)
            with act.Fori(1, NI // 2) as j:
                rows_out(j * 2, 0)
                router_out(j * 2 - 1, 1)
                rows_out(j * 2 + 1, 1)
                router_out(j * 2, 0)
            router_out(NI - 1, 1)
            act.wait_ge(s_route, 12)
            act.activation(rc["e"][:], rc["d"][:], ACT.Exp).then_inc(s_gap, 1)

            def high_weights(m, par, w):
                act.wait_ge(s_wl[w], 16 * m + 16)
                if w == 0:
                    act.wait_ge(s_gu, START + (m - 1) * FP)
                if w == 2:
                    act.wait_ge(s_down, START + m - 1)
                act.copy(WH[par][:, w, :], RAWW[:, w, :]).then_inc(s_wh, 1)

            def high_rows(m, par):
                act.wait_ge(s_bt, START + m + 1)
                act.copy(XH[par][:].rearrange("p c n -> p (c n)"), PS[:, 7, :]).then_inc(s_bh, 1)

            def expert_block(m, par, first=False, last=False):
                for q in range(FP):
                    at = m * FP + q
                    act.wait_ge(s_gu, START + at + 1)
                    act.wait_ge(s_hm, START + at - 1)
                    act.activation(SG[:, q % 2], PS[:, 2 * (q % 2):2 * (q % 2) + 2, 0:BLK], ACT.Silu).then_inc(s_silu, 1)
                    if not last and q != 2:
                        high_weights(m + 1, 1 - par, {0: 0, 1: 1, 3: 2}[q])
                    if q == 2 and not first:
                        block_out(m - 1, 1 - par)
                    act.wait_ge(s_hm, START + at + 1)
                    if q == 0:
                        act.wait_ge(s_down, START + m - 1)
                    act.copy(HH[par][:, 2 * q:2 * q + 2, :], HF[:, q % 2]).then_inc(s_hh, 1)
                    if q == 0 and not last:
                        high_rows(m + 1, 1 - par)

            def block_out(m, par):
                act.wait_ge(s_down, START + m + 1)
                act.wait_ge(s_eof, START + m - 1)
                act.copy(EO[:, par].rearrange("p a d -> p (a d)"), PS[:, 4 + par, :]).then_inc(s_eo, 1)

            for w in range(3):
                high_weights(0, 0, w)
            high_rows(0, 0)
            expert_block(0, 0, first=True)
            with act.Fori(0, NBLK // 2 - 1) as j:
                expert_block(j * 2 + 1, 1)
                expert_block(j * 2 + 2, 0)
            expert_block(NBLK - 2, 1)
            expert_block(NBLK - 1, 0, last=True)
            block_out(NBLK - 1, 0)
            for i in range(NI):
                roots(2, i)
                act.wait_ge(s_shift, i + 1)
                for t in range(i * U, i * U + U):
                    last = act.activation(X[:, t, :], X[:, t, :], ACT.Identity, bias=shift[:, t:t + 1], scale=rstd[:, t:t + 1])
                last.then_inc(s_fin, 1)

        @block.vector
        def _(dve):
            dve.sem_inc(s_ssq, START)
            dve.sem_inc(s_rstd, START)
            dve.sem_inc(s_xn, START)
            dve.sem_inc(s_dve, START)
            dve.sem_inc(s_hss, START)
            dve.sem_inc(s_split, START)
            dve.sem_inc(s_rest, START)
            dve.sem_inc(s_ke, START)
            dve.sem_inc(s_low, START)
            dve.sem_inc(s_osum, START)
            dve.sem_inc(s_on, START)
            dve.sem_inc(s_res, START)
            for s in (s_bn, s_clog, s_cmax, s_csub, s_crec, s_con, s_cres, s_wlo, s_bl, s_hm, s_hl):
                dve.sem_inc(s, START)

            def sums(n, i):
                dve.wait_ge(s_square, START + n + 1)
                dve.tensor_reduce(ssq[:, ds(i * U, U)], RS[:, ds(i % 2, 1)].rearrange("p a u n -> p (a u n)")[:, 0:U * D]
                                  .rearrange("p (u n) -> p u n", u=U), AX.X, ALU.add).then_inc(s_ssq, 1)

            def statistics(i):
                for u in range(U):
                    last = dve.bn_stats(ST[:, ds(i * U + u, 1), :].rearrange("p a s -> p (a s)"),
                                        X[:, ds(i * U + u, 1), :].rearrange("p a d -> p (a d)"))
                last.then_inc(s_stat, 1)

            def moments(n, i):
                dve.wait_ge(s_stat, n * NI + i + 1)
                for t in range(i * U, i * U + U):
                    last = dve.bn_aggr(MV[:, t, :], ST[:, t, :])
                last.then_inc(s_mv, 1)

            def deviations(n, i):
                dve.wait_ge(s_root, START + (2 + n) * NI + i + 1)
                dve.reciprocal(rstd[:, i * U:i * U + U], root[:, i * U:i * U + U]).then_inc(s_rstd, 1)
                dve.wait_ge(s_rstd, START + (2 + n) * NI + i + 1)
                dve.wait_ge(s_mv, n * NI + i + 1)

            def rows(k, i):
                dve.wait_ge(s_xt, START + (k * NI + i - 1) * XB)
                dve.wait_ge(s_xb if k == 4 else s_keep, START + i - 1)
                for u in range(U):
                    t = i * U + u
                    last = dve.tensor_scalar(XS[:, i % 2, u, :], X[:, t, :], MV[:, t:t + 1, 0], rstd[:, t:t + 1],
                                             ALU.subtract, ALU.mult)
                last.then_inc(s_xn, 1)

            def add_product(l, i):
                dve.wait_ge(s_oproj, START + (l * NI + i) * U + U)
                xs = X[:, ds(i * U, U), :]
                dve.tensor_tensor(xs, xs, ps_p[:, :, 0:D], ALU.add).then_inc(s_res, 1)

            def rms(l, i):
                dve.wait_ge(s_root, START + l * NI + i + 1)
                dve.reciprocal(rstd[:, i * U:i * U + U], root[:, i * U:i * U + U]).then_inc(s_rstd, 1)
                dve.wait_ge(s_rstd, START + l * NI + i + 1)

            def normalise(l, i):
                dve.wait_ge(s_xt, START + (2 * l * NI + i) * XB)
                dve.tensor_tensor(XN[:], X[:, ds(i * U, U), :],
                                  rstd[:, ds(i * U, U)].unsqueeze(2).to_broadcast([P, U, D]), ALU.mult).then_inc(s_xn, 1)

            def rotate(l, i, stacks=True):
                n = l * NI + i
                step = START + n * NDVE
                out = (lambda u: stack_out(l, i - 1, u)) if stacks else (lambda u: None)
                dve.wait_ge(s_raw, START + n * U + U)
                four = lambda a: a.rearrange("p u (h d) -> p u h d", h=QKH)
                out(0)
                dve.tensor_tensor(four(R1), RAW.rearrange("p u (h d) -> p u h d", h=QKH),
                                  rope_sb[:, l, 0, ds(i * U, U), :].unsqueeze(2).to_broadcast([P, U, QKH, HD]),
                                  ALU.mult).then_inc(s_dve, 1)
                out(1)
                out(2)
                dve.tensor_reduce(ss[:], SQ.rearrange("p u (h d) -> p (u h) d", d=HD), AX.X, ALU.add).then_inc(s_hss, 1)
                out(3)
                dve.wait_ge(s_rot2, START + n + 1)
                dve.wait_ge(s_dve, step + 1)
                dve.tensor_tensor(R1, R1, R2, ALU.add).then_inc(s_dve, 1)
                dve.wait_ge(s_hroot, START + n + 1)
                dve.reciprocal(rn[:], sr[:]).then_inc(s_dve, 1)
                dve.wait_ge(s_dve, step + 3)
                dve.wait_ge(s_stack, START + n)
                r = four(R1)
                inv = rn[:].rearrange("p (u h) -> p u h", u=U)
                for dst, a, b in ((RQ, 0, H), (RK, H, QKH)):
                    last = dve.tensor_tensor(dst[:].rearrange("p (u h) d -> p u h d", u=U), r[:, :, a:b, :],
                                             inv[:, :, a:b].unsqueeze(3).to_broadcast([P, U, b - a, HD]), ALU.mult)
                last.then_inc(s_dve, 1)

            def split(l, i):
                n = l * NI + i
                step = START + n * NDVE
                dve.wait_ge(s_qkt, START + n * U)
                dve.wait_ge(s_dve, step + 4)
                dve.tensor_copy(KS[:, :, 0, :], RK[:])
                dve.tensor_copy(QS[:, :, 0, :], RQ[:]).then_inc(s_dve, 1)
                dve.wait_ge(s_dve, step + 5)
                dve.tensor_tensor(KS[:, :, 1, :], RK[:], KS[:, :, 0, :], ALU.subtract).then_inc(s_split, 1)
                dve.tensor_tensor(QS[:, :, 2, :], RQ[:], QS[:, :, 0, :], ALU.subtract)
                dve.wait_ge(s_split, START + n + 1)
                k2 = KS[:].rearrange("p n (r c) d -> p n r (c d)", r=4)
                dve.tensor_copy(k2[:, :, 1:4, :], k2[:, :, 0:1, :].to_broadcast([P, U * G, 3, 2 * HD])).then_inc(s_rest, 1)

            def stack_out(l, i, u):
                k4 = KT[:].rearrange("p (g e) t -> p g e t", e=2)
                t = ds((i * U + u) * P, P)
                dve.wait_ge(s_qkt, START + (l * NI + i) * U + u + 1)
                dve.tensor_copy(k4[0:64, :, 0, t], ps_k[u % 2][0:64])
                dve.tensor_copy(k4[64:P, :, 1, t], ps_k[u % 2][64:P]).then_inc(s_ke, 1)

            def attend(l, it, first=False):
                for n, step in enumerate(STEPS[l]):
                    at = BASE[l] + it * len(STEPS[l]) + n
                    cut, cols = low_share(step)
                    done = [(it, q) for q in range(TB) if DONE[l][q] == n - 2]
                    if not first:
                        done += [(it - 1, q) for q in range(TB) if DONE[l][q] == n - 2 + len(STEPS[l])]
                    for pair, q in done:
                        add_parts(l, pair, q)
                    dve.wait_ge(s_exp, START + at + 1)
                    dve.wait_ge(s_pv, START + at - SLOT_REUSE[l][n] + 1)
                    pf = PF[:, SLOT_OF[l][n], 0:cut]
                    dve.tensor_tensor(PL[:, SLOT_OF[l][n], 0:cut], pf, high_part(pf), ALU.subtract).then_inc(s_low, 1)
                    for pair, q in done:
                        divide(l, pair, q)

            def add_parts(l, it, q):
                dve.wait_ge(s_pv, START + BASE[l] + it * len(STEPS[l]) + DONE[l][q] + 1)
                dve.reciprocal(OR[:, q % 2], ps_o[:, q % 2, :, 3 * HD:VW])
                dve.tensor_reduce(OS[:, q % 2], ps_o[:, q % 2, :, 0:3 * HD].rearrange("p h (c d) -> p h d c", c=3),
                                  AX.X, ALU.add).then_inc(s_osum, 1)

            def divide(l, it, q):
                dve.wait_ge(s_osum, START + l * BG * TB + it * TB + q + 1)
                dve.tensor_tensor(OA[:, ds(it // G * TB + q, 1), ds(it % G * (HG * HD), HG * HD)]
                                  .rearrange("p a (h d) -> p (a h) d", h=HG),
                                  OS[:, q % 2], OR[:, q % 2].to_broadcast([P, HG, HD]), ALU.mult).then_inc(s_on, 1)

            def context():
                for c in range(DC):
                    dve.tensor_scalar(W[1][:, c, :], W[1][:, c, :], nw[:, 1, c:c + 1], None, ALU.mult)
                dve.wait_ge(s_cload, NCLOAD)
                dve.wait_ge(s_ckv, 1)
                for o in range(DC):
                    last = dve.tensor_scalar(KB[:, o, :], PS[:, 6, o * NB * CL:(o + 1) * NB * CL], xb[:, 1, o:o + 1], None, ALU.add)
                for b in range(NB):
                    last = dve.tensor_tensor(VC[:, b * H:(b + 1) * H, :], PS[0:CL, 7, b * D:(b + 1) * D].rearrange("k (h d) -> k h d", h=H),
                                             BV[:].rearrange("k (h d) -> k h d", h=H), ALU.add)
                last.then_inc(s_ckb, 1)
                dve.wait_ge(s_ckb, 1)
                for b in range(NB):
                    for o in range(DC):
                        last = dve.tensor_tensor(KZ[:, b, o], KB[:, o, b * CL:(b + 1) * CL].unsqueeze(1).to_broadcast([P, CH, CL]),
                                                 own.unsqueeze(2).to_broadcast([P, CH, CL]), ALU.mult)
                dve.tensor_scalar(MF[:], MF[:], FMAX, None, ALU.mult)
                part = [VX[:, :, c * HD:(c + 1) * HD] for c in range(3)]
                dve.memset(VX[:, :, 3 * HD:VW], 1.0)
                dve.tensor_copy(part[0], VC).then_inc(s_ckz, 1)
                dve.wait_ge(s_ckz, 1)
                dve.tensor_tensor(VC2, VC, part[0], ALU.subtract).then_inc(s_ckz, 1)
                dve.wait_ge(s_ckz, 2)
                dve.tensor_copy(part[1], VC2).then_inc(s_ckz, 1)
                dve.wait_ge(s_ckz, 3)
                dve.tensor_tensor(part[2], VC2, part[1], ALU.subtract).then_inc(s_ckz, 1)

            k4 = KT[:].rearrange("p (g e) t -> p g e t", e=2)
            dve.memset(k4[64:P, :, 0, :], 0.0)
            dve.memset(k4[0:64, :, 1, :], 0.0)
            sums(0, 0)
            sums(1, 1)
            rms(0, 0)
            normalise(0, 0)
            for i in range(2, NI):
                sums(i, i)
                rms(0, i - 1)
            rms(0, NI - 1)
            dve.wait_ge(s_loadw, NLOAD)
            dve.wait_ge(s_fuse, 1)
            for c in range(DC):
                dve.tensor_scalar(W[0][:, c, D:QKV], PS[:, 6 + c, 0:P], nw[:, 0, c:c + 1], None, ALU.mult)
                last = dve.tensor_scalar(W[0][:, c, 0:D], W[0][:, c, 0:D], nw[:, 0, c:c + 1], None, ALU.mult)
            last.then_inc(s_weights, 1)
            for l in range(2):
                normalise(l, 1)
                rotate(l, 0, stacks=False)
                split(l, 0)
                if l == 0:
                    context()
                with dve.Fori(2, NI) as i:
                    normalise(l, i)
                    rotate(l, i - 1)
                    split(l, i - 1)
                rotate(l, NI - 1)
                split(l, NI - 1)
                for u in range(U):
                    stack_out(l, NI - 1, u)
                attend(l, 0, first=True)
                with dve.Fori(1, BG) as it:
                    attend(l, it)
                for q in range(TB):
                    if DONE[l][q] >= len(STEPS[l]) - 2:
                        add_parts(l, BG - 1, q)
                        divide(l, BG - 1, q)
                if l == 0:
                    for i in range(NI):
                        add_product(0, i)
                        sums(NI + i, i)
                        if i == NI - 2:
                            rms(1, 0)
                            normalise(1, 0)
                    for i in range(1, NI):
                        rms(1, i)

            for i in range(NI):
                add_product(1, i)
                dve.wait_ge(s_x0[i % 2], 16 * (i // 2 + 1))
                dve.wait_ge(s_res, START + NI + i + 1)
                xs = X[:, i * U:i * U + U, :]
                dve.tensor_tensor(xs, xs, OA[:, i * U:i * U + U, :], ALU.add).then_inc(s_bn, 1)
                dve.wait_ge(s_bn, START + i + 1)
                statistics(i)
                moments(0, i)
                if i >= NI - 2:
                    for early in range(i % 2 * 2, i % 2 * 2 + 2):
                        deviations(0, early)
                        rows(4, early)

            def cross_step(i, m, earlier):
                u, a, c, at = m // DC, m % 2, m % CLS, i * CS + m
                dve.wait_ge(s_cs, START + at + 1)
                dve.wait_ge(s_cexp, START + at - CLS + 1)
                ps = PS[:, 4 + 2 * a:6 + 2 * a, 0:CH // 2 * CL].rearrange("p b (h k) -> p b h k", h=CH // 2)
                lg = CLG[:, c].rearrange("p (b h) k -> p b h k", b=2)
                mf = MF[:, ds(i * U + u, 1), :]
                dve.tensor_tensor(lg, ps, mf.unsqueeze(1).to_broadcast([P, 2, CH // 2, CL]), ALU.subtract).then_inc(s_clog, 1)
                if earlier:
                    cross_parts(*earlier)
                dve.wait_ge(s_clog, START + at + 1)
                dve.tensor_reduce(CMX[:, a], CLG[:, c], AX.X, ALU.max).then_inc(s_cmax, 1)
                if earlier:
                    cross_divide(*earlier)
                dve.wait_ge(s_cmax, START + at + 1)
                dve.tensor_tensor(CLG[:, c], CLG[:, c], CMX[:, a].to_broadcast([P, CH, CL]), ALU.subtract).then_inc(s_csub, 1)

            def cross_parts(i, m):
                o, a = m % DC, m % 2
                dve.wait_ge(s_cpv, START + i * CS + m + 1)
                ps = PS[:, 2 + o, 0:CH * VW].rearrange("p (h v) -> p h v", h=CH)
                dve.reciprocal(CR[:, a], ps[:, :, 3 * HD:VW])
                dve.tensor_reduce(CA[:, a], ps[:, :, 0:3 * HD].rearrange("p h (c d) -> p h d c", c=3),
                                  AX.X, ALU.add).then_inc(s_crec, 1)

            def cross_divide(i, m):
                u, o, a = m // DC, m % DC, m % 2
                dve.wait_ge(s_crec, START + i * CS + m + 1)
                dve.tensor_tensor(OX[:, ds(i * U + u, 1), o * P:(o + 1) * P].rearrange("p a (h d) -> p (a h) d", h=CH),
                                  CA[:, a], CR[:, a].to_broadcast([P, CH, HD]), ALU.mult).then_inc(s_con, 1)

            for m in range(CS):
                cross_step(0, m, (0, m - LATER) if m >= LATER else None)
            with dve.Fori(1, NI) as i:
                for m in range(CS):
                    cross_step(i, m, (i, m - LATER) if m >= LATER else (i - 1, m - LATER + CS))
            for m in range(CS - LATER, CS):
                cross_parts(NI - 1, m)
                cross_divide(NI - 1, m)
            for i in range(NI):
                dve.wait_ge(s_cwo, START + i * XB + XB)
                xs, a = X[:, i * U:i * U + U, :], i % 2
                dve.tensor_tensor(xs, xs, PS[:, 2 + 2 * a:4 + 2 * a, :].rearrange("p b (u d) -> p (b u) d", u=2),
                                  ALU.add).then_inc(s_cres, 1)
                dve.wait_ge(s_cres, START + i + 1)
                statistics(i)
                moments(1, i)
                if i >= NI - 2:
                    for early in range(i % 2 * 2, i % 2 * 2 + 2):
                        deviations(1, early)
                        rows(6, early)

            count = [0]

            def then(ins):
                count[0] += 1
                ins.then_inc(s_route, 1)
                dve.wait_ge(s_route, count[0])

            te = [P, NT, E]
            dve.wait_ge(s_rle, START + NI)
            wide = lambda a: a.unsqueeze(2).to_broadcast(te)
            each = lambda a: a.unsqueeze(1).to_broadcast(te)
            for k, logits in (("1", LG[:]), ("2", rt["left"][:])):
                if k == "2":
                    then(dve.scalar_tensor_tensor(out=rt["left"][:], in0=rt["one1"][:], scalar=-FMAX, in1=LG[:],
                                                  op0=ALU.mult, op1=ALU.add))
                then(dve.tensor_reduce(rc["m" + k][:], logits, AX.X, ALU.max))
                then(dve.tensor_tensor(rt["eq" + k][:], logits, wide(rc["m" + k][:]), ALU.is_equal))
                then(dve.scalar_tensor_tensor(out=rt["code" + k][:], in0=rt["eq" + k][:], scalar=-float(E),
                                              in1=each(expert_no), op0=ALU.mult, op1=ALU.add))
                then(dve.tensor_reduce(rc["i" + k][:], rt["code" + k][:], AX.X, ALU.min))
                then(dve.tensor_tensor(rt["one" + k][:], rt["code" + k][:], wide(rc["i" + k][:]), ALU.is_equal))
            then(dve.tensor_tensor(rc["d"][:], rc["m2"][:], rc["m1"][:], ALU.subtract))
            then(dve.tensor_tensor(SW[:, :, 0:E], rt["one1"][:], rt["one2"][:], ALU.add))
            dve.wait_ge(s_gap, 1)
            then(dve.tensor_scalar(rc["den"][:], rc["e"][:], 1.0, None, ALU.add))
            then(dve.reciprocal(rc["r"][:], rc["den"][:]))
            then(dve.tensor_tensor(rc["p2"][:], rc["e"][:], rc["r"][:], ALU.mult))
            then(dve.tensor_tensor(rt["w1"][:], rt["one1"][:], wide(rc["r"][:]), ALU.mult))
            then(dve.tensor_tensor(rt["w2"][:], rt["one2"][:], wide(rc["p2"][:]), ALU.mult))
            then(dve.tensor_tensor(SW[:, :, E:2 * E], rt["w1"][:], rt["w2"][:], ALU.add))
            assert count[0] == NSHARES
            dve.wait_ge(s_tot, 1)
            then(dve.tensor_copy(TOT[:].rearrange("p t e -> p (t e)"), PS[:, 3, 0:NT * 2 * E]))
            dve.memset(rt["pfa"][:, 0:1, :], 0.0)
            then(dve.tensor_copy(rt["pfa"][:, 1:NT, :], TOT[:, 0:NT - 1, 0:E]))
            a, b = rt["pfa"], rt["pfb"]
            for d in (1, 2, 4, 8):
                dve.tensor_copy(b[:, 0:d, :], a[:, 0:d, :])
                then(dve.tensor_tensor(b[:, d:NT, :], a[:, d:NT, :], a[:, 0:NT - d, :], ALU.add))
                a, b = b, a
            then(dve.tensor_tensor(rt["t1"][:], a[:], PS[:, 4, 0:NT * E].rearrange("p (t e) -> p t e", e=E), ALU.add))
            then(dve.tensor_tensor(re["cnt"][:], a[:, NT - 1, :], TOT[:, NT - 1, 0:E], ALU.add))
            then(dve.tensor_tensor(GTJ[:], re["cnt"][:].unsqueeze(2).to_broadcast([P, E, NJ]),
                                   block_rows.rearrange("p (e j) -> p e j", e=E), ALU.is_gt))
            then(dve.tensor_reduce(re["nb"][:], GTJ[:], AX.X, ALU.add))
            dve.memset(re["bba"][:, 0:1], 0.0)
            then(dve.tensor_copy(re["bba"][:, 1:E], re["nb"][:, 0:E - 1]))
            a, b = re["bba"], re["bbb"]
            for d in (1, 2, 4):
                dve.tensor_copy(b[:, 0:d], a[:, 0:d])
                then(dve.tensor_tensor(b[:, d:E], a[:, d:E], a[:, 0:E - d], ALU.add))
                a, b = b, a
            then(dve.tensor_tensor(re["end"][:], a[:], re["nb"][:], ALU.add))
            then(dve.tensor_tensor(LEB[:], re["end"][:].unsqueeze(1).to_broadcast([P, NBLK, E]),
                                   block_no.unsqueeze(2).to_broadcast([P, NBLK, E]), ALU.is_le))
            then(dve.tensor_reduce(EBF[:], LEB[:], AX.X, ALU.add))
            then(dve.tensor_scalar(EB[:], EBF[:], float(E - 1), None, ALU.min))
            assert count[0] == NEXPERT
            then(dve.scalar_tensor_tensor(out=rt["slot"][:], in0=each(a[:]), scalar=float(BLK), in1=rt["t1"][:],
                                          op0=ALU.mult, op1=ALU.add))
            for k in range(2):
                then(dve.tensor_tensor(rt["t2"][:], rt[f"one{k + 1}"][:], rt["slot"][:], ALU.mult))
                then(dve.tensor_reduce(POSF[:, k], rt["t2"][:], AX.X, ALU.add))
            then(dve.tensor_copy(SLOT[:], POSF[:]))
            then(dve.tensor_scalar(RUN[:, 0], SLOT[:], 7, None, ALU.logical_shift_right))
            then(dve.tensor_scalar(RUN[:, 1], SLOT[:], P - 1, None, ALU.bitwise_and))
            then(dve.tensor_copy(RUNF[:], RUN[:].rearrange("p a k t -> p a (k t)")))
            then(dve.tensor_tensor(ISRUN[:], counting[:, 0:NR].unsqueeze(1).to_broadcast([P, 2 * NT, NR]),
                                   RUNF[:, 0].unsqueeze(2).to_broadcast([P, 2 * NT, NR]), ALU.is_equal))
            then(dve.tensor_scalar(WHO[:, :, 1, :], ISRUN[:], row_no, None, ALU.mult))
            then(dve.tensor_tensor(WHO[:, :, 0, :], ISRUN[:], counting[:, 1:2 * NT + 1].unsqueeze(2)
                                   .to_broadcast([P, 2 * NT, NR]), ALU.mult))
            for c in range(0, 2 * NT, 8):
                then(dve.tensor_tensor(PLACE[:, c:c + 8, :], counting.unsqueeze(1).to_broadcast([P, 8, P]),
                                       RUNF[:, 1, c:c + 8].unsqueeze(2).to_broadcast([P, 8, P]), ALU.is_equal))
            assert count[0] == NSLOT
            then(dve.tensor_reduce(re["sumw"][:], TOT[:, :, E:2 * E].rearrange("p t e -> p e t"), AX.X, ALU.add))
            then(dve.tensor_scalar(re["one"][:], re["cnt"][:], 1.0, None, ALU.max))
            then(dve.reciprocal(re["inv"][:], re["one"][:]))
            then(dve.tensor_tensor(re["mean"][:], re["sumw"][:], re["inv"][:], ALU.mult))
            for k in range(2):
                then(dve.tensor_tensor(rt["t2"][:], rt[f"one{k + 1}"][:], each(re["mean"][:]), ALU.mult))
                then(dve.tensor_reduce(CO[:, k], rt["t2"][:], AX.X, ALU.add))
            dve.wait_ge(s_map, 1)
            then(dve.tensor_copy(inv["spare"][:], PS[:, 5, 0:NR]))
            then(dve.scalar_tensor_tensor(out=inv["of"][:], in0=inv["spare"][:], scalar=float(P), in1=PS[:, 5, NR:2 * NR],
                                          op0=ALU.mult, op1=ALU.add))
            then(dve.tensor_scalar(inv["none"][:], inv["of"][:], float(P), None, ALU.is_lt))
            then(dve.tensor_tensor(inv["spare"][:], inv["none"][:], spare, ALU.mult))
            then(dve.scalar_tensor_tensor(out=TARGET[:], in0=inv["of"][:], scalar=-float(P), in1=inv["spare"][:],
                                          op0=ALU.add, op1=ALU.add))
            then(dve.tensor_scalar(inv["token"][:], inv["of"][:], -float(P), 0.0, ALU.add, ALU.max))
            then(dve.tensor_scalar(inv["second"][:], inv["token"][:], float(T), None, ALU.is_ge))
            then(dve.scalar_tensor_tensor(out=SOURCE[:], in0=inv["second"][:], scalar=-float(T), in1=inv["token"][:],
                                          op0=ALU.mult, op1=ALU.add))
            assert count[0] == NROUTE

            def low_weights(m, par, w):
                dve.wait_ge(s_wh, START + m * 3 + w + 1)
                if w == 2:
                    dve.wait_ge(s_down, START + m - 1)
                dve.tensor_tensor(WL[par][:, w, :], RAWW[:, w, :], WH[par][:, w, :].bitcast(F32), ALU.subtract).then_inc(s_wlo, 1)

            def low_rows(m, par):
                dve.wait_ge(s_bh, START + m + 1)
                dve.tensor_tensor(XL[par][:].rearrange("p c n -> p (c n)"), PS[:, 7, :],
                                  XH[par][:].rearrange("p c n -> p (c n)").bitcast(F32), ALU.subtract).then_inc(s_bl, 1)

            def expert_block(m, par, last=False):
                for q in range(FP):
                    at = m * FP + q
                    dve.wait_ge(s_silu, START + at + 1)
                    dve.wait_ge(s_hh, START + at - 1)
                    dve.tensor_tensor(HF[:, q % 2], SG[:, q % 2], PS[:, 2 * (q % 2):2 * (q % 2) + 2, BLK:2 * BLK],
                                      ALU.mult).then_inc(s_hm, 1)
                    if not last and q != 2:
                        low_weights(m + 1, 1 - par, {0: 0, 1: 1, 3: 2}[q])
                    dve.wait_ge(s_hh, START + at + 1)
                    if q == 0:
                        dve.wait_ge(s_down, START + m - 1)
                    dve.tensor_tensor(HL[par][:, 2 * q:2 * q + 2, :], HF[:, q % 2],
                                      HH[par][:, 2 * q:2 * q + 2, :].bitcast(F32), ALU.subtract).then_inc(s_hl, 1)
                    if q == 0 and not last:
                        low_rows(m + 1, 1 - par)

            low_weights(0, 0, 0)
            low_weights(0, 0, 1)
            low_rows(0, 0)
            low_weights(0, 0, 2)
            expert_block(0, 0)
            with dve.Fori(0, NBLK // 2 - 1) as j:
                expert_block(j * 2 + 1, 1)
                expert_block(j * 2 + 2, 0)
            expert_block(NBLK - 2, 1)
            expert_block(NBLK - 1, 0, last=True)

            for i in range(NI):
                dve.wait_ge(s_gat[i % 2], 2 * 16 * (i // 2 + 1))
                for k in range(2):
                    for u in range(U):
                        t = i * U + u
                        last = dve.scalar_tensor_tensor(out=X[:, t, :], in0=YB[:, i % 2, k, u, :], scalar=CO[:, k, t:t + 1],
                                                        in1=X[:, t, :], op0=ALU.mult, op1=ALU.add)
                    last.then_inc(s_mix, 1)
                    dve.wait_ge(s_mix, 2 * i + k + 1)
                statistics(i)
                moments(2, i)
                deviations(2, i)
                tiles = slice(i * U, i * U + U)
                dve.scalar_tensor_tensor(out=shift[:, tiles], in0=MV[:, tiles, 0], scalar=-1.0, in1=rstd[:, tiles],
                                         op0=ALU.mult, op1=ALU.mult).then_inc(s_shift, 1)

        @block.tensor
        def _(pe):
            pe.sem_inc(s_xt, START)
            pe.sem_inc(s_proj, START)
            pe.sem_inc(s_qkt, START)
            pe.sem_inc(s_score, START)
            pe.sem_inc(s_pv, START)
            pe.sem_inc(s_oproj, START)
            for s in (s_cq, s_cs, s_cpt, s_cpv, s_cwo, s_rl, s_bt, s_gu, s_down):
                pe.sem_inc(s, START)

            pe.wait_ge(s_loadw, NLOAD)
            for c in range(DC):
                last = pe.matmul(PS[:, 6 + c, 0:P], kvd_sb[:, c * P:(c + 1) * P], kvup_sb[:], start=True, stop=True)
            last.then_inc(s_fuse, 1)
            def context():
                pe.wait_ge(s_cload, NCLOAD)
                for o in range(DC):
                    for c in range(DC):
                        pe.matmul(PS[:, 6, o * NB * CL:(o + 1) * NB * CL], WX[:, 1, c, o * P:(o + 1) * P], ctx_sb[:, c, :],
                                  start=(c == 0), stop=(c == DC - 1))
                for b in range(NB):
                    for c in range(DC):
                        last = pe.matmul(PS[0:CL, 7, b * D:(b + 1) * D], ctx_sb[:, c, b * CL:(b + 1) * CL], WX[:, 2, c, :],
                                         start=(c == 0), stop=(c == DC - 1))
                last.then_inc(s_ckv, 1)

            def transposes(k, i):
                pe.wait_ge(s_xn, START + k * NI + i + 1)
                transpose_group(k * NI + i, XN)

            def transpose_group(n, rows):
                pe.wait_ge(s_xte, START + n * XB)
                for v in range(XB):
                    for u in (2 * v, 2 * v + 1):
                        for c in range(DC):
                            last = pe.transpose(ps_x[:, u, c * P:(c + 1) * P], rows[:, u, c * P:(c + 1) * P], identF)
                    last.then_inc(s_xt, 1)

            def products(k, i, w, cols, s_done, s_free, free):
                for u in range(U):
                    if u % 2 == 0:
                        pe.wait_ge(s_xte, START + (k * NI + i) * XB + u // 2 + 1)
                    if u == 0:
                        pe.wait_ge(s_free, START + free)
                    for c in range(DC):
                        last = pe.matmul(ps_p[:, u, 0:cols], XT[:, u, c, :], w[:, c, 0:cols],
                                         start=(c == 0), stop=(c == DC - 1))
                    last.then_inc(s_done, 1)

            def stack_transposes(l, i):
                n = l * NI + i
                pe.wait_ge(s_stack, START + n + 1)
                pe.wait_ge(s_rest, START + n + 1)
                pe.wait_ge(s_dup, START + n + 1)
                for u in range(U):
                    pe.wait_ge(s_qe, START + n * U + u - 1)
                    pe.wait_ge(s_ke, START + n * U + u - 1)
                    for h in range(H // 2):
                        pe.transpose(ps_q[u % 2][:, h, :], QS2[:, u * H // 2 + h, :], identH[:])
                    for g in range(G):
                        last = pe.transpose(ps_k[u % 2][:, g, :], KS2[:, u * G + g, :], identH[:])
                    last.then_inc(s_qkt, 1)

            def scores(l, it, n):
                at = BASE[l] + it * len(STEPS[l]) + n
                b, g = it // G, it % G
                pe.wait_ge(s_exp, START + at - BANK_REUSE[l][n] + 1)
                col = 0
                for q, k, w in STEPS[l][n]:
                    into = ps_s[:, BANK_OF[l][n], col:col + HG * w]
                    table = None if k < q and l == 0 else 0 if l == 0 else 1 if k == q else 2
                    if table is not None:
                        pe.matmul(into, identB[:], hide[:, table, :, 0:w], start=True, stop=False, skip_group_check=True)
                    for e in range(2):
                        last = pe.matmul(into[:, e * 2 * w:(e + 1) * 2 * w], KTf[:, ds((g * 2 + e) * T + b * S + k * P, P)],
                                         QT[:, ds(g * 2, 2), ds(b * S + q * P, w)],
                                         start=(table is None and e == 0), stop=(e == 1), skip_group_check=True)
                    col += HG * w
                last.then_inc(s_score, 1)

            def values(l, it, n):
                at = BASE[l] + it * len(STEPS[l]) + n
                b, g = it // G, it % G
                pe.wait_ge(s_exp, START + at + 1)
                pe.wait_ge(s_low, START + at + 1)
                pe.wait_ge(s_lowp, START + at + 1)
                col = 0
                for q, k, w in STEPS[l][n]:
                    first = k == 0 if l == 0 else k == q
                    if first:
                        pe.wait_ge(s_osum, START + l * BG * TB + it * TB + q - 1)
                    vs = VSf[:, ds(((b * TB + k) * G + g) * VW, VW)]
                    for h in range(HG):
                        at_h = head_column(h, w) + col
                        pf = high_part(PF[:, SLOT_OF[l][n], at_h:at_h + w])
                        pl = PL[:, SLOT_OF[l][n], at_h:at_h + w]
                        for part, p in enumerate((pf, pl)):
                            last = pe.matmul(ps_o[0:w, q % 2, h, :], p, vs, start=(first and h == 0 and part == 0),
                                             stop=True, skip_group_check=True)
                    col += HG * w
                last.then_inc(s_pv, 1)

            def attend(l, it, last=False):
                for n in range(len(STEPS[l])):
                    if n + BANKS < len(STEPS[l]):
                        scores(l, it, n + BANKS)
                    elif not last:
                        scores(l, it + 1, n + BANKS - len(STEPS[l]))
                    values(l, it, n)

            def head_column(h, w):
                return ((h % 2) * 2 + h // 2) * w

            for l in range(2):
                def project(i, first=False):
                    pe.wait_ge(s_qe, START + (l * NI + i - 1) * U - 1)
                    pe.wait_ge(s_ke, START + (l * NI + i - 1) * U - 1)
                    transposes(2 * l, i)
                    if first:
                        if l:
                            pe.wait_ge(s_res, START + NI)
                        else:
                            pe.wait_ge(s_weights, 1)
                    products(2 * l, i, W[l], QKV, s_proj, s_raw, (l * NI + i) * U)
                project(0, first=True)
                if l == 0:
                    context()
                project(1)
                if l == 0:
                    pe.wait_ge(s_ckb, 1)
                    pe.wait_ge(s_const, 2)
                with pe.Fori(2, NI) as i:
                    pe.wait_ge(s_xte, START + (2 * l * NI + i) * XB)
                    stack_transposes(l, i - 2)
                    project(i)
                pe.wait_ge(s_xte, START + (2 * l + 1) * NI * XB)
                stack_transposes(l, NI - 2)
                stack_transposes(l, NI - 1)
                pe.wait_ge(s_qe, START + (l + 1) * NT)
                pe.wait_ge(s_ke, START + (l + 1) * NT)
                pe.wait_ge(s_vs, START + (l + 1) * NI * NVS)
                for n in range(BANKS):
                    scores(l, 0, n)
                with pe.Fori(0, BG - 1) as it:
                    attend(l, it)
                attend(l, BG - 1, last=True)
                with pe.Fori(0, NI) as i:
                    transposes(2 * l + 1, i)
                    products(2 * l + 1, i, WO[l], D, s_oproj, s_res, l * NI + i)

            def cross_scores(i, m):
                u, o, a, n = m // DC, m % DC, m % 2, i * CS + m
                if o == 0:
                    pe.wait_ge(s_qg, START + i * U + u + 1)
                pe.wait_ge(s_clog, START + n - 1)
                for j in range(2):
                    w = CH // 2 * CL
                    last = pe.matmul(PS[:, 4 + 2 * a + j, 0:w], QG[:, o, u * P:(u + 1) * P],
                                     KZf[:, ds(((i // (NI // NB) * DC + o) * 2 + j) * w, w)], start=True, stop=True)
                last.then_inc(s_cs, 1)

            def cross_transposes(i, m):
                n = i * CS + m
                pe.wait_ge(s_cexp, START + n + 1)
                pe.wait_ge(s_cpe, START + n)
                for h in range(CH):
                    last = pe.transpose(PS[0:CL, h // 4, (h % 4) * P:(h % 4 + 1) * P], CPX[:, m % 2, h, :], identF)
                last.then_inc(s_cpt, 1)

            def cross_values(i, m):
                o, a, n = m % DC, m % 2, i * CS + m
                pe.wait_ge(s_cpe, START + n + 1)
                pe.wait_ge(s_cpl, START + n + 1)
                pe.wait_ge(s_crec, START + n - 1)
                for h in range(CH):
                    for part, p in enumerate((high_part(CPT[:, a, h, :]), CPL[:, a, h, :])):
                        last = pe.matmul(PS[:, 2 + o, h * VW:(h + 1) * VW], p,
                                         VXf[:, ds((i // (NI // NB) * H + o * CH + h) * VW, VW)],
                                         start=(h == 0 and part == 0), stop=True, skip_group_check=True)
                last.then_inc(s_cpv, 1)

            def cross_group(i, first=False):
                for m in range(CS):
                    if m >= LATE:
                        cross_transposes(i, m - LATE)
                    elif not first:
                        cross_transposes(i - 1, m - LATE + CS)
                    cross_scores(i, m)
                    if m >= LATER:
                        cross_values(i, m - LATER)
                    elif not first:
                        cross_values(i - 1, m - LATER + CS)

            pe.wait_ge(s_ckz, 4)
            pe.wait_ge(s_res, START + 2 * NI)
            with pe.Fori(0, NI // 2) as j:
                for a in range(2):
                    i = j * 2 + a
                    pe.wait_ge(s_xn, START + 4 * NI + i + 1)
                    transpose_group(4 * NI + i, XS[:, a])
                    pe.wait_ge(s_xte, START + (4 * NI + i + 1) * XB)
                    for o in range(DC):
                        pe.wait_ge(s_cqe, START + (i - 1) * DC + o + 1)
                        for c in range(DC):
                            last = pe.matmul(PS[:, 2 + o, :], WX[:, 0, c, o * P:(o + 1) * P], XM[:, a, c, :],
                                             start=(c == 0), stop=(c == DC - 1))
                        last.then_inc(s_cq, 1)
            cross_group(0, first=True)
            with pe.Fori(1, NI) as i:
                cross_group(i)
            for m in range(CS - LATE, CS):
                cross_transposes(NI - 1, m)
                cross_values(NI - 1, m - 1)
            cross_values(NI - 1, CS - 1)
            pe.wait_ge(s_con, START + NI * CS)
            with pe.Fori(0, NI // 2) as j:
                for a in range(2):
                    i = j * 2 + a
                    pe.wait_ge(s_ostage, START + i + 1)
                    transpose_group(5 * NI + i, XS[:, a])
                    pe.wait_ge(s_cres, START + i - 1)
                    for u in range(U):
                        if u % 2 == 0:
                            pe.wait_ge(s_xte, START + (5 * NI + i) * XB + u // 2 + 1)
                        for c in range(DC):
                            last = pe.matmul(PS[:, 2 + 2 * a + u // 2, (u % 2) * D:(u % 2 + 1) * D], XT[:, u, c, :], WX[:, 3, c, :],
                                             start=(c == 0), stop=(c == DC - 1))
                        if u % 2:
                            last.then_inc(s_cwo, 1)

            def router_transposes(i, a):
                pe.wait_ge(s_xn, START + 5 * NI + i + 1)
                transpose_group(6 * NI + i, XS[:, a])

            def router_products(i, a):
                pe.wait_ge(s_xte, START + (6 * NI + i + 1) * XB)
                pe.wait_ge(s_rle, START + i - 1)
                xt = XM[:, a].rearrange("p c n -> p (c n)").rearrange("p (u c n) -> p u c n", u=U, c=DC)
                for u in range(U):
                    for c in range(DC):
                        last = pe.matmul(PS[:, 2 + a, u * E:(u + 1) * E], xt[:, u, c, :], RW[:, c, :],
                                         start=(c == 0), stop=(c == DC - 1))
                last.then_inc(s_rl, 1)

            router_transposes(0, 0)
            router_transposes(1, 1)
            router_products(0, 0)
            with pe.Fori(1, NI // 2) as j:
                router_transposes(j * 2, 0)
                router_products(j * 2 - 1, 1)
                router_transposes(j * 2 + 1, 1)
                router_products(j * 2, 0)
            router_products(NI - 1, 1)
            pe.wait_ge(s_route, NSHARES)
            pe.matmul(PS[:, 3, 0:NT * 2 * E], ONES[:], SW[:].rearrange("p t e -> p (t e)"), start=True, stop=True)
            pe.matmul(PS[:, 4, 0:NT * E], before, SW[:, :, 0:E], start=True, stop=True).then_inc(s_tot, 1)

            for c in range(2 * NT):
                if c % 8 == 0:
                    pe.wait_ge(s_route, NSLOT - 3 + c // 8)
                last = pe.matmul(PS[:, 5, 0:2 * NR], PLACE[:, c, :], WHO[:, c].rearrange("p a r -> p (a r)"),
                                 start=(c == 0), stop=(c == 2 * NT - 1))
            last.then_inc(s_map, 1)

            def three(into, hs, ls, hm, lm, start, stop):
                pe.matmul(into, hs, hm, start=start, stop=False, skip_group_check=True)
                pe.matmul(into, hs, lm, start=False, stop=False, skip_group_check=True)
                return pe.matmul(into, ls, hm, start=False, stop=stop, skip_group_check=True)

            def block_rows_in(m, par, half):
                pe.wait_ge(s_xbl[par], 16 * BA * (half + 1))
                pe.wait_ge(s_bl, START + m)
                for c in range(DC):
                    for a in range(BA):
                        last = pe.transpose(PS[:, 7, (c * BA + a) * P:(c * BA + a + 1) * P],
                                            XR[:, par, a, c * P:(c + 1) * P], identF)
                last.then_inc(s_bt, 1)

            def down(m, par):
                pe.wait_ge(s_hl, START + m * FP + FP)
                pe.wait_ge(s_wlo, START + m * 3 + 3)
                pe.wait_ge(s_eo, START + m - 1)
                for a in range(BA):
                    for f in range(FC):
                        last = three(PS[:, 4 + par, a * D:(a + 1) * D],
                                     HH[par][:, f, a * P:(a + 1) * P], HL[par][:, f, a * P:(a + 1) * P],
                                     WH[par][:, 2, f * D:(f + 1) * D], WL[par][:, 2, f * D:(f + 1) * D],
                                     start=(a == 0 and f == 0), stop=(f == FC - 1))
                last.then_inc(s_down, 1)

            def expert_block(m, par, half, first=False, last=False):
                pe.wait_ge(s_bl, START + m + 1)
                pe.wait_ge(s_wlo, START + m * 3 + 2)
                for q in range(FP):
                    pe.wait_ge(s_hm, START + m * FP + q - 1)
                    for f in (2 * q, 2 * q + 1):
                        for w in range(2):
                            for c in range(DC):
                                at = c * FI + f * P
                                done = three(PS[:, 2 * (q % 2) + f % 2, w * BLK:(w + 1) * BLK],
                                             WH[par][:, w, at:at + P], WL[par][:, w, at:at + P],
                                             XH[par][:, c, :], XL[par][:, c, :],
                                             start=(w == 0 and c == 0), stop=(c == DC - 1))
                    done.then_inc(s_gu, 1)
                    if q == 1 and not first:
                        down(m - 1, 1 - par)
                    if q == 0 and not last:
                        block_rows_in(m + 1, 1 - par, half if par == 0 else half + 1)

            block_rows_in(0, 0, 0)
            expert_block(0, 0, 0, first=True)
            with pe.Fori(0, NBLK // 2 - 1) as j:
                expert_block(j * 2 + 1, 1, j)
                expert_block(j * 2 + 2, 0, j + 1)
            expert_block(NBLK - 2, 1, NBLK // 2 - 1)
            expert_block(NBLK - 1, 0, NBLK // 2, last=True)
            down(NBLK - 1, 0)


def low_share(step):
    cols = sum(HG * w for _, _, w in step)
    return cols * 5 // 8, cols


def high_part(a):
    return a.bitcast(BF16).rearrange("p (n two) -> p n two", two=2)[:, :, 1]


def constants():
    f = np.float32
    rope = np.zeros((P, 2, 2, NT, HD), f)
    for l, base in enumerate((1000000.0, 10000.0)):
        inv = f(1.0) / np.power(f(base), np.arange(0, HD, 2, dtype=f) / f(HD)).astype(f)
        ang = (np.arange(S, dtype=f)[:, None] * inv[None, :]).astype(f)
        c, s = np.cos(ang).astype(f), np.sin(ang).astype(f)
        both = np.stack([np.repeat(c, 2, 1), np.stack([-s, s], -1).reshape(S, HD)])
        both = np.tile(both.reshape(2, TB, P, HD), (1, NB, 1, 1))
        rope[:, l] = both.transpose(2, 0, 1, 3)
    small = np.zeros((P, AT_ROW + 1), f)
    small[:, 0:CH] = SCALE * (np.arange(P)[:, None] // HD == np.arange(CH)[None, :])
    small[:, 8:16] = np.arange(E)
    small[:, 2 * CH:AT_BLOCK] = np.tile(np.arange(NJ) * BLK, E)
    small[:, AT_BLOCK:AT_BEFORE] = np.arange(NBLK)
    small[:, AT_BEFORE:AT_COUNT] = np.arange(P)[:, None] < np.arange(P)[None, :]
    small[:, AT_COUNT:AT_SPARE] = np.arange(P)
    small[:, AT_SPARE:AT_ROW] = P + 2 * T + np.arange(NR)[None, :] * P + np.arange(P)[:, None]
    small[:, AT_ROW] = np.arange(P)
    tri = np.zeros((P, 4, P), f)
    k, q = np.arange(P)[:, None], np.arange(P)[None, :]
    tri[:, 0] = np.where(q >= k, 0.0, HIDE)
    tri[:, 1] = np.where((q >= k) & (q - k < WIN), 0.0, HIDE)
    tri[:, 2] = np.where(P + q - k < WIN, 0.0, HIDE)
    tri[:, 3] = np.eye(P)
    return rope, tri, small


_OUT = (NB, S, D)


def kernel(**inputs):
    import numpy as _np
    import concourse.bacc as _bacc
    from concourse import mybir as _mybir
    from concourse.bass_utils import run_bass_kernel_spmd as _run

    a = {k.replace("L0_", ""): _np.asarray(v) for k, v in inputs.items()}
    rope, tri, small = constants()
    column = lambda v: v.reshape(DC, P).T
    chunked = lambda w: w.reshape(E, -1, P, w.shape[-1]).transpose(0, 2, 1, 3).reshape(E, P, THIRD)
    gate, up = (chunked(a[f"ffn_{n}_w"].transpose(0, 2, 1)) for n in ("gate", "up"))
    lower = chunked(a["ffn_down_w"].transpose(0, 2, 1))
    arrays = {
        "x": a["x"].reshape(T, D),
        "wq0": a["attn_g_wq"], "kvdT": a["attn_g_kv_down"].T,
        "kvup": _np.concatenate([a["attn_g_k_up"], a["attn_g_v_up"]], 1), "wo0": a["attn_g_wo"],
        "wq1": a["attn_l_wq"], "wk1": a["attn_l_wk"], "wv1": a["attn_l_wv"], "wo1": a["attn_l_wo"],
        "n1": column(a["attn_norm1_w"]), "n2": column(a["attn_norm2_w"]), "rope": rope, "tri": tri,
        "ctxT": a["ctx_1024"].reshape(NB * CL, D).T, "mask": a["mask_1x1xSxS2_ff0"].reshape(S, CL),
        "xwq": a["xattn_Wq"], "xwk": a["xattn_Wk"], "xwv": a["xattn_Wv"], "xwo": a["xattn_Wo"],
        "xbq": column(a["xattn_bq"]), "xbk": column(a["xattn_bk"]),
        "xbv": a["xattn_bv"].reshape(1, D), "xbo": a["xattn_bo"].reshape(1, D),
        "router": a["ffn_router_w"].T, "experts": _np.concatenate([gate, up, lower], 2), "small": small,
    }
    arrays = {f"in_{n}": _np.ascontiguousarray(v) for n, v in arrays.items()}
    nc = _bacc.Bacc("TRN2", target_bir_lowering=False, num_devices=1)
    args = [nc.dram_tensor(n, v.shape, _mybir.dt.from_np(v.dtype), kind="ExternalInput").ap() for n, v in arrays.items()]
    args.append(nc.dram_tensor("out_0", (T, D), F32, kind="ExternalOutput").ap())
    build_decoder(nc, *args)
    r = _run(nc, [arrays], core_ids=[0])
    return r.results[0]["out_0"].reshape(_OUT)
```
